# Optimizing a Trainium2 kernel written in Bass

```python
import numpy as np
import jax
import jax.numpy as jnp

def _softmax(x, axis=-1):
    return jax.nn.softmax(x, axis=axis)

def _gelu(x):
    return jax.nn.gelu(x, approximate=True)

def _silu(x):
    return jax.nn.silu(x)

def _sigmoid(x):
    return jax.nn.sigmoid(x)

def _layernorm(x, axis=-1, eps=1e-05):
    m = jnp.mean(x, axis=axis, keepdims=True)
    v = jnp.var(x, axis=axis, keepdims=True)
    return (x - m) / jnp.sqrt(v + eps)

def _scatter_add(tgt, idx, src, axis=0):
    return tgt.at[idx].add(src)

def _segment_sum(src, seg, n):
    return jax.ops.segment_sum(src, seg, n)
kernel_name = 'mk_gps_d1_gnn_r8_9fde68'

def setup_inputs(seed: int=0):
    np.random.seed(seed)
    _w = jnp.asarray

    def _rec_inputs():
        import jax
        import jax.numpy as jnp
        _gk = jax.random.key(seed)
        x = -0.0003713 + 1 * jax.random.normal(jax.random.fold_in(_gk, 1), (6250, 256), jnp.float32)
        src = jax.random.randint(jax.random.fold_in(_gk, 2), (200000,), 0, 6250, jnp.int32)
        dst = jax.random.randint(jax.random.fold_in(_gk, 3), (200000,), 0, 6250, jnp.int32)
        _o = jnp.argsort(dst, stable=True)
        src = src[_o]
        dst = dst[_o]
        edge_weight = -7.32377e-05 + 0.176746 * jax.random.normal(jax.random.fold_in(_gk, 12), (200000,), jnp.float32)
        return (x, src, dst, edge_weight)
    x, src, dst, edge_weight = _rec_inputs()

    def _L0_gnn_setup():
        import jax, jax.numpy as jnp
        import numpy as np
        N_NODES = 6250
        NNZ = 200000
        D_FEAT = 256
        key = jax.random.key(seed)
        k_x, k_v, k_r, k_c = jax.random.split(key, 4)
        x = jax.random.normal(k_x, (N_NODES, D_FEAT), dtype=jnp.float32)
        std = 1.0 / np.sqrt(NNZ / N_NODES)
        values = jax.random.normal(k_v, (NNZ,), dtype=jnp.float32) * std
        row = jax.random.randint(k_r, (NNZ,), 0, N_NODES, dtype=jnp.int64)
        col = jax.random.randint(k_c, (NNZ,), 0, N_NODES, dtype=jnp.int64)
        return {'x': x, 'values': values, 'row': row, 'col': col}
    _L0_gnn_all = _L0_gnn_setup()
    _L0_gnn_in = {k: v for k, v in _L0_gnn_all.items() if k in ()}
    del _L0_gnn_all

    def _L0_mix_setup():
        import jax, jax.numpy as jnp
        import numpy as np
        BN_EPS = 1e-05
        key = jax.random.key(seed)
        ks = jax.random.split(key, 4)
        B, N, D = (8, 1024, 256)
        outD = 256
        s = 1.0 / np.sqrt(D)
        return {'feature': jax.random.normal(ks[0], (B, N, D), dtype=jnp.float32), 'W_qk': jax.random.normal(ks[1], (2, D, D), dtype=jnp.float32) * s, 'b_qk': jnp.zeros((2, D), dtype=jnp.float32), 'W_v': jax.random.normal(ks[2], (D, outD), dtype=jnp.float32) * s, 'b_v': jnp.zeros((outD,), dtype=jnp.float32), 'gamma': jnp.ones((D,), dtype=jnp.float32), 'beta': jnp.zeros((D,), dtype=jnp.float32)}
    _L0_mix_all = _L0_mix_setup()
    _L0_mix_in = {k: v for k, v in _L0_mix_all.items() if k in ('W_qk', 'b_qk', 'W_v', 'b_v', 'gamma', 'beta')}
    del _L0_mix_all

    def _L0_ffn_setup():
        import jax, jax.numpy as jnp
        import numpy as np
        NUM_EXPERTS = 8
        TOP_K = 2
        B, S, D = (8, 1024, 256)

        def _moe(tokens, router_w, w1, b1, w2, b2):
            N = tokens.shape[0]
            E = router_w.shape[0]
            logits = tokens.astype(jnp.float32) @ router_w.astype(jnp.float32).T
            probs = jax.nn.softmax(logits, axis=-1)
            rw, re = jax.lax.top_k(probs, TOP_K)
            if TOP_K > 1:
                rw = rw / jnp.maximum(rw.sum(-1, keepdims=True), 1e-12)
            rw = rw.astype(tokens.dtype)
            combine = jnp.zeros((N, E), tokens.dtype).at[jnp.arange(N)[:, None], re].set(rw)
            out = tokens
            for e in range(E):
                h = jax.nn.gelu(tokens @ w1[e] + b1[e], approximate=False)
                y = h @ w2[e] + b2[e]
                out = out + combine[:, e:e + 1] * y
            return out
        key = jax.random.key(seed)
        ks = jax.random.split(key, 4)
        scale = 1.0 / np.sqrt(D).astype(np.float32)
        return {'input_embeddings': jax.random.normal(ks[0], (B, S, D), jnp.float32), 'router_w': jax.random.normal(ks[1], (NUM_EXPERTS, D), jnp.float32) * scale, 'w1': jax.random.normal(ks[2], (NUM_EXPERTS, D, D), jnp.float32) * scale, 'b1': jnp.zeros((NUM_EXPERTS, D), jnp.float32), 'w2': jax.random.normal(ks[3], (NUM_EXPERTS, D, D), jnp.float32) * scale, 'b2': jnp.zeros((NUM_EXPERTS, D), jnp.float32)}
    _L0_ffn_all = _L0_ffn_setup()
    _L0_ffn_in = {k: v for k, v in _L0_ffn_all.items() if k in ('router_w', 'w1', 'b1', 'w2', 'b2')}
    del _L0_ffn_all
    return {'x': x, 'src': src, 'dst': dst, 'edge_weight': edge_weight, 'L0_mix_W_qk': _L0_mix_in['W_qk'], 'L0_mix_b_qk': _L0_mix_in['b_qk'], 'L0_mix_W_v': _L0_mix_in['W_v'], 'L0_mix_b_v': _L0_mix_in['b_v'], 'L0_mix_gamma': _L0_mix_in['gamma'], 'L0_mix_beta': _L0_mix_in['beta'], 'L0_ffn_router_w': _L0_ffn_in['router_w'], 'L0_ffn_w1': _L0_ffn_in['w1'], 'L0_ffn_b1': _L0_ffn_in['b1'], 'L0_ffn_w2': _L0_ffn_in['w2'], 'L0_ffn_b2': _L0_ffn_in['b2']}

def reference(x, src, dst, edge_weight, L0_mix_W_qk, L0_mix_b_qk, L0_mix_W_v, L0_mix_b_v, L0_mix_gamma, L0_mix_beta, L0_ffn_router_w, L0_ffn_w1, L0_ffn_b1, L0_ffn_w2, L0_ffn_b2):
    import jax
    import jax.numpy as jnp

    def _L0_gnn_ref(x, values, row, col):
        import jax, jax.numpy as jnp
        import numpy as np
        N_NODES = 6250
        NNZ = 200000
        D_FEAT = 256
        msgs = values[:, None] * x[col]
        out = jax.ops.segment_sum(msgs, row, num_segments=N_NODES)
        return out

    def _L0_mix_ref(feature, W_qk, b_qk, W_v, b_v, gamma, beta):
        import jax, jax.numpy as jnp
        import numpy as np
        BN_EPS = 1e-05
        QK = jnp.einsum('bnd,kde->bkne', feature, W_qk) + b_qk[None, :, None, :]
        value = jnp.einsum('bnd,de->bne', feature, W_v) + b_v
        query = QK[:, 0]
        key = QK[:, 1]
        sm = jax.nn.softmax(key, axis=1)
        lam = jnp.einsum('bnd,bne->bde', sm, value)
        mean = jnp.mean(lam, axis=(0, 2), keepdims=True)
        var = jnp.var(lam, axis=(0, 2), keepdims=True)
        bn = (lam - mean) * jax.lax.rsqrt(var + BN_EPS)
        bn = bn * gamma[None, :, None] + beta[None, :, None]
        return jnp.einsum('bnd,bde->bne', query, bn)

    def _L0_ffn_ref(input_embeddings, router_w, w1, b1, w2, b2):
        import jax, jax.numpy as jnp
        import numpy as np
        NUM_EXPERTS = 8
        TOP_K = 2
        B, S, D = (8, 1024, 256)

        def _moe(tokens, router_w, w1, b1, w2, b2):
            N = tokens.shape[0]
            E = router_w.shape[0]
            logits = tokens.astype(jnp.float32) @ router_w.astype(jnp.float32).T
            probs = jax.nn.softmax(logits, axis=-1)
            rw, re = jax.lax.top_k(probs, TOP_K)
            if TOP_K > 1:
                rw = rw / jnp.maximum(rw.sum(-1, keepdims=True), 1e-12)
            rw = rw.astype(tokens.dtype)
            combine = jnp.zeros((N, E), tokens.dtype).at[jnp.arange(N)[:, None], re].set(rw)
            out = tokens
            for e in range(E):
                h = jax.nn.gelu(tokens @ w1[e] + b1[e], approximate=False)
                y = h @ w2[e] + b2[e]
                out = out + combine[:, e:e + 1] * y
            return out
        b, s, d = input_embeddings.shape
        tokens = input_embeddings.reshape(b * s, d)
        return _moe(tokens, router_w, w1, b1, w2, b2).reshape(b, s, d)
    xn = _layernorm(x, axis=-1)
    x = x + _L0_gnn_ref(xn, edge_weight, src, dst) + _L0_mix_ref(xn[None], L0_mix_W_qk, L0_mix_b_qk, L0_mix_W_v, L0_mix_b_v, L0_mix_gamma, L0_mix_beta)[0]
    x = x + _L0_ffn_ref(_layernorm(x, axis=-1)[None], L0_ffn_router_w, L0_ffn_w1, L0_ffn_b1, L0_ffn_w2, L0_ffn_b2)[0]
    return x

_drawn_inputs = setup_inputs


def setup_inputs(seed=0):
    import zlib

    import numpy as np

    out = dict(_drawn_inputs(seed))
    spreads = {'L0_mix_b_qk': (0.0, 0.1),
     'L0_mix_b_v': (0.0, 0.1),
     'L0_mix_gamma': (1.0, 0.2),
     'L0_mix_beta': (0.0, 0.1),
     'L0_ffn_b1': (0.0, 2.0),
     'L0_ffn_b2': (0.0, 0.8)}
    factors = {}
    for name, (base, spread) in spreads.items():
        noise = np.random.default_rng([zlib.crc32(name.encode()), seed]).standard_normal(out[name].shape)
        drawn = base * np.exp(spread * noise) if base else spread * noise
        out[name] = jnp.asarray(drawn.astype(out[name].dtype))
    for name, factor in factors.items():
        out[name] = (out[name] * factor).astype(out[name].dtype)
    return out
```

```python
from contextlib import ExitStack

import concourse.bass as bass
from concourse import mybir
import numpy as np

F32 = mybir.dt.float32
BF16 = mybir.dt.bfloat16
I32 = mybir.dt.int32
U32 = mybir.dt.uint32
ALU = mybir.AluOpType
ACT = mybir.ActivationFunctionType
AX = mybir.AxisListType

P = 128
N = 6250
D = 256
KC = D // P
E = 200000
NEXP = 8
EPS = 1e-5
GT = 4
GROUP = GT * P
NG = N // GROUP
TAIL = N - NG * GROUP
NT = NG * GT + 1
CT = 29
NC_ = -(-E // (CT * P))
ET = NC_ * CT
assert 0 < TAIL <= P and NG % 2 == 0


def groups(eng, step):
    for j in range(2):
        step(j, 0, j, [P] * GT)
    with eng.Fori(1, NG // 2) as pair:
        for j in range(2):
            step(pair * 2 + j, pair, j, [P] * GT)
    step(NG, NG // 2, 0, [TAIL])


class Stage:

    def __init__(self, nc, name):
        self.nc, self.name, self.ctx, self.spaced = nc, name, ExitStack(), {}

    def __enter__(self):
        self.ctx.__enter__()
        return self

    def __exit__(self, *a):
        return self.ctx.__exit__(*a)

    def sb(self, name, shape, dt=F32):
        return self.ctx.enter_context(self.nc.sbuf_tensor(f"{self.name}_{name}", shape, dt))

    def ps(self, name, shape, dt=F32):
        return self.ctx.enter_context(self.nc.psum_tensor(f"{self.name}_{name}", shape, dt))

    def sem(self, name):
        return self.ctx.enter_context(self.nc.semaphore(f"{self.name}_{name}"))


def wait_then_pass(eng, sem, value, passed):
    if isinstance(value, int):
        if value > 0:
            eng.wait_ge(sem, value)
        return
    eng.wait_ge(sem, value)
    eng.sem_inc(passed, 1)


def node_view(dram, g, rows):
    if len(rows) == GT:
        return dram[bass.ds(g * GROUP, GROUP), :].rearrange("(s p) d -> p s d", p=P)
    return dram[g * GROUP:g * GROUP + rows[0], :]


def node_tiles(sb, g, rows):
    if len(rows) == GT:
        return sb[:, bass.ds(g * GT, GT), :]
    return sb[0:rows[0], g * GT, :]


def norm_stage(nc, x, xn_dram, xn, xnT, ident):
    with Stage(nc, "ln") as st:
        xin = st.sb("xin", [P, 2, GT, D])
        stats = st.sb("stats", [P, 2, GT, 6])
        mv = st.sb("mv", [P, 2, GT, 2])
        std = st.sb("std", [P, 2, GT])
        rstd = st.sb("rstd", [P, 2, GT])
        xnb = st.sb("xnb", [P, 2, GT, D])
        eps = st.sb("eps", [P, 1])
        tp = [st.ps(f"tp{k}", [P, GROUP]) for k in range(2 * KC)]
        x_in = [st.sem(f"x_in{j}") for j in range(2)]
        xn_out = [st.sem(f"xn_out{j}") for j in range(2)]
        xn_kept = [st.sem(f"xn_kept{j}") for j in range(2)]
        eps_set = st.sem("eps_set")
        stats_done = st.sem("stats_done")
        var_done = st.sem("var_done")
        std_done = st.sem("std_done")
        rstd_done = st.sem("rstd_done")
        xn_done = st.sem("xn_done")
        turned = st.sem("turned")
        evacuated = st.sem("evacuated")
        passed = {e: st.sem(f"passed_{e}") for e in ("sp", "act", "pe", "dve", "pool")}
        with nc.Block() as block:

            @block.sync
            def _(sp):
                def load(g, pair, j, rows):
                    wait_then_pass(sp, xn_done, g + 1, passed["sp"])
                    dst = xin[:, j, :, :] if len(rows) == GT else xin[0:rows[0], j, 0, :]
                    sp.dma_start(dst, node_view(x, g, rows)).then_inc(x_in[j], 16)

                groups(sp, load)

            @block.vector
            def _(dve):
                nc.vector.memset(eps[:, :], EPS).then_inc(eps_set, 1)
                dve.sem_inc(xn_done, 2)

                def normalise(g, pair, j, rows):
                    n, r = len(rows), rows[0]
                    wait_then_pass(dve, x_in[j], pair * 16 + 16, passed["dve"])
                    for s in range(n):
                        last = nc.vector.bn_stats(stats[:r, j, s, :], xin[:r, j, s, :])
                    last.then_inc(stats_done, 1)
                    wait_then_pass(dve, stats_done, g + 1, passed["dve"])
                    for s in range(n):
                        last = nc.vector.bn_aggr(mv[:r, j, s, :], stats[:r, j, s, :])
                    last.then_inc(var_done, 1)
                    wait_then_pass(dve, std_done, g + 1, passed["dve"])
                    nc.vector.reciprocal(rstd[:r, j, 0:n], std[:r, j, 0:n]).then_inc(rstd_done, 1)
                    wait_then_pass(dve, rstd_done, g + 1, passed["dve"])
                    wait_then_pass(dve, xn_out[j], pair * 16, passed["dve"])
                    wait_then_pass(dve, xn_kept[j], pair * 16, passed["dve"])
                    wait_then_pass(dve, evacuated, g + 1, passed["dve"])
                    for s in range(n):
                        last = nc.vector.tensor_scalar(
                            xnb[:r, j, s, :], xin[:r, j, s, :], mv[:r, j, s, 0:1],
                            rstd[:r, j, s:s + 1], ALU.subtract, ALU.mult)
                    last.then_inc(xn_done, 1)

                groups(dve, normalise)

            @block.tensor
            def _(pe):
                pe.sem_inc(evacuated, 2)

                def turn(g, pair, j, rows):
                    n, r = len(rows), rows[0]
                    wait_then_pass(pe, xn_done, g + 3, passed["pe"])
                    wait_then_pass(pe, evacuated, g + 1, passed["pe"])
                    for s in range(n):
                        for k in range(KC):
                            last = transpose(nc, tp[2 * j + k][:, s * P:s * P + r],
                                             xnb[:r, j, s, k * P:(k + 1) * P], ident, r)
                    last.then_inc(turned, 1)

                groups(pe, turn)

            @block.scalar
            def _(act):
                act.wait_ge(eps_set, 1)

                def finish(g, pair, j, rows):
                    n, r = len(rows), rows[0]
                    wait_then_pass(act, var_done, g + 1, passed["act"])
                    nc.scalar.activation(std[:r, j, 0:n], mv[:r, j, 0:n, 1], ACT.Sqrt,
                                         bias=eps[:r, :]).then_inc(std_done, 1)
                    wait_then_pass(act, xn_done, g + 3, passed["act"])
                    src = xnb[:, j, :, :] if n == GT else xnb[:r, j, 0, :]
                    act.dma_start(node_view(xn_dram, g, rows), src).then_inc(xn_out[j], 16)
                    act.dma_start(node_tiles(xn, g, rows), src).then_inc(xn_kept[j], 16)
                    wait_then_pass(act, turned, g + 1, passed["act"])
                    w = sum(rows)
                    for k in range(KC):
                        last = nc.scalar.copy(xnT[:, k, bass.ds(g * GROUP, w)], tp[2 * j + k][:, 0:w])
                    last.then_inc(evacuated, 1)

                groups(act, finish)
                for out in (xn_out, xn_kept):
                    act.wait_ge(out[0], 16 * (NG // 2 + 1))
                    act.wait_ge(out[1], 16 * (NG // 2))


def transpose(nc, out, in_, ident, rows):
    return nc.tensor.transpose(out, in_, ident[0:rows, 0:rows])


def mix_stage(nc, x, W_qk, b_qk, W_v, b_v, gamma, beta, xn, xnT, ident):
    with Stage(nc, "mix") as st:
        wq = st.sb("wq", [P, KC, D])
        wk = st.sb("wk", [P, KC, D])
        wv = st.sb("wv", [P, KC, D])
        bq = st.sb("bq", [P, KC])
        bk = st.sb("bk", [P, KC])
        bv = st.sb("bv", [1, D])
        gam = st.sb("gam", [P, KC])
        bet = st.sb("bet", [P, KC])
        ones = st.sb("ones", [P, P])
        zeros = st.sb("zeros", [P, P])
        eps = st.sb("eps", [P, 1])
        keyT = st.sb("keyT", [P, KC, N])
        ek = st.sb("ek", [P, 2, KC, GROUP])
        gsum = st.sb("gsum", [P, KC, NG + 1])
        tmax = st.sb("tmax", [P, KC])
        nmax = st.sb("nmax", [P, KC])
        esum = st.sb("esum", [P, KC])
        rsum = st.sb("rsum", [P, KC])
        pt = st.sb("pt", [P, 2, GT, D])
        M = st.sb("M", [P, KC, D])
        MT = st.sb("MT", [P, KC, D])
        wqT = st.sb("wqT", [P, KC, D])
        lam = st.sb("lam", [P, KC, D])
        bn = st.sb("bn", [P, KC, D])
        stats = st.sb("stats", [P, KC, 6])
        mv = st.sb("mv", [P, KC, 2])
        std = st.sb("std", [P, KC])
        rstd = st.sb("rstd", [P, KC])
        scl = st.sb("scl", [P, KC])
        msc = st.sb("msc", [P, KC])
        shf = st.sb("shf", [P, KC])
        bqb = st.sb("bqb", [P, KC, P])
        wqbn = st.sb("wqbn", [P, KC, D])
        qbias = st.sb("qbias", [P, D])
        xin = st.sb("xin", [P, 2, GT, D])
        xs = ek
        kp = [st.ps(f"kp{k}", [P, GROUP]) for k in range(4)]
        mp = [st.ps(f"mp{k}", [P, GROUP]) for k in range(2)]
        lp = [st.ps(f"lp{k}", [P, GROUP]) for k in range(2)]
        w_in = st.sem("w_in")
        const = st.sem("const")
        keyed = st.sem("keyed")
        key_out = st.sem("key_out")
        maxed = st.sem("maxed")
        neg = st.sem("neg")
        exped = st.sem("exped")
        p_turned = st.sem("p_turned")
        p_out = st.sem("p_out")
        p_used = st.sem("p_used")
        m_done = st.sem("m_done")
        c = st.sem("c")
        pe_c = st.sem("pe_c")
        act_c = st.sem("act_c")
        x_in = [st.sem(f"x_in{j}") for j in range(2)]
        xs_done = st.sem("xs_done")
        mixed = st.sem("mixed")
        xq_done = st.sem("xq_done")
        h_done = st.sem("h_done")
        passed = {e: st.sem(f"passed_{e}") for e in ("sp", "act", "pe", "dve")}
        W_LOADS = 8

        with nc.Block() as block:

            @block.sync
            def _(sp):
                for dst, src in ((wk, W_qk[1]), (wq, W_qk[0]), (wv, W_v)):
                    sp.dma_start(dst[:, :, :], src.rearrange("(c p) e -> p c e", p=P)).then_inc(w_in, 16)
                with nc.allow_non_contiguous_dma(reason="one column per feature block"):
                    for dst, src in ((bk, b_qk[1]), (bq, b_qk[0]), (gam, gamma), (bet, beta)):
                        sp.dma_start(dst[:, :], src.rearrange("(c p) -> p c", p=P)).then_inc(w_in, 16)
                sp.dma_start(bv[:, :], b_v.rearrange("(a e) -> a e", a=1)).then_inc(w_in, 16)

                def load(g, pair, j, rows):
                    wait_then_pass(sp, h_done, g + 1, passed["sp"])
                    dst = xin[:, j, :, :] if len(rows) == GT else xin[0:rows[0], j, 0, :]
                    sp.dma_start(dst, node_view(x, g, rows)).then_inc(x_in[j], 16)

                groups(sp, load)

            @block.tensor
            def _(pe):
                pe.wait_ge(w_in, 16 * W_LOADS)
                pe.wait_ge(const, 3)
                pe.sem_inc(key_out, 2)

                def keys(g, pair, j, rows):
                    w = sum(rows)
                    wait_then_pass(pe, key_out, g + 1, passed["pe"])
                    for e in range(KC):
                        for k in range(KC):
                            last = nc.tensor.matmul(kp[2 * j + e][:, 0:w], wk[:, k, e * P:(e + 1) * P],
                                                    xnT[:, k, bass.ds(g * GROUP, w)],
                                                    start=k == 0, stop=k == KC - 1)
                    last.then_inc(keyed, 1)

                groups(pe, keys)
                for e in range(KC):
                    nc.tensor.matmul(mp[e][:, 0:D], zeros[:, :], wk[:, 0, :], start=True, stop=False)
                pe.sem_inc(p_out, 2)

                def turn(g, j, rows):
                    wait_then_pass(pe, exped, g + 1, passed["pe"])
                    wait_then_pass(pe, p_out, g + 1, passed["pe"])
                    for s, r in enumerate(rows):
                        for e in range(KC):
                            last = transpose(nc, kp[2 * j + s // 2][0:r, (s % 2) * D + e * P:(s % 2) * D + (e + 1) * P],
                                             ek[:, j, e, s * P:s * P + r], ident, P)
                    last.then_inc(p_turned, 1)

                def accumulate(g, j, rows, stop):
                    wait_then_pass(pe, p_out, g + 3, passed["pe"])
                    for s, r in enumerate(rows):
                        xt = xn[:r, g * GT, :] if stop else \
                            xn[:, bass.ds(g * GT + s, 1), :].rearrange("p a d -> p (a d)")
                        for e in range(KC):
                            last = nc.tensor.matmul(mp[e][:, 0:D], pt[:r, j, s, e * P:(e + 1) * P], xt,
                                                    start=False, stop=stop)
                    last.then_inc(p_used, 1)

                whole = [P] * GT
                turn(0, 0, whole)
                with pe.Fori(0, NG // 2 - 1) as i:
                    turn(i * 2 + 1, 1, whole)
                    accumulate(i * 2, 0, whole, False)
                    turn(i * 2 + 2, 0, whole)
                    accumulate(i * 2 + 1, 1, whole, False)
                turn(NG - 1, 1, whole)
                accumulate(NG - 2, 0, whole, False)
                turn(NG, 0, [TAIL])
                accumulate(NG - 1, 1, whole, False)
                accumulate(NG, 0, [TAIL], True)
                pe.wait_ge(c, 4)
                for a in range(KC):
                    for b in range(KC):
                        nc.tensor.transpose(kp[a][:, b * P:(b + 1) * P], M[:, b, a * P:(a + 1) * P], ident[:, :])
                for a in range(KC):
                    for b in range(KC):
                        last = nc.tensor.transpose(kp[2 + a][:, b * P:(b + 1) * P], wq[:, b, a * P:(a + 1) * P],
                                                   ident[:, :])
                last.then_inc(pe_c, 1)
                pe.wait_ge(c, 5)
                for a in range(KC):
                    for k in range(KC):
                        nc.tensor.matmul(lp[a][:, 0:D], MT[:, k, a * P:(a + 1) * P], wv[:, k, :],
                                         start=k == 0, stop=False)
                    last = nc.tensor.matmul(lp[a][:, 0:D], ones[0:1, :], bv[:, :], start=False, stop=True)
                last.then_inc(pe_c, 1)
                pe.wait_ge(c, 13)
                for a in range(KC):
                    for k in range(KC):
                        nc.tensor.matmul(kp[a][:, 0:D], wqT[:, k, a * P:(a + 1) * P], bn[:, k, :],
                                         start=k == 0, stop=k == KC - 1)
                for k in range(KC):
                    last = nc.tensor.matmul(kp[2][:, 0:D], bqb[:, k, :], bn[:, k, :],
                                            start=k == 0, stop=k == KC - 1)
                last.then_inc(pe_c, 1)
                pe.wait_ge(c, 14)
                pe.sem_inc(xq_done, 2)

                def mix(g, pair, j, rows):
                    wait_then_pass(pe, xs_done, g + 3, passed["pe"])
                    wait_then_pass(pe, xq_done, g + 1, passed["pe"])
                    for s, r in enumerate(rows):
                        for k in range(KC):
                            last = nc.tensor.matmul(kp[2 * j + s // 2][:r, (s % 2) * D:(s % 2 + 1) * D],
                                                    xs[:, j, k, s * P:s * P + r], wqbn[:, k, :],
                                                    start=k == 0, stop=k == KC - 1)
                    last.then_inc(mixed, 1)

                groups(pe, mix)

            @block.scalar
            def _(act):
                act.wait_ge(w_in, 16 * W_LOADS)

                def key_evac(g, pair, j, rows):
                    w = sum(rows)
                    wait_then_pass(act, keyed, g + 1, passed["act"])
                    for e in range(KC):
                        last = nc.scalar.activation(keyT[:, e, bass.ds(g * GROUP, w)], kp[2 * j + e][:, 0:w],
                                                    ACT.Identity, bias=bk[:, e:e + 1])
                    last.then_inc(key_out, 1)

                groups(act, key_evac)
                act.wait_ge(neg, 1)

                def exps(g, pair, j, rows):
                    w = sum(rows)
                    wait_then_pass(act, p_turned, g + 1, passed["act"])
                    for e in range(KC):
                        last = nc.scalar.activation(ek[:, j, e, 0:w], keyT[:, e, bass.ds(g * GROUP, w)], ACT.Exp,
                                                    bias=nmax[:, e:e + 1], accum_out=gsum[:, e, bass.ds(g, 1)])
                    last.then_inc(exped, 1)

                act.sem_inc(p_turned, 2)
                groups(act, exps)
                act.wait_ge(c, 7)
                nc.scalar.activation(std[:, :], mv[:, :, 1], ACT.Sqrt, bias=eps[:, :]).then_inc(act_c, 1)
                act.sem_inc(xs_done, 2)

                def fix(g, pair, j, rows):
                    w = sum(rows)
                    wait_then_pass(act, mixed, g + 1, passed["act"])
                    for k in range(KC):
                        last = nc.scalar.copy(xs[:, j, k, 0:w], xnT[:, k, bass.ds(g * GROUP, w)])
                    last.then_inc(xs_done, 1)

                act.sem_inc(mixed, 2)
                groups(act, fix)

            @block.vector
            def _(dve):
                nc.vector.memset(ones[:, :], 1.0).then_inc(const, 1)
                nc.vector.memset(zeros[:, :], 0.0).then_inc(const, 1)
                nc.vector.memset(eps[:, :], EPS).then_inc(const, 1)
                dve.wait_ge(key_out, 2 + NG + 1)
                for e in range(KC):
                    last = nc.vector.reduce_max(tmax[:, e:e + 1], keyT[:, e, :], AX.X)
                last.then_inc(maxed, 1)
                dve.wait_ge(maxed, 1)
                nc.vector.tensor_scalar_mul(nmax[:, :], tmax[:, :], -1.0).then_inc(neg, 1)
                dve.sem_inc(p_used, 2)

                def evac(g, pair, j, rows):
                    wait_then_pass(dve, p_turned, g + 3, passed["dve"])
                    wait_then_pass(dve, p_used, g + 1, passed["dve"])
                    if len(rows) == GT:
                        for b in range(2):
                            last = nc.vector.tensor_copy(pt[:, j, 2 * b:2 * b + 2, :],
                                                         kp[2 * j + b][:, :].rearrange("p (s d) -> p s d", s=2))
                    else:
                        last = nc.vector.tensor_copy(pt[:rows[0], j, 0, :], kp[2 * j][:rows[0], 0:D])
                    last.then_inc(p_out, 1)

                groups(dve, evac)
                dve.wait_ge(exped, NG + 1)

                n = [0]

                def link(ins):
                    n[0] += 1
                    ins.then_inc(c, 1)
                    dve.wait_ge(c, n[0])

                for e in range(KC):
                    last = nc.vector.reduce_sum(esum[:, e:e + 1], gsum[:, e, :], AX.X)
                link(last)
                link(nc.vector.reciprocal(rsum[:, :], esum[:, :]))
                dve.wait_ge(p_used, NG + 3)
                for e in range(KC):
                    link(nc.vector.tensor_scalar(M[:, e, :], mp[e][:, 0:D], rsum[:, e:e + 1], None, ALU.mult))
                dve.wait_ge(pe_c, 1)
                for a in range(KC):
                    nc.vector.tensor_copy(MT[:, a, :], kp[a][:, 0:D])
                for a in range(KC):
                    last = nc.vector.tensor_copy(wqT[:, a, :], kp[2 + a][:, 0:D])
                link(last)
                dve.wait_ge(pe_c, 2)
                for a in range(KC):
                    nc.vector.tensor_copy(lam[:, a, :], lp[a][:, 0:D])
                    last = nc.vector.bn_stats(stats[:, a, :], lp[a][:, 0:D])
                link(last)
                for a in range(KC):
                    last = nc.vector.bn_aggr(mv[:, a, :], stats[:, a, :])
                link(last)
                dve.wait_ge(act_c, 1)
                link(nc.vector.reciprocal(rstd[:, :], std[:, :]))
                link(nc.vector.tensor_tensor(scl[:, :], rstd[:, :], gam[:, :], ALU.mult))
                link(nc.vector.tensor_tensor(msc[:, :], mv[:, :, 0], scl[:, :], ALU.mult))
                link(nc.vector.tensor_tensor(shf[:, :], bet[:, :], msc[:, :], ALU.subtract))
                for k in range(KC):
                    last = nc.vector.tensor_scalar(bn[:, k, :], lam[:, k, :], scl[:, k:k + 1], shf[:, k:k + 1],
                                                   ALU.mult, ALU.add)
                link(last)
                for k in range(KC):
                    last = nc.vector.tensor_scalar(bqb[:, k, :], ones[:, :], bq[:, k:k + 1], None, ALU.mult)
                link(last)
                assert n[0] == 13, n
                dve.wait_ge(pe_c, 3)
                for k in range(KC):
                    nc.vector.tensor_copy(wqbn[:, k, :], kp[k][:, 0:D])
                link(nc.vector.tensor_copy(qbias[:, :], kp[2][:, 0:D]))
                dve.sem_inc(h_done, 2)

                def add(g, pair, j, rows):
                    n, r = len(rows), rows[0]
                    wait_then_pass(dve, x_in[j], pair * 16 + 16, passed["dve"])
                    wait_then_pass(dve, mixed, g + 3, passed["dve"])
                    for s in range(n):
                        last = nc.vector.tensor_tensor(xin[:r, j, s, :], kp[2 * j + s // 2][:r, (s % 2) * D:(s % 2 + 1) * D],
                                                       xin[:r, j, s, :], ALU.add)
                    last.then_inc(xq_done, 1)
                    wait_then_pass(dve, xq_done, g + 3, passed["dve"])
                    if n == GT:
                        out, a, b = xn[:, bass.ds(g * GT, GT), :], xin[:, j, :, :], \
                            qbias[:, :].rearrange("p (a d) -> p a d", a=1).to_broadcast([P, GT, D])
                    else:
                        out, a, b = xn[:r, g * GT, :], xin[:r, j, 0, :], qbias[:r, :]
                    nc.vector.tensor_tensor(out, a, b, ALU.add).then_inc(h_done, 1)

                groups(dve, add)


def edges_any_order(nc, src_t, dst_t, ew_t, xn_dram, sum_dram, h, ident, below):
    with Stage(nc, "any") as st:
        src_i = st.sb("src_i", [P, ET], I32)
        dst_i = st.sb("dst_i", [P, ET], I32)
        ew = st.sb("ew", [P, ET])
        src_f = st.sb("src_f", [P, ET])
        ones = st.sb("ones", [P, P])
        zrow = st.sb("zrow", [P, D])
        to_i = st.sb("to_i", [P, 1], I32)
        from_i = st.sb("from_i", [P, 1], I32)
        first_i = st.sb("first_i", [P, 1], I32)
        to_f = st.sb("to_f", [P, 1])
        wt = st.sb("wt", [P, 1])
        diag = st.sb("diag", [P, P])
        same = st.sb("same", [P, P])
        early = st.sb("early", [P, P])
        ecount = st.sb("ecount", [P, 1])
        first_f = st.sb("first_f", [P, 1])
        rows = st.sb("rows", [P, D])
        msg = st.sb("msg", [P, D])
        old = st.sb("old", [P, D])
        new = st.sb("new", [P, D])
        hin = st.sb("hin", [P, 2, GT, D])
        bc = st.ps("bc", [P, P])
        merged = st.ps("merged", [P, D])
        e_in = st.sem("e_in")
        const = st.sem("const")
        zeroed = st.sem("zeroed")
        picked = st.sem("picked")
        gathered = st.sem("gathered")
        old_in = st.sem("old_in")
        c = st.sem("c")
        spread = st.sem("spread")
        eq_done = st.sem("eq_done")
        merge_done = st.sem("merge_done")
        new_done = st.sem("new_done")
        stored = st.sem("stored")
        h_in = [st.sem(f"h_in{j}") for j in range(2)]
        h_done = st.sem("h_done")
        passed = {e: st.sem(f"passed_{e}") for e in ("sp", "pool", "pe", "dve")}
        STEP = 8
        with nc.Block() as block:

            @block.sync
            def _(sp):
                for d, s in ((src_i, src_t), (dst_i, dst_t), (ew, ew_t)):
                    sp.dma_start(d[:, :], s).then_inc(e_in, 16)
                sp.wait_ge(const, 2)
                with sp.Fori(0, NT - 1) as t:
                    sp.dma_start(sum_dram[bass.ds(t * P, P), :], zrow[:, :]).then_inc(zeroed, 16)
                sp.wait_ge(stored, 16 * (ET + 1))

                def load(g, pair, j, rows):
                    wait_then_pass(sp, h_done, g + 1, passed["sp"])
                    dst = hin[:, j, :, :] if len(rows) == GT else hin[0:rows[0], j, 0, :]
                    sp.dma_start(dst, node_view(sum_dram, g, rows)).then_inc(h_in[j], 16)

                groups(sp, load)

            @block.gpsimd
            def _(pool):
                pool.wait_ge(const, 2)
                pool.dma_start(sum_dram[(NT - 1) * P:NT * P, :], zrow[:, :]).then_inc(stored, 16)
                pool.wait_ge(zeroed, 16 * (NT - 1))
                with pool.Fori(0, ET) as t:
                    wait_then_pass(pool, picked, t + 1, passed["pool"])
                    pool.indirect_dma_start(
                        out=rows[:, :], out_offset=None, in_=xn_dram,
                        in_offset=bass.IndirectOffsetOnAxis(ap=from_i[:, 0:1], axis=0)).then_inc(gathered, 16)
                    wait_then_pass(pool, stored, t * 16 + 16, passed["pool"])
                    pool.indirect_dma_start(
                        out=old[:, :], out_offset=None, in_=sum_dram,
                        in_offset=bass.IndirectOffsetOnAxis(ap=to_i[:, 0:1], axis=0)).then_inc(old_in, 16)
                    wait_then_pass(pool, new_done, t + 1, passed["pool"])
                    pool.indirect_dma_start(
                        out=sum_dram, out_offset=bass.IndirectOffsetOnAxis(ap=first_i[:, 0:1], axis=0),
                        in_=new[:, :], in_offset=None, bounds_check=NT * P - 1, oob_is_err=False).then_inc(stored, 16)

            @block.tensor
            def _(pe):
                pe.wait_ge(const, 2)
                with pe.Fori(0, ET) as t:
                    wait_then_pass(pe, c, t * STEP + 3, passed["pe"])
                    nc.tensor.matmul(bc[:, :], ones[:, :], diag[:, :], start=True, stop=True).then_inc(spread, 1)
                    wait_then_pass(pe, c, t * STEP + 7, passed["pe"])
                    nc.tensor.matmul(merged[:, :], same[:, :], msg[:, :], start=True, stop=True).then_inc(merge_done, 1)

            @block.vector
            def _(dve):
                nc.vector.memset(ones[:, :], 1.0).then_inc(const, 1)
                nc.vector.memset(zrow[:, :], 0.0).then_inc(const, 1)
                dve.wait_ge(e_in, 48)
                nc.vector.tensor_copy(src_f[:, :], src_i[:, :]).then_inc(c, 1)
                dve.wait_ge(c, 1)
                with dve.Fori(0, ET) as t:
                    k = [1]

                    def link(ins, t=t):
                        k[0] += 1
                        ins.then_inc(c, 1)
                        wait_then_pass(dve, c, t * STEP + k[0], passed["dve"])

                    wait_then_pass(dve, stored, t * 16 + 16, passed["dve"])
                    nc.vector.tensor_copy(wt[:, :], ew[:, bass.ds(t, 1)])
                    nc.vector.tensor_copy(to_i[:, :], src_i[:, bass.ds(t, 1)])
                    nc.vector.tensor_copy(from_i[:, :], dst_i[:, bass.ds(t, 1)]).then_inc(picked, 1)
                    link(nc.vector.tensor_copy(to_f[:, :], src_f[:, bass.ds(t, 1)]))
                    link(nc.vector.tensor_scalar(diag[:, :], ident[:, :], to_f[:, 0:1], None, ALU.mult))
                    wait_then_pass(dve, spread, t + 1, passed["dve"])
                    link(nc.vector.tensor_scalar(same[:, :], bc[:, :], to_f[:, 0:1], None, ALU.is_equal))
                    link(nc.vector.tensor_tensor(early[:, :], same[:, :], below[:, :], ALU.mult))
                    link(nc.vector.reduce_max(ecount[:, :], early[:, :], AX.X))
                    wait_then_pass(dve, gathered, t * 16 + 16, passed["dve"])
                    link(nc.vector.tensor_scalar(msg[:, :], rows[:, :], wt[:, 0:1], None, ALU.mult))
                    link(nc.vector.scalar_tensor_tensor(first_f[:, :], ecount[:, :], float(2 * NT * P), to_f[:, :],
                                                        ALU.mult, ALU.add))
                    link(nc.vector.tensor_copy(first_i[:, :], first_f[:, :]))
                    assert k[0] == STEP + 1
                    wait_then_pass(dve, merge_done, t + 1, passed["dve"])
                    wait_then_pass(dve, old_in, t * 16 + 16, passed["dve"])
                    nc.vector.tensor_tensor(new[:, :], merged[:, :], old[:, :], ALU.add).then_inc(new_done, 1)
                dve.sem_inc(h_done, 2)

                def add(g, pair, j, rows):
                    r = rows[0]
                    wait_then_pass(dve, h_in[j], pair * 16 + 16, passed["dve"])
                    a = hin[:, j, :, :] if len(rows) == GT else hin[:r, j, 0, :]
                    nc.vector.tensor_tensor(node_tiles(h, g, rows), node_tiles(h, g, rows), a,
                                            ALU.add).then_inc(h_done, 1)

                groups(dve, add)


def ffn_stage(nc, router_w, w1, b1, w2, b2, h, ident, iota8, out):
    with Stage(nc, "ffn") as st:
        w1s = st.sb("w1s", [P, NEXP, KC, D])
        w2s = st.sb("w2s", [P, NEXP, KC, D])
        b1s = st.sb("b1s", [P, NEXP, KC])
        b2s = st.sb("b2s", [NEXP, D])
        rws = st.sb("rws", [NEXP, D])
        rwT = st.sb("rwT", [P, KC, NEXP])
        eps = st.sb("eps", [P, 1])
        stats = st.sb("stats", [P, GT, 6])
        mv = st.sb("mv", [P, GT, 2])
        std = st.sb("std", [P, GT])
        rstd = st.sb("rstd", [P, GT])
        hn = st.sb("hn", [P, GT, D])
        hnT = st.sb("hnT", [P, 2, KC, GROUP])
        logits = st.sb("logits", [P, GT, NEXP])
        top = st.sb("top", [P, GT, 8])
        nmax = st.sb("nmax", [P, GT])
        ex = st.sb("ex", [P, GT, NEXP])
        z = st.sb("z", [P, GT])
        rz = st.sb("rz", [P, GT])
        prob = st.sb("prob", [P, GT, NEXP])
        best = st.sb("best", [P, GT, 8])
        best_i = st.sb("best_i", [P, GT, 8], U32)
        best_f = st.sb("best_f", [P, GT, 8])
        psum2 = st.sb("psum2", [P, GT])
        rs2 = st.sb("rs2", [P, GT])
        rw = st.sb("rw", [P, GT, 2])
        comb = st.sb("comb", [P, 2, GT, NEXP])
        comb2 = st.sb("comb2", [P, GT, NEXP])
        combT = st.sb("combT", [NEXP, GROUP])
        g1 = st.sb("g1", [P, 2, KC, GROUP])
        acc = st.sb("acc", [P, 2, GT, D])
        hp = [st.ps(f"hp{k}", [P, GROUP]) for k in range(2)]
        yp = [st.ps(f"yp{k}", [P, GROUP]) for k in range(4)]
        tp = [st.ps(f"tp{k}", [P, GROUP]) for k in range(2)]
        w_in = st.sem("w_in")
        const = st.sem("const")
        rw_turned = st.sem("rw_turned")
        rw_out = st.sem("rw_out")
        c = st.sem("c")
        std_done = st.sem("std_done")
        hn_turned = st.sem("hn_turned")
        hnT_out = st.sem("hnT_out")
        routed = st.sem("routed")
        expd = st.sem("expd")
        comb_done = st.sem("comb_done")
        comb_turned = st.sem("comb_turned")
        combT_out = st.sem("combT_out")
        b2_done = st.sem("b2_done")
        up = st.sem("up")
        act_done = st.sem("act_done")
        down = st.sem("down")
        added = st.sem("added")
        acc_done = st.sem("acc_done")
        out_done = [st.sem(f"out_done{j}") for j in range(2)]
        passed = {e: st.sem(f"passed_{e}") for e in ("sp", "act", "pe", "dve")}
        W_LOADS = 5

        with nc.Block() as block:

            @block.sync
            def _(sp):
                sp.dma_start(rws[:, :], router_w).then_inc(w_in, 16)
                sp.dma_start(w1s[:, :, :, :], w1.rearrange("e (c p) f -> p e c f", p=P)).then_inc(w_in, 16)
                sp.dma_start(w2s[:, :, :, :], w2.rearrange("e (c p) f -> p e c f", p=P)).then_inc(w_in, 16)
                with nc.allow_non_contiguous_dma(reason="one column per expert and feature block"):
                    for e in range(NEXP):
                        sp.dma_start(b1s[:, e, :], b1[e].rearrange("(c p) -> p c", p=P)).then_inc(w_in, 16)
                sp.dma_start(b2s[:, :], b2).then_inc(w_in, 16)

                def store(g, pair, j, rows):
                    wait_then_pass(sp, acc_done, g + 1, passed["sp"])
                    src = acc[:, j, :, :] if len(rows) == GT else acc[0:rows[0], j, 0, :]
                    sp.dma_start(node_view(out, g, rows), src).then_inc(out_done[j], 16)

                groups(sp, store)
                sp.wait_ge(out_done[0], 16 * (NG // 2 + 1))
                sp.wait_ge(out_done[1], 16 * (NG // 2))

            @block.tensor
            def _(pe):
                pe.wait_ge(w_in, 16 * (4 + NEXP))
                for k in range(KC):
                    last = nc.tensor.transpose(tp[0][:, k * NEXP:(k + 1) * NEXP], rws[:, k * P:(k + 1) * P],
                                               ident[0:NEXP, 0:NEXP])
                last.then_inc(rw_turned, 1)
                pe.wait_ge(rw_out, 1)
                pe.sem_inc(act_done, 1)
                pe.sem_inc(added, 2)

                def prep(g, pair, j, rows):
                    n, r = len(rows), rows[0]
                    wait_then_pass(pe, c, g * 9 + 3, passed["pe"])
                    for k in range(KC):
                        for s in range(n):
                            last = transpose(nc, tp[k][:, s * P:s * P + r], hn[:r, s, k * P:(k + 1) * P], ident, r)
                    last.then_inc(hn_turned, 1)
                    wait_then_pass(pe, hnT_out, g + 1, passed["pe"])
                    for s in range(n):
                        for k in range(KC):
                            last = nc.tensor.matmul(tp[0][:r, s * NEXP:(s + 1) * NEXP],
                                                    hnT[:, j, k, s * P:s * P + r], rwT[:, k, :],
                                                    start=k == 0, stop=k == KC - 1)
                    last.then_inc(routed, 1)
                    wait_then_pass(pe, comb_done, g + 1, passed["pe"])
                    for s in range(n):
                        last = transpose(nc, tp[1][0:NEXP, s * P:s * P + r], comb[:r, j, s, :], ident, r)
                    last.then_inc(comb_turned, 1)

                def experts(g, pair, j, rows):
                    n, r, w = len(rows), rows[0], sum(rows)
                    wait_then_pass(pe, combT_out, g + 1, passed["pe"])

                    def down_rows(dst_of, lhs_of, rhs_of, parts):
                        for s in range(n):
                            for k in range(parts):
                                last = nc.tensor.matmul(dst_of(s), lhs_of(s, k), rhs_of(k),
                                                        start=k == 0, stop=k == parts - 1)
                        return last

                    def y(s, half):
                        return yp[2 * half + s // 2][:r, (s % 2) * D:(s % 2 + 1) * D]

                    wait_then_pass(pe, added, g * (NEXP + 1) + 1, passed["pe"])
                    down_rows(lambda s: y(s, 0), lambda s, k: combT[:, s * P:s * P + r],
                              lambda k: b2s[:, :], 1).then_inc(b2_done, 1)
                    for e in range(NEXP + 1):
                        if e < NEXP:
                            wait_then_pass(pe, act_done, g * NEXP + e + 1, passed["pe"])
                            for f in range(KC):
                                for k in range(KC):
                                    last = nc.tensor.matmul(hp[f][:, 0:w], w1s[:, e, k, f * P:(f + 1) * P],
                                                            hnT[:, j, k, 0:w], start=k == 0, stop=k == KC - 1)
                            last.then_inc(up, 1)
                        if e > 0:
                            d = e - 1
                            half = (d + 1) % 2
                            wait_then_pass(pe, act_done, g * NEXP + d + 2, passed["pe"])
                            wait_then_pass(pe, added, g * (NEXP + 1) + d + 2, passed["pe"])
                            down_rows(lambda s: y(s, half), lambda s, k: g1[:, d % 2, k, s * P:s * P + r],
                                      lambda k: w2s[:, d, k, :], KC).then_inc(down, 1)

                def both(g, pair, j, rows):
                    prep(g, pair, j, rows)
                    experts(g, pair, j, rows)

                groups(pe, both)

            @block.scalar
            def _(act):
                act.wait_ge(const, 1)
                act.wait_ge(rw_turned, 1)
                nc.scalar.copy(rwT[:, :, :].rearrange("p c e -> p (c e)"), tp[0][:, 0:KC * NEXP]).then_inc(rw_out, 1)
                act.wait_ge(w_in, 16 * (4 + NEXP))
                act.wait_ge(rw_out, 1)

                def run(g, pair, j, rows):
                    n, r, w = len(rows), rows[0], sum(rows)
                    wait_then_pass(act, c, g * 9 + 1, passed["act"])
                    nc.scalar.activation(std[:r, 0:n], mv[:r, 0:n, 1], ACT.Sqrt, bias=eps[:r, :]).then_inc(std_done, 1)
                    wait_then_pass(act, hn_turned, g + 1, passed["act"])
                    for k in range(KC):
                        last = nc.scalar.copy(hnT[:, j, k, 0:w], tp[k][:, 0:w])
                    last.then_inc(hnT_out, 1)
                    wait_then_pass(act, c, g * 9 + 5, passed["act"])
                    for s in range(n):
                        last = nc.scalar.activation(ex[:r, s, :], logits[:r, s, :], ACT.Exp, bias=nmax[:r, s:s + 1],
                                                    accum_out=z[:r, s:s + 1])
                    last.then_inc(expd, 1)
                    wait_then_pass(act, comb_turned, g + 1, passed["act"])
                    nc.scalar.copy(combT[:, 0:w], tp[1][0:NEXP, 0:w]).then_inc(combT_out, 1)
                    for e in range(NEXP):
                        wait_then_pass(act, up, g * NEXP + e + 1, passed["act"])
                        if e >= 2:
                            wait_then_pass(act, down, g * NEXP + e - 1, passed["act"])
                        for f in range(KC):
                            last = nc.scalar.activation(g1[:, e % 2, f, 0:w], hp[f][:, 0:w], ACT.Gelu,
                                                        bias=b1s[:, e, f:f + 1])
                        last.then_inc(act_done, 1)

                groups(act, run)

            @block.vector
            def _(dve):
                nc.vector.memset(eps[:, :], EPS).then_inc(const, 1)

                def run(g, pair, j, rows):
                    n, r = len(rows), rows[0]
                    k = [0]

                    def link(ins):
                        k[0] += 1
                        ins.then_inc(c, 1)
                        wait_then_pass(dve, c, g * 9 + k[0], passed["dve"])

                    def tile(s):
                        return h[:r, g * GT, :] if n == 1 else h[:, bass.ds(g * GT + s, 1), :].rearrange("p a d -> p (a d)")

                    for s in range(n):
                        last = nc.vector.bn_stats(stats[:r, s, :], tile(s))
                    last.then_inc(const, 1)
                    wait_then_pass(dve, const, g + 2, passed["dve"])
                    for s in range(n):
                        last = nc.vector.bn_aggr(mv[:r, s, :], stats[:r, s, :])
                    link(last)
                    wait_then_pass(dve, std_done, g + 1, passed["dve"])
                    link(nc.vector.reciprocal(rstd[:r, 0:n], std[:r, 0:n]))
                    for s in range(n):
                        last = nc.vector.tensor_scalar(hn[:r, s, :], tile(s), mv[:r, s, 0:1], rstd[:r, s:s + 1],
                                                       ALU.subtract, ALU.mult)
                    link(last)
                    wait_then_pass(dve, routed, g + 1, passed["dve"])
                    nc.vector.tensor_copy(logits[:r, 0:n, :].rearrange("p s e -> p (s e)"), tp[0][:r, 0:n * NEXP])
                    for s in range(n):
                        last = nc.vector.max(top[:r, s, :], tp[0][:r, s * NEXP:(s + 1) * NEXP])
                    link(last)
                    link(nc.vector.tensor_scalar_mul(nmax[:r, 0:n], top[:r, 0:n, 0], -1.0))
                    wait_then_pass(dve, expd, g + 1, passed["dve"])
                    link(nc.vector.reciprocal(rz[:r, 0:n], z[:r, 0:n]))
                    for s in range(n):
                        last = nc.vector.tensor_scalar(prob[:r, s, :], ex[:r, s, :], rz[:r, s:s + 1], None, ALU.mult)
                    last.then_inc(top2, 1)
                    wait_then_pass(dve, top2, g * 6 + 1, passed["dve"])
                    for s in range(n):
                        last = nc.vector.max(best[:r, s, :], prob[:r, s, :])
                    last.then_inc(top2, 1)
                    wait_then_pass(dve, top2, g * 6 + 2, passed["dve"])
                    for s in range(n):
                        nc.vector.max_index(best_i[:r, s, :], best[:r, s, :], prob[:r, s, :])
                    nc.vector.tensor_tensor(psum2[:r, 0:n], best[:r, 0:n, 0], best[:r, 0:n, 1], ALU.add).then_inc(top2, 1)
                    wait_then_pass(dve, top2, g * 6 + 3, passed["dve"])
                    nc.vector.tensor_copy(best_f[:r, 0:n, :], best_i[:r, 0:n, :])
                    nc.vector.tensor_scalar_max(psum2[:r, 0:n], psum2[:r, 0:n], 1e-12).then_inc(top2, 1)
                    wait_then_pass(dve, top2, g * 6 + 4, passed["dve"])
                    nc.vector.reciprocal(rs2[:r, 0:n], psum2[:r, 0:n]).then_inc(top2, 1)
                    wait_then_pass(dve, top2, g * 6 + 5, passed["dve"])
                    for s in range(n):
                        last = nc.vector.tensor_scalar(rw[:r, s, :], best[:r, s, 0:2], rs2[:r, s:s + 1], None, ALU.mult)
                    last.then_inc(top2, 1)
                    wait_then_pass(dve, top2, g * 6 + 6, passed["dve"])
                    for s in range(n):
                        nc.vector.tensor_scalar(comb[:r, j, s, :], iota8[:r, :], best_f[:r, s, 0:1], rw[:r, s, 0:1],
                                                ALU.is_equal, ALU.mult)
                        last = nc.vector.tensor_scalar(comb2[:r, s, :], iota8[:r, :], best_f[:r, s, 1:2],
                                                       rw[:r, s, 1:2], ALU.is_equal, ALU.mult)
                    link(last)
                    nc.vector.tensor_tensor(comb[:r, j, 0:n, :], comb[:r, j, 0:n, :], comb2[:r, 0:n, :],
                                            ALU.add).then_inc(comb_done, 1)
                    wait_then_pass(dve, out_done[j], pair * 16, passed["dve"])
                    for s in range(n):
                        last = nc.vector.tensor_tensor(acc[:r, j, s, :], tile(s), hn[:r, s, :], ALU.add)
                    link(last)
                    wait_then_pass(dve, b2_done, g + 1, passed["dve"])
                    for s in range(n):
                        last = nc.vector.tensor_tensor(acc[:r, j, s, :], acc[:r, j, s, :],
                                                       yp[s // 2][:r, (s % 2) * D:(s % 2 + 1) * D], ALU.add)
                    last.then_inc(added, 1)
                    for e in range(NEXP):
                        half = (e + 1) % 2
                        wait_then_pass(dve, down, g * NEXP + e + 1, passed["dve"])
                        wait_then_pass(dve, added, g * (NEXP + 1) + e + 3, passed["dve"])
                        for s in range(n):
                            last = nc.vector.scalar_tensor_tensor(
                                acc[:r, j, s, :], yp[2 * half + s // 2][:r, (s % 2) * D:(s % 2 + 1) * D],
                                comb[:r, j, s, e:e + 1], acc[:r, j, s, :], ALU.mult, ALU.add)
                        last.then_inc(added, 1)
                    wait_then_pass(dve, added, g * (NEXP + 1) + NEXP + 3, passed["dve"])
                    dve.sem_inc(acc_done, 1)
                    link(nc.vector.memset(z1[:, :], 0.0))
                    assert k[0] == 9, k

                top2 = st.sem("top2")
                z1 = st.sb("z1", [P, 1])
                groups(dve, run)


def gps_layer(nc, x, src_t, dst_t, ew_t, W_qk, b_qk, W_v, b_v, gamma, beta, router_w, w1, b1, w2, b2, out):
    xn_dram = nc.dram_tensor("xn_scratch", [N, D], F32).ap()
    sum_dram = nc.dram_tensor("sum_scratch", [NT * P, D], F32).ap()
    with Stage(nc, "all") as st:
        ident = st.sb("ident", [P, P])
        below = st.sb("below", [P, P])
        iota8 = st.sb("iota8", [P, NEXP])
        iota8_i = st.sb("iota8_i", [P, NEXP], I32)
        xn = st.sb("xn", [P, NT, D])
        set_ = st.sem("set")
        with nc.Block() as block:

            @block.gpsimd
            def _(pool):
                pool.memset(ident[:, :], 0.0).then_inc(set_, 1)
                pool.memset(below[:, :], 1.0).then_inc(set_, 1)
                pool.iota(iota8_i[:, :], [[1, NEXP]], base=0, channel_multiplier=0).then_inc(set_, 1)
                pool.wait_ge(set_, 3)
                pool.affine_select(out=ident[:, :], in_=ident[:, :], compare_op=ALU.not_equal, fill=1.0,
                                   base=0, pattern=[[-1, P]], channel_multiplier=1)
                pool.affine_select(out=below[:, :], in_=below[:, :], compare_op=ALU.is_gt, fill=0.0,
                                   base=0, pattern=[[-1, P]], channel_multiplier=1)
                pool.tensor_copy(iota8[:, :], iota8_i[:, :])

        with Stage(nc, "turned") as tr:
            xnT = tr.sb("xnT", [P, KC, N])
            norm_stage(nc, x, xn_dram, xn, xnT, ident)
            mix_stage(nc, x, W_qk, b_qk, W_v, b_v, gamma, beta, xn, xnT, ident)
        edges_any_order(nc, src_t, dst_t, ew_t, xn_dram, sum_dram, xn, ident, below)
        ffn_stage(nc, router_w, w1, b1, w2, b2, xn, ident, iota8, out)


def edge_tiles(a, fill):
    return np.ascontiguousarray(np.concatenate([a, fill.astype(a.dtype)]).reshape(ET, P).T)


def kernel(x, src, dst, edge_weight, L0_mix_W_qk, L0_mix_b_qk, L0_mix_W_v, L0_mix_b_v, L0_mix_gamma, L0_mix_beta,
           L0_ffn_router_w, L0_ffn_w1, L0_ffn_b1, L0_ffn_w2, L0_ffn_b2):
    import concourse.bacc as bacc
    from concourse.bass_utils import run_bass_kernel_spmd

    pad = ET * P - E
    arrays = {
        "x": x,
        "src": edge_tiles(np.asarray(src), np.arange(pad) * P % N),
        "dst": edge_tiles(np.asarray(dst), np.full(pad, N - 1)),
        "edge_weight": edge_tiles(np.asarray(edge_weight), np.zeros(pad)),
        "W_qk": L0_mix_W_qk, "b_qk": L0_mix_b_qk, "W_v": L0_mix_W_v, "b_v": L0_mix_b_v,
        "gamma": L0_mix_gamma, "beta": L0_mix_beta, "router_w": L0_ffn_router_w,
        "w1": L0_ffn_w1, "b1": L0_ffn_b1, "w2": L0_ffn_w2, "b2": L0_ffn_b2,
    }
    arrays = {f"in_{k}": np.ascontiguousarray(v) for k, v in arrays.items()}
    nc = bacc.Bacc("TRN2", target_bir_lowering=False, num_devices=1)
    args = [nc.dram_tensor(k, v.shape, mybir.dt.from_np(v.dtype), kind="ExternalInput").ap() for k, v in arrays.items()]
    out = nc.dram_tensor("out", (N, D), F32, kind="ExternalOutput").ap()
    gps_layer(nc, *args, out)
    r = run_bass_kernel_spmd(nc, [arrays], core_ids=[0])
    return r.results[0]["out"]
```

```python
from contextlib import ExitStack

import concourse.bass as bass
from concourse import mybir
import numpy as np

F32 = mybir.dt.float32
BF16 = mybir.dt.bfloat16
I32 = mybir.dt.int32
U32 = mybir.dt.uint32
ALU = mybir.AluOpType
ACT = mybir.ActivationFunctionType
AX = mybir.AxisListType

P = 128
N = 6250
D = 256
KC = D // P
E = 200000
NEXP = 8
EPS = 1e-5
GT = 4
GROUP = GT * P
NG = N // GROUP
TAIL = N - NG * GROUP
NT = NG * GT + 1
CT = 29
NCH = -(-E // (CT * P))
ET = NCH * CT
NB = NT
CB = 6
NQ = NCH // CB
U3 = 3
NU = NCH // U3
assert 0 < TAIL <= P and NG % 2 == 0 and NQ * CB == NCH and NU * U3 == NCH and NB % 2 == 1 and NU % 2 == 0


def groups(eng, step):
    for j in range(2):
        step(j, 0, j, [P] * GT)
    with eng.Fori(1, NG // 2) as pair:
        for j in range(2):
            step(pair * 2 + j, pair, j, [P] * GT)
    step(NG, NG // 2, 0, [TAIL])


class Stage:

    def __init__(self, nc, name):
        self.nc, self.name, self.ctx, self.spaced = nc, name, ExitStack(), {}

    def __enter__(self):
        self.ctx.__enter__()
        return self

    def __exit__(self, *a):
        return self.ctx.__exit__(*a)

    def sb(self, name, shape, dt=F32):
        return self.ctx.enter_context(self.nc.sbuf_tensor(f"{self.name}_{name}", shape, dt))

    def ps(self, name, shape, dt=F32):
        return self.ctx.enter_context(self.nc.psum_tensor(f"{self.name}_{name}", shape, dt))

    def sem(self, name):
        return self.ctx.enter_context(self.nc.semaphore(f"{self.name}_{name}"))


def wait_then_pass(eng, sem, value, passed):
    if isinstance(value, int):
        if value > 0:
            eng.wait_ge(sem, value)
        return
    eng.wait_ge(sem, value)
    eng.sem_inc(passed, 1)


def node_view(dram, g, rows):
    if len(rows) == GT:
        return dram[bass.ds(g * GROUP, GROUP), :].rearrange("(s p) d -> p s d", p=P)
    return dram[g * GROUP:g * GROUP + rows[0], :]


def node_tiles(sb, g, rows):
    if len(rows) == GT:
        return sb[:, bass.ds(g * GT, GT), :]
    return sb[0:rows[0], g * GT, :]


def norm_stage(nc, x, xn_dram, xn, xnT, ident):
    with Stage(nc, "ln") as st:
        xin = st.sb("xin", [P, 2, GT, D])
        stats = st.sb("stats", [P, 2, GT, 6])
        mv = st.sb("mv", [P, 2, GT, 2])
        std = st.sb("std", [P, 2, GT])
        rstd = st.sb("rstd", [P, 2, GT])
        xnb = st.sb("xnb", [P, 2, GT, D])
        eps = st.sb("eps", [P, 1])
        tp = [st.ps(f"tp{k}", [P, GROUP]) for k in range(2 * KC)]
        x_in = [st.sem(f"x_in{j}") for j in range(2)]
        xn_out = [st.sem(f"xn_out{j}") for j in range(2)]
        xn_kept = [st.sem(f"xn_kept{j}") for j in range(2)]
        eps_set = st.sem("eps_set")
        stats_done = st.sem("stats_done")
        var_done = st.sem("var_done")
        std_done = st.sem("std_done")
        rstd_done = st.sem("rstd_done")
        xn_done = st.sem("xn_done")
        turned = st.sem("turned")
        evacuated = st.sem("evacuated")
        passed = {e: st.sem(f"passed_{e}") for e in ("sp", "act", "pe", "dve", "pool")}
        with nc.Block() as block:

            @block.sync
            def _(sp):
                def load(g, pair, j, rows):
                    wait_then_pass(sp, xn_done, g + 1, passed["sp"])
                    dst = xin[:, j, :, :] if len(rows) == GT else xin[0:rows[0], j, 0, :]
                    sp.dma_start(dst, node_view(x, g, rows)).then_inc(x_in[j], 16)

                groups(sp, load)

            @block.vector
            def _(dve):
                nc.vector.memset(eps[:, :], EPS).then_inc(eps_set, 1)
                dve.sem_inc(xn_done, 2)

                def normalise(g, pair, j, rows):
                    n, r = len(rows), rows[0]
                    wait_then_pass(dve, x_in[j], pair * 16 + 16, passed["dve"])
                    for s in range(n):
                        last = nc.vector.bn_stats(stats[:r, j, s, :], xin[:r, j, s, :])
                    last.then_inc(stats_done, 1)
                    wait_then_pass(dve, stats_done, g + 1, passed["dve"])
                    for s in range(n):
                        last = nc.vector.bn_aggr(mv[:r, j, s, :], stats[:r, j, s, :])
                    last.then_inc(var_done, 1)
                    wait_then_pass(dve, std_done, g + 1, passed["dve"])
                    nc.vector.reciprocal(rstd[:r, j, 0:n], std[:r, j, 0:n]).then_inc(rstd_done, 1)
                    wait_then_pass(dve, rstd_done, g + 1, passed["dve"])
                    wait_then_pass(dve, xn_out[j], pair * 16, passed["dve"])
                    wait_then_pass(dve, xn_kept[j], pair * 16, passed["dve"])
                    wait_then_pass(dve, evacuated, g + 1, passed["dve"])
                    for s in range(n):
                        last = nc.vector.tensor_scalar(
                            xnb[:r, j, s, :], xin[:r, j, s, :], mv[:r, j, s, 0:1],
                            rstd[:r, j, s:s + 1], ALU.subtract, ALU.mult)
                    last.then_inc(xn_done, 1)

                groups(dve, normalise)

            @block.tensor
            def _(pe):
                pe.sem_inc(evacuated, 2)

                def turn(g, pair, j, rows):
                    n, r = len(rows), rows[0]
                    wait_then_pass(pe, xn_done, g + 3, passed["pe"])
                    wait_then_pass(pe, evacuated, g + 1, passed["pe"])
                    for s in range(n):
                        for k in range(KC):
                            last = transpose(nc, tp[2 * j + k][:, s * P:s * P + r],
                                             xnb[:r, j, s, k * P:(k + 1) * P], ident, r)
                    last.then_inc(turned, 1)

                groups(pe, turn)

            @block.scalar
            def _(act):
                act.wait_ge(eps_set, 1)

                def finish(g, pair, j, rows):
                    n, r = len(rows), rows[0]
                    wait_then_pass(act, var_done, g + 1, passed["act"])
                    nc.scalar.activation(std[:r, j, 0:n], mv[:r, j, 0:n, 1], ACT.Sqrt,
                                         bias=eps[:r, :]).then_inc(std_done, 1)
                    wait_then_pass(act, xn_done, g + 3, passed["act"])
                    src = xnb[:, j, :, :] if n == GT else xnb[:r, j, 0, :]
                    act.dma_start(node_view(xn_dram, g, rows), src).then_inc(xn_out[j], 16)
                    act.dma_start(node_tiles(xn, g, rows), src).then_inc(xn_kept[j], 16)
                    wait_then_pass(act, turned, g + 1, passed["act"])
                    w = sum(rows)
                    for k in range(KC):
                        last = nc.scalar.copy(xnT[:, k, bass.ds(g * GROUP, w)], tp[2 * j + k][:, 0:w])
                    last.then_inc(evacuated, 1)

                groups(act, finish)
                for out in (xn_out, xn_kept):
                    act.wait_ge(out[0], 16 * (NG // 2 + 1))
                    act.wait_ge(out[1], 16 * (NG // 2))


def transpose(nc, out, in_, ident, rows):
    return nc.tensor.transpose(out, in_, ident[0:rows, 0:rows])


def mix_stage(nc, x, W_qk, b_qk, W_v, b_v, gamma, beta, xn, xnT, ident):
    with Stage(nc, "mix") as st:
        wq = st.sb("wq", [P, KC, D])
        wk = st.sb("wk", [P, KC, D])
        wv = st.sb("wv", [P, KC, D])
        bq = st.sb("bq", [P, KC])
        bk = st.sb("bk", [P, KC])
        bv = st.sb("bv", [1, D])
        gam = st.sb("gam", [P, KC])
        bet = st.sb("bet", [P, KC])
        ones = st.sb("ones", [P, P])
        zeros = st.sb("zeros", [P, P])
        eps = st.sb("eps", [P, 1])
        keyT = st.sb("keyT", [P, KC, N])
        ek = st.sb("ek", [P, 2, KC, GROUP])
        gsum = st.sb("gsum", [P, KC, NG + 1])
        tmax = st.sb("tmax", [P, KC])
        nmax = st.sb("nmax", [P, KC])
        esum = st.sb("esum", [P, KC])
        rsum = st.sb("rsum", [P, KC])
        pt = st.sb("pt", [P, 2, GT, D])
        M = st.sb("M", [P, KC, D])
        MT = st.sb("MT", [P, KC, D])
        wqT = st.sb("wqT", [P, KC, D])
        lam = st.sb("lam", [P, KC, D])
        bn = st.sb("bn", [P, KC, D])
        stats = st.sb("stats", [P, KC, 6])
        mv = st.sb("mv", [P, KC, 2])
        std = st.sb("std", [P, KC])
        rstd = st.sb("rstd", [P, KC])
        scl = st.sb("scl", [P, KC])
        msc = st.sb("msc", [P, KC])
        shf = st.sb("shf", [P, KC])
        bqb = st.sb("bqb", [P, KC, P])
        wqbn = st.sb("wqbn", [P, KC, D])
        qbias = st.sb("qbias", [P, D])
        xin = st.sb("xin", [P, 2, GT, D])
        xs = ek
        kp = [st.ps(f"kp{k}", [P, GROUP]) for k in range(4)]
        mp = [st.ps(f"mp{k}", [P, GROUP]) for k in range(2)]
        lp = [st.ps(f"lp{k}", [P, GROUP]) for k in range(2)]
        w_in = st.sem("w_in")
        const = st.sem("const")
        keyed = st.sem("keyed")
        key_out = st.sem("key_out")
        maxed = st.sem("maxed")
        neg = st.sem("neg")
        exped = st.sem("exped")
        p_turned = st.sem("p_turned")
        p_out = st.sem("p_out")
        p_used = st.sem("p_used")
        m_done = st.sem("m_done")
        c = st.sem("c")
        pe_c = st.sem("pe_c")
        act_c = st.sem("act_c")
        x_in = [st.sem(f"x_in{j}") for j in range(2)]
        xs_done = st.sem("xs_done")
        mixed = st.sem("mixed")
        xq_done = st.sem("xq_done")
        h_done = st.sem("h_done")
        passed = {e: st.sem(f"passed_{e}") for e in ("sp", "act", "pe", "dve")}
        W_LOADS = 8

        with nc.Block() as block:

            @block.sync
            def _(sp):
                for dst, src in ((wk, W_qk[1]), (wq, W_qk[0]), (wv, W_v)):
                    sp.dma_start(dst[:, :, :], src.rearrange("(c p) e -> p c e", p=P)).then_inc(w_in, 16)
                with nc.allow_non_contiguous_dma(reason="one column per feature block"):
                    for dst, src in ((bk, b_qk[1]), (bq, b_qk[0]), (gam, gamma), (bet, beta)):
                        sp.dma_start(dst[:, :], src.rearrange("(c p) -> p c", p=P)).then_inc(w_in, 16)
                sp.dma_start(bv[:, :], b_v.rearrange("(a e) -> a e", a=1)).then_inc(w_in, 16)

                def load(g, pair, j, rows):
                    wait_then_pass(sp, h_done, g + 1, passed["sp"])
                    dst = xin[:, j, :, :] if len(rows) == GT else xin[0:rows[0], j, 0, :]
                    sp.dma_start(dst, node_view(x, g, rows)).then_inc(x_in[j], 16)

                groups(sp, load)

            @block.tensor
            def _(pe):
                pe.wait_ge(w_in, 16 * W_LOADS)
                pe.wait_ge(const, 3)
                pe.sem_inc(key_out, 2)

                def keys(g, pair, j, rows):
                    w = sum(rows)
                    wait_then_pass(pe, key_out, g + 1, passed["pe"])
                    for e in range(KC):
                        for k in range(KC):
                            last = nc.tensor.matmul(kp[2 * j + e][:, 0:w], wk[:, k, e * P:(e + 1) * P],
                                                    xnT[:, k, bass.ds(g * GROUP, w)],
                                                    start=k == 0, stop=k == KC - 1)
                    last.then_inc(keyed, 1)

                groups(pe, keys)
                for e in range(KC):
                    nc.tensor.matmul(mp[e][:, 0:D], zeros[:, :], wk[:, 0, :], start=True, stop=False)
                pe.sem_inc(p_out, 2)

                def turn(g, j, rows):
                    wait_then_pass(pe, exped, g + 1, passed["pe"])
                    wait_then_pass(pe, p_out, g + 1, passed["pe"])
                    for s, r in enumerate(rows):
                        for e in range(KC):
                            last = transpose(nc, kp[2 * j + s // 2][0:r, (s % 2) * D + e * P:(s % 2) * D + (e + 1) * P],
                                             ek[:, j, e, s * P:s * P + r], ident, P)
                    last.then_inc(p_turned, 1)

                def accumulate(g, j, rows, stop):
                    wait_then_pass(pe, p_out, g + 3, passed["pe"])
                    for s, r in enumerate(rows):
                        xt = xn[:r, g * GT, :] if stop else \
                            xn[:, bass.ds(g * GT + s, 1), :].rearrange("p a d -> p (a d)")
                        for e in range(KC):
                            last = nc.tensor.matmul(mp[e][:, 0:D], pt[:r, j, s, e * P:(e + 1) * P], xt,
                                                    start=False, stop=stop)
                    last.then_inc(p_used, 1)

                whole = [P] * GT
                turn(0, 0, whole)
                with pe.Fori(0, NG // 2 - 1) as i:
                    turn(i * 2 + 1, 1, whole)
                    accumulate(i * 2, 0, whole, False)
                    turn(i * 2 + 2, 0, whole)
                    accumulate(i * 2 + 1, 1, whole, False)
                turn(NG - 1, 1, whole)
                accumulate(NG - 2, 0, whole, False)
                turn(NG, 0, [TAIL])
                accumulate(NG - 1, 1, whole, False)
                accumulate(NG, 0, [TAIL], True)
                pe.wait_ge(c, 4)
                for a in range(KC):
                    for b in range(KC):
                        nc.tensor.transpose(kp[a][:, b * P:(b + 1) * P], M[:, b, a * P:(a + 1) * P], ident[:, :])
                for a in range(KC):
                    for b in range(KC):
                        last = nc.tensor.transpose(kp[2 + a][:, b * P:(b + 1) * P], wq[:, b, a * P:(a + 1) * P],
                                                   ident[:, :])
                last.then_inc(pe_c, 1)
                pe.wait_ge(c, 5)
                for a in range(KC):
                    for k in range(KC):
                        nc.tensor.matmul(lp[a][:, 0:D], MT[:, k, a * P:(a + 1) * P], wv[:, k, :],
                                         start=k == 0, stop=False)
                    last = nc.tensor.matmul(lp[a][:, 0:D], ones[0:1, :], bv[:, :], start=False, stop=True)
                last.then_inc(pe_c, 1)
                pe.wait_ge(c, 13)
                for a in range(KC):
                    for k in range(KC):
                        nc.tensor.matmul(kp[a][:, 0:D], wqT[:, k, a * P:(a + 1) * P], bn[:, k, :],
                                         start=k == 0, stop=k == KC - 1)
                for k in range(KC):
                    last = nc.tensor.matmul(kp[2][:, 0:D], bqb[:, k, :], bn[:, k, :],
                                            start=k == 0, stop=k == KC - 1)
                last.then_inc(pe_c, 1)
                pe.wait_ge(c, 14)
                pe.sem_inc(xq_done, 2)

                def mix(g, pair, j, rows):
                    wait_then_pass(pe, xs_done, g + 3, passed["pe"])
                    wait_then_pass(pe, xq_done, g + 1, passed["pe"])
                    for s, r in enumerate(rows):
                        for k in range(KC):
                            last = nc.tensor.matmul(kp[2 * j + s // 2][:r, (s % 2) * D:(s % 2 + 1) * D],
                                                    xs[:, j, k, s * P:s * P + r], wqbn[:, k, :],
                                                    start=k == 0, stop=k == KC - 1)
                    last.then_inc(mixed, 1)

                groups(pe, mix)

            @block.scalar
            def _(act):
                act.wait_ge(w_in, 16 * W_LOADS)

                def key_evac(g, pair, j, rows):
                    w = sum(rows)
                    wait_then_pass(act, keyed, g + 1, passed["act"])
                    for e in range(KC):
                        last = nc.scalar.activation(keyT[:, e, bass.ds(g * GROUP, w)], kp[2 * j + e][:, 0:w],
                                                    ACT.Identity, bias=bk[:, e:e + 1])
                    last.then_inc(key_out, 1)

                groups(act, key_evac)
                act.wait_ge(neg, 1)

                def exps(g, pair, j, rows):
                    w = sum(rows)
                    wait_then_pass(act, p_turned, g + 1, passed["act"])
                    for e in range(KC):
                        last = nc.scalar.activation(ek[:, j, e, 0:w], keyT[:, e, bass.ds(g * GROUP, w)], ACT.Exp,
                                                    bias=nmax[:, e:e + 1], accum_out=gsum[:, e, bass.ds(g, 1)])
                    last.then_inc(exped, 1)

                act.sem_inc(p_turned, 2)
                groups(act, exps)
                act.wait_ge(c, 7)
                nc.scalar.activation(std[:, :], mv[:, :, 1], ACT.Sqrt, bias=eps[:, :]).then_inc(act_c, 1)
                act.sem_inc(xs_done, 2)

                def fix(g, pair, j, rows):
                    w = sum(rows)
                    wait_then_pass(act, mixed, g + 1, passed["act"])
                    for k in range(KC):
                        last = nc.scalar.copy(xs[:, j, k, 0:w], xnT[:, k, bass.ds(g * GROUP, w)])
                    last.then_inc(xs_done, 1)

                act.sem_inc(mixed, 2)
                groups(act, fix)

            @block.vector
            def _(dve):
                nc.vector.memset(ones[:, :], 1.0).then_inc(const, 1)
                nc.vector.memset(zeros[:, :], 0.0).then_inc(const, 1)
                nc.vector.memset(eps[:, :], EPS).then_inc(const, 1)
                dve.wait_ge(key_out, 2 + NG + 1)
                for e in range(KC):
                    last = nc.vector.reduce_max(tmax[:, e:e + 1], keyT[:, e, :], AX.X)
                last.then_inc(maxed, 1)
                dve.wait_ge(maxed, 1)
                nc.vector.tensor_scalar_mul(nmax[:, :], tmax[:, :], -1.0).then_inc(neg, 1)
                dve.sem_inc(p_used, 2)

                def evac(g, pair, j, rows):
                    wait_then_pass(dve, p_turned, g + 3, passed["dve"])
                    wait_then_pass(dve, p_used, g + 1, passed["dve"])
                    if len(rows) == GT:
                        for b in range(2):
                            last = nc.vector.tensor_copy(pt[:, j, 2 * b:2 * b + 2, :],
                                                         kp[2 * j + b][:, :].rearrange("p (s d) -> p s d", s=2))
                    else:
                        last = nc.vector.tensor_copy(pt[:rows[0], j, 0, :], kp[2 * j][:rows[0], 0:D])
                    last.then_inc(p_out, 1)

                groups(dve, evac)
                dve.wait_ge(exped, NG + 1)

                n = [0]

                def link(ins):
                    n[0] += 1
                    ins.then_inc(c, 1)
                    dve.wait_ge(c, n[0])

                for e in range(KC):
                    last = nc.vector.reduce_sum(esum[:, e:e + 1], gsum[:, e, :], AX.X)
                link(last)
                link(nc.vector.reciprocal(rsum[:, :], esum[:, :]))
                dve.wait_ge(p_used, NG + 3)
                for e in range(KC):
                    link(nc.vector.tensor_scalar(M[:, e, :], mp[e][:, 0:D], rsum[:, e:e + 1], None, ALU.mult))
                dve.wait_ge(pe_c, 1)
                for a in range(KC):
                    nc.vector.tensor_copy(MT[:, a, :], kp[a][:, 0:D])
                for a in range(KC):
                    last = nc.vector.tensor_copy(wqT[:, a, :], kp[2 + a][:, 0:D])
                link(last)
                dve.wait_ge(pe_c, 2)
                for a in range(KC):
                    nc.vector.tensor_copy(lam[:, a, :], lp[a][:, 0:D])
                    last = nc.vector.bn_stats(stats[:, a, :], lp[a][:, 0:D])
                link(last)
                for a in range(KC):
                    last = nc.vector.bn_aggr(mv[:, a, :], stats[:, a, :])
                link(last)
                dve.wait_ge(act_c, 1)
                link(nc.vector.reciprocal(rstd[:, :], std[:, :]))
                link(nc.vector.tensor_tensor(scl[:, :], rstd[:, :], gam[:, :], ALU.mult))
                link(nc.vector.tensor_tensor(msc[:, :], mv[:, :, 0], scl[:, :], ALU.mult))
                link(nc.vector.tensor_tensor(shf[:, :], bet[:, :], msc[:, :], ALU.subtract))
                for k in range(KC):
                    last = nc.vector.tensor_scalar(bn[:, k, :], lam[:, k, :], scl[:, k:k + 1], shf[:, k:k + 1],
                                                   ALU.mult, ALU.add)
                link(last)
                for k in range(KC):
                    last = nc.vector.tensor_scalar(bqb[:, k, :], ones[:, :], bq[:, k:k + 1], None, ALU.mult)
                link(last)
                assert n[0] == 13, n
                dve.wait_ge(pe_c, 3)
                for k in range(KC):
                    nc.vector.tensor_copy(wqbn[:, k, :], kp[k][:, 0:D])
                link(nc.vector.tensor_copy(qbias[:, :], kp[2][:, 0:D]))
                dve.sem_inc(h_done, 2)

                def add(g, pair, j, rows):
                    n, r = len(rows), rows[0]
                    wait_then_pass(dve, x_in[j], pair * 16 + 16, passed["dve"])
                    wait_then_pass(dve, mixed, g + 3, passed["dve"])
                    for s in range(n):
                        last = nc.vector.tensor_tensor(xin[:r, j, s, :], kp[2 * j + s // 2][:r, (s % 2) * D:(s % 2 + 1) * D],
                                                       xin[:r, j, s, :], ALU.add)
                    last.then_inc(xq_done, 1)
                    wait_then_pass(dve, xq_done, g + 3, passed["dve"])
                    if n == GT:
                        out, a, b = xn[:, bass.ds(g * GT, GT), :], xin[:, j, :, :], \
                            qbias[:, :].rearrange("p (a d) -> p a d", a=1).to_broadcast([P, GT, D])
                    else:
                        out, a, b = xn[:r, g * GT, :], xin[:r, j, 0, :], qbias[:r, :]
                    nc.vector.tensor_tensor(out, a, b, ALU.add).then_inc(h_done, 1)

                groups(dve, add)


def bin_stage(nc, src_t, dst_t, ew_t, rec, low_i, flag, ident, above, iota49, iota128):
    with Stage(nc, "bin") as st:
        src_i = st.sb("src_i", [P, ET], I32)
        dst_i = st.sb("dst_i", [P, ET], I32)
        ew = st.sb("ew", [P, ET])
        tmp_i = st.sb("tmp_i", [P, ET], I32)
        blk = st.sb("blk", [P, ET], BF16)
        dst_f = tmp_i[:, :].bitcast(F32)
        code = dst_i[:, :].bitcast(F32)
        cmin = st.sb("cmin", [P, NCH])
        cmax = st.sb("cmax", [P, NCH])
        low = st.sb("low", [NCH, 1])
        high = st.sb("high", [NCH, 1])
        span = st.sb("span", [NCH, 1])
        diag = st.sb("diag", [NCH, NCH])
        ones = st.sb("ones", [NCH, P])
        lowb = st.sb("lowb", [P, NCH])
        onehot = st.sb("onehot", [P, CT, CB, NB], BF16)
        before = st.sb("before", [P, CT + 1, CB, NB], BF16)
        slot = st.sb("slot", [P, CT, CB])
        most = st.sb("most", [P, NQ])
        most1 = st.sb("most1", [P, 1])
        R = st.sb("R", [P, 2, CT, 2, NB])
        SL = st.sb("SL", [P, 2, CT, P])
        row = st.sb("row", [1, P + NCH])
        bad = st.sb("bad", [1, 2])
        bad1 = st.sb("bad1", [1, 1])
        mm = st.ps("mm", [P, GROUP])
        base = st.ps("base", [P, CB * NB])
        bp = [st.ps(f"bp{j}", [P, 2 * NB]) for j in range(2)]
        e_in = st.sem("e_in")
        c = st.sem("c")
        pe_c = st.sem("pe_c")
        hot = st.sem("hot")
        based = st.sem("based")
        chain = st.sem("chain")
        rs_done = st.sem("rs_done")
        binned = st.sem("binned")
        kept = st.sem("kept")
        based_free = st.sem("based_free")
        flag_in = st.sem("flag_in")
        passed = {e: st.sem(f"passed_{e}") for e in ("act", "pe", "dve")}
        PIECES = [(0, 10), (10, 20), (20, CT)]
        LINKS = CT + 4

        with nc.Block() as block:

            @block.sync
            def _(sp):
                for d, x in ((src_i, src_t), (dst_i, dst_t), (ew, ew_t)):
                    sp.dma_start(d[:, :], x).then_inc(e_in, 16)

            @block.tensor
            def _(pe):
                pe.wait_ge(c, 5)
                nc.tensor.transpose(mm[0:NCH, 0:P], cmin[:, :], ident[:, :])
                nc.tensor.transpose(mm[0:NCH, P:2 * P], cmax[:, :], ident[:, :]).then_inc(pe_c, 1)
                pe.wait_ge(c, 9)
                nc.tensor.matmul(mm[:, 0:NCH], ones[:, :], diag[:, :], start=True, stop=True).then_inc(pe_c, 1)
                pe.sem_inc(kept, 2)

                with pe.Fori(0, NQ) as q:
                    for piece, (a, b) in enumerate(PIECES):
                        wait_then_pass(pe, hot, q * len(PIECES) + piece + 1, passed["pe"])
                        if piece == 0:
                            wait_then_pass(pe, based_free, q + 1, passed["pe"])
                        for j in range(a, b):
                            last = nc.tensor.matmul(base[:, :], above[:, :],
                                                    onehot[:, j, :, :].rearrange("p c b -> p (c b)"),
                                                    start=j == 0, stop=j == CT - 1)
                    last.then_inc(based, 1)
                    for k in range(CB):
                        wait_then_pass(pe, rs_done, q * CB + k + 1, passed["pe"])
                        wait_then_pass(pe, kept, q * CB + k + 1, passed["pe"])
                        for j in range(CT):
                            last = nc.tensor.matmul(bp[k % 2][:, :], SL[:, k % 2, j, :],
                                                    R[:, k % 2, j, :, :].rearrange("p w b -> p (w b)"),
                                                    start=j == 0, stop=j == CT - 1)
                        last.then_inc(binned, 1)
                pe.wait_ge(flag_in, 1)
                nc.tensor.transpose(mm[0:1, 0:P], most1[:, :], ident[:, :])
                nc.tensor.transpose(mm[0:1, P:P + NCH], span[:, :], ident[0:NCH, 0:NCH]).then_inc(pe_c, 1)

            @block.scalar
            def _(act):
                with act.Fori(0, NQ) as q:
                    for k in range(CB):
                        wait_then_pass(act, binned, q * CB + k + 3, passed["act"])
                        nc.scalar.copy(rec[:, :, 1:3, bass.ds(q * CB + k, 1)],
                                       bp[k % 2][:, :].rearrange("p (w b a) -> p b w a", w=2, a=1)).then_inc(kept, 1)

            @block.vector
            def _(dve):
                n = [0]

                def link(ins):
                    n[0] += 1
                    ins.then_inc(c, 1)
                    dve.wait_ge(c, n[0])

                nc.vector.memset(ones[:, :], 1.0)
                dve.wait_ge(e_in, 48)
                link(nc.vector.tensor_single_scalar(tmp_i[:, :], src_i[:, :], 7, op=ALU.arith_shift_right))
                link(nc.vector.tensor_copy(blk[:, :], tmp_i[:, :]))
                nc.vector.tensor_single_scalar(src_i[:, :], src_i[:, :], P - 1, op=ALU.bitwise_and)
                link(nc.vector.tensor_copy(dst_f, dst_i[:, :]))
                by_chunk = dst_f.rearrange("p (c j) -> p c j", j=CT)
                link(nc.vector.tensor_reduce(cmin[:, :], by_chunk, AX.X, ALU.min))
                link(nc.vector.tensor_reduce(cmax[:, :], by_chunk, AX.X, ALU.max))
                dve.wait_ge(pe_c, 1)
                nc.vector.tensor_reduce(low[:, :], mm[0:NCH, 0:P], AX.X, ALU.min)
                link(nc.vector.tensor_reduce(high[:, :], mm[0:NCH, P:2 * P], AX.X, ALU.max))
                link(nc.vector.tensor_scalar_min(low[:, :], low[:, :], float(N - P)))
                link(nc.vector.tensor_tensor(span[:, :], high[:, :], low[:, :], ALU.subtract))
                link(nc.vector.tensor_scalar(diag[:, :], ident[0:NCH, 0:NCH], low[:, 0:1], None, ALU.mult))
                dve.wait_ge(pe_c, 2)
                nc.vector.tensor_copy(low_i[:, :], mm[0:1, 0:NCH])
                link(nc.vector.tensor_copy(lowb[:, :], mm[:, 0:NCH]))
                link(nc.vector.tensor_tensor(by_chunk, by_chunk,
                                             lowb[:, :].rearrange("p (c a) -> p c a", a=1).to_broadcast([P, NCH, CT]),
                                             ALU.subtract))
                link(nc.vector.tensor_copy(code, src_i[:, :]))
                link(nc.vector.scalar_tensor_tensor(code, code, float(P), dst_f, ALU.mult, ALU.add))
                dve.sem_inc(based_free, 1)
                dve.sem_inc(binned, 2)

                with dve.Fori(0, NQ) as q:
                    m = [0]

                    def next_link(ins):
                        m[0] += 1
                        ins.then_inc(chain, 1)
                        wait_then_pass(dve, chain, q * LINKS + m[0], passed["dve"])

                    for a, b in PIECES:
                        for t in range(CB):
                            last = nc.vector.tensor_tensor(
                                onehot[:, a:b, t, :],
                                iota49[:, :].rearrange("p (a b) -> p a b", a=1).to_broadcast([P, b - a, NB]),
                                blk[:, bass.ds(q * CB * CT + t * CT + a, b - a)]
                                .rearrange("p (j a) -> p j a", a=1).to_broadcast([P, b - a, NB]), ALU.is_equal)
                        last.then_inc(hot, 1)
                    wait_then_pass(dve, based, q + 1, passed["dve"])
                    ins = nc.vector.tensor_copy(before[:, 0, :, :].rearrange("p c b -> p (c b)"), base[:, :])
                    next_link(ins)
                    dve.sem_inc(based_free, 1)
                    for j in range(CT):
                        next_link(nc.vector.tensor_tensor(before[:, j + 1, :, :], before[:, j, :, :],
                                                          onehot[:, j, :, :], ALU.add))
                    nc.vector.tensor_reduce(most[:, bass.ds(q, 1)],
                                            before[:, CT, :, :].rearrange("p c b -> p (c b)"), AX.X, ALU.max)
                    next_link(nc.vector.tensor_tensor(before[:, 0:CT, :, :].rearrange("p j c b -> p (j c b)"),
                                                      before[:, 0:CT, :, :].rearrange("p j c b -> p (j c b)"),
                                                      onehot[:, :, :, :].rearrange("p j c b -> p (j c b)"), ALU.mult))
                    next_link(nc.vector.tensor_reduce(slot[:, :, :].rearrange("p j c -> p (j c)"),
                                                      before[:, 0:CT, :, :].rearrange("p j c b -> p (j c) b"),
                                                      AX.X, ALU.add))
                    for k in range(CB):
                        wait_then_pass(dve, binned, q * CB + k + 1, passed["dve"])
                        for w, a in enumerate((code, ew[:, :])):
                            nc.vector.tensor_tensor(
                                R[:, k % 2, :, w, :], onehot[:, :, k, :],
                                a[:, bass.ds(q * CB * CT + k * CT, CT)]
                                .rearrange("p (j a) -> p j a", a=1).to_broadcast([P, CT, NB]), ALU.mult)
                        nc.vector.tensor_tensor(
                            SL[:, k % 2, :, :],
                            iota128[:, :].rearrange("p (a s) -> p a s", a=1).to_broadcast([P, CT, P]),
                            slot[:, :, k:k + 1].to_broadcast([P, CT, P]), ALU.is_equal).then_inc(rs_done, 1)
                    next_link(nc.vector.memset(most1[:, :], 0.0))
                    assert m[0] == LINKS, m
                dve.wait_ge(kept, NCH + 2)
                code_i = SL[:, 0, :, :].rearrange("p j s -> p (j s)")[:, 0:NB * NCH].bitcast(I32)
                part_i = SL[:, 1, :, :].rearrange("p j s -> p (j s)")[:, 0:NB * NCH].bitcast(I32)
                code_v = code_i.rearrange("p (b c) -> p b c", b=NB)
                link(nc.vector.tensor_copy(code_v, rec[:, :, 1, :]))
                link(nc.vector.tensor_single_scalar(part_i, code_i, P - 1, op=ALU.bitwise_and))
                link(nc.vector.tensor_copy(rec[:, :, 0, :], part_i.rearrange("p (b c) -> p b c", b=NB)))
                link(nc.vector.tensor_single_scalar(part_i, code_i, 7, op=ALU.arith_shift_right))
                link(nc.vector.tensor_copy(rec[:, :, 1, :], part_i.rearrange("p (b c) -> p b c", b=NB)))
                nc.vector.tensor_reduce(most1[:, :], most[:, :], AX.X, ALU.max).then_inc(flag_in, 1)
                dve.wait_ge(pe_c, 3)
                nc.vector.tensor_reduce(bad[:, 0:1], mm[0:1, 0:P], AX.X, ALU.max)
                link(nc.vector.tensor_reduce(bad[:, 1:2], mm[0:1, P:P + NCH], AX.X, ALU.max))
                nc.vector.tensor_single_scalar(row[:, 0:1], bad[:, 0:1], float(P), op=ALU.is_gt)
                link(nc.vector.tensor_single_scalar(row[:, 1:2], bad[:, 1:2], float(P), op=ALU.is_ge))
                link(nc.vector.tensor_reduce(bad1[:, :], row[:, 0:2], AX.X, ALU.max))
                link(nc.vector.tensor_copy(flag[:, :], bad1[:, :]))


def sum_stage(nc, src_t, dst_t, ew_t, xn_dram, sum_dram, rec, low_i, flag, h, ident, below, iota128):
    with Stage(nc, "sum") as st:
        win = st.sb("win", [P, NCH, D])
        col = st.sb("col", [P, 2, 3, NCH])
        src1h = st.sb("src1h", [P, 2, U3, P])
        dst1h = st.sb("dst1h", [P, 2, U3, P])
        A = st.sb("A", [P, 2, U3, P])
        ap = [st.ps(f"ap{j}", [P, U3 * P]) for j in range(2)]
        op = [st.ps(f"op{j}", [P, D]) for j in range(2)]
        win_in = st.sem("win_in")
        col_done = st.sem("col_done")
        hot_done = st.sem("hot_done")
        a_done = st.sem("a_done")
        a_kept = st.sem("a_kept")
        a_used = st.sem("a_used")
        summed = st.sem("summed")
        src_i = st.sb("src_i", [P, ET], I32)
        dst_i = st.sb("dst_i", [P, ET], I32)
        ew = st.sb("ew", [P, ET])
        src_f = st.sb("src_f", [P, ET])
        ones = st.sb("ones", [P, P])
        zrow = st.sb("zrow", [P, D])
        to_i = st.sb("to_i", [P, 1], I32)
        from_i = st.sb("from_i", [P, 1], I32)
        first_i = st.sb("first_i", [P, 1], I32)
        to_f = st.sb("to_f", [P, 1])
        wt = st.sb("wt", [P, 1])
        diag = st.sb("diag", [P, P])
        same = st.sb("same", [P, P])
        early = st.sb("early", [P, P])
        ecount = st.sb("ecount", [P, 1])
        first_f = st.sb("first_f", [P, 1])
        rows = st.sb("rows", [P, D])
        msg = st.sb("msg", [P, D])
        old = st.sb("old", [P, D])
        new = st.sb("new", [P, D])
        hin = st.sb("hin", [P, 2, GT, D])
        bc = st.ps("bc", [P, P])
        merged = st.ps("merged", [P, D])
        e_in = st.sem("e_in")
        const = st.sem("const")
        zeroed = st.sem("zeroed")
        picked = st.sem("picked")
        gathered = st.sem("gathered")
        old_in = st.sem("old_in")
        c = st.sem("c")
        spread = st.sem("spread")
        eq_done = st.sem("eq_done")
        merge_done = st.sem("merge_done")
        new_done = st.sem("new_done")
        stored = st.sem("stored")
        h_in = [st.sem(f"h_in{j}") for j in range(2)]
        h_done = st.sem("h_done")
        passed = {e: st.sem(f"passed_{e}") for e in ("sp", "pool", "pe", "dve", "act")}
        STEP = 8
        with nc.Block() as block:

            @block.sync
            def _(sp):
                with sp.If(sp.value_load(flag[0:1, 0:1], min_val=0, max_val=1) < 1):
                    with sp.Fori(0, NCH) as k:
                        first = sp.value_load(low_i[0:1, bass.ds(k, 1)], min_val=0, max_val=N - P)
                        sp.dma_start(win[:, bass.ds(k, 1), :], xn_dram[bass.ds(first, P), :]).then_inc(win_in, 16)
                with sp.Else():
                    for d, s in ((src_i, src_t), (dst_i, dst_t), (ew, ew_t)):
                        sp.dma_start(d[:, :], s).then_inc(e_in, 16)
                    sp.wait_ge(const, 2)
                    with sp.Fori(0, NT - 1) as t:
                        sp.dma_start(sum_dram[bass.ds(t * P, P), :], zrow[:, :]).then_inc(zeroed, 16)
                    sp.wait_ge(stored, 16 * (ET + 1))

                    def load(g, pair, j, rows):
                        wait_then_pass(sp, h_done, g + 1, passed["sp"])
                        dst = hin[:, j, :, :] if len(rows) == GT else hin[0:rows[0], j, 0, :]
                        sp.dma_start(dst, node_view(sum_dram, g, rows)).then_inc(h_in[j], 16)

                    groups(sp, load)

            @block.gpsimd
            def _(pool):
                with pool.If(pool.value_load(flag[0:1, 0:1], min_val=0, max_val=1) < 1):
                    pool.nop()
                with pool.Else():
                    pool.wait_ge(const, 2)
                    pool.dma_start(sum_dram[(NT - 1) * P:NT * P, :], zrow[:, :]).then_inc(stored, 16)
                    pool.wait_ge(zeroed, 16 * (NT - 1))
                    with pool.Fori(0, ET) as t:
                        wait_then_pass(pool, picked, t + 1, passed["pool"])
                        pool.indirect_dma_start(
                            out=rows[:, :], out_offset=None, in_=xn_dram,
                            in_offset=bass.IndirectOffsetOnAxis(ap=from_i[:, 0:1], axis=0)).then_inc(gathered, 16)
                        wait_then_pass(pool, stored, t * 16 + 16, passed["pool"])
                        pool.indirect_dma_start(
                            out=old[:, :], out_offset=None, in_=sum_dram,
                            in_offset=bass.IndirectOffsetOnAxis(ap=to_i[:, 0:1], axis=0)).then_inc(old_in, 16)
                        wait_then_pass(pool, new_done, t + 1, passed["pool"])
                        pool.indirect_dma_start(
                            out=sum_dram, out_offset=bass.IndirectOffsetOnAxis(ap=first_i[:, 0:1], axis=0),
                            in_=new[:, :], in_offset=None, bounds_check=NT * P - 1, oob_is_err=False).then_inc(stored, 16)

            @block.tensor
            def _(pe):
                with pe.If(pe.value_load(flag[0:1, 0:1], min_val=0, max_val=1) < 1):
                    pe.wait_ge(win_in, 16 * NCH)
                    pe.sem_inc(a_kept, 2)

                    def products(b, j):
                        wait_then_pass(pe, summed, b + 1, passed["pe"])
                        for u in range(NU + 1):
                            if u < NU:
                                wait_then_pass(pe, hot_done, b * NU + u + 1, passed["pe"])
                                wait_then_pass(pe, a_kept, b * NU + u + 1, passed["pe"])
                                for i in range(U3):
                                    last = nc.tensor.matmul(ap[u % 2][:, i * P:(i + 1) * P], src1h[:, u % 2, i, :],
                                                            dst1h[:, u % 2, i, :], start=True, stop=True)
                                last.then_inc(a_done, 1)
                            if u > 0:
                                v = u - 1
                                wait_then_pass(pe, a_kept, b * NU + v + 3, passed["pe"])
                                for i in range(U3):
                                    last = nc.tensor.matmul(op[j][:, :], A[:, v % 2, i, :], win[:, v * U3 + i, :],
                                                            start=v + i == 0, stop=v == NU - 1 and i == U3 - 1)
                                last.then_inc(a_used, 1)

                    with pe.Fori(0, NB // 2) as pair:
                        for j in range(2):
                            products(pair * 2 + j, j)
                    products(NB - 1, 0)
                with pe.Else():
                    pe.wait_ge(const, 2)
                    with pe.Fori(0, ET) as t:
                        wait_then_pass(pe, c, t * STEP + 3, passed["pe"])
                        nc.tensor.matmul(bc[:, :], ones[:, :], diag[:, :], start=True, stop=True).then_inc(spread, 1)
                        wait_then_pass(pe, c, t * STEP + 7, passed["pe"])
                        nc.tensor.matmul(merged[:, :], same[:, :], msg[:, :], start=True, stop=True).then_inc(merge_done, 1)

            @block.scalar
            def _(act):
                with act.If(act.value_load(flag[0:1, 0:1], min_val=0, max_val=1) < 1):
                    act.sem_inc(a_used, 2)

                    def keep(b):
                        for u in range(NU):
                            wait_then_pass(act, a_done, b * NU + u + 3, passed["act"])
                            wait_then_pass(act, a_used, b * NU + u + 1, passed["act"])
                            nc.scalar.copy(A[:, u % 2, :, :].rearrange("p c s -> p (c s)"),
                                           ap[u % 2][:, :]).then_inc(a_kept, 1)

                    with act.Fori(0, NB) as b:
                        keep(b)
                with act.Else():
                    act.nop()

            @block.vector
            def _(dve):
                with dve.If(dve.value_load(flag[0:1, 0:1], min_val=0, max_val=1) < 1):
                    dve.sem_inc(a_done, 2)
                    dve.sem_inc(summed, 2)

                    def finish(b, j, rows):
                        wait_then_pass(dve, a_used, b * NU + NU + 2, passed["dve"])
                        if isinstance(b, int):
                            out = h[:rows, b, :]
                        else:
                            out = h[:, bass.ds(b, 1), :].rearrange("p a d -> p (a d)")
                        nc.vector.tensor_tensor(out, out, op[j][:rows, :], ALU.add).then_inc(summed, 1)

                    def one_hots(b, j, before):
                        wait_then_pass(dve, hot_done, b * NU, passed["dve"])
                        nc.vector.tensor_copy(col[:, j, :, :], rec[:, b, :, :] if isinstance(b, int) else
                                              rec[:, bass.ds(b, 1), :, :].rearrange("p a w c -> p (a w) c"))\
                            .then_inc(col_done, 1)
                        wait_then_pass(dve, col_done, b + 1, passed["dve"])
                        for u in range(NU):
                            wait_then_pass(dve, a_done, b * NU + u + 1, passed["dve"])
                            nc.vector.tensor_tensor(
                                src1h[:, u % 2, :, :],
                                iota128[:, :].rearrange("p (a s) -> p a s", a=1).to_broadcast([P, U3, P]),
                                col[:, j, 0, u * U3:(u + 1) * U3].rearrange("p (c a) -> p c a", a=1)
                                .to_broadcast([P, U3, P]), ALU.is_equal)
                            for i in range(U3):
                                c_ = u * U3 + i
                                last = nc.vector.tensor_scalar(dst1h[:, u % 2, i, :], iota128[:, :],
                                                               col[:, j, 1, c_:c_ + 1], col[:, j, 2, c_:c_ + 1],
                                                               ALU.is_equal, ALU.mult)
                            last.then_inc(hot_done, 1)
                            if u == 3 and before:
                                before()

                    one_hots(0, 0, None)
                    with dve.Fori(0, NB // 2) as pair:
                        b = pair * 2
                        one_hots(b + 1, 1, lambda: finish(b, 0, P))
                        one_hots(b + 2, 0, lambda: finish(b + 1, 1, P))
                    finish(NB - 1, 0, TAIL)
                with dve.Else():
                    nc.vector.memset(ones[:, :], 1.0).then_inc(const, 1)
                    nc.vector.memset(zrow[:, :], 0.0).then_inc(const, 1)
                    dve.wait_ge(e_in, 48)
                    nc.vector.tensor_copy(src_f[:, :], src_i[:, :]).then_inc(c, 1)
                    dve.wait_ge(c, 1)
                    with dve.Fori(0, ET) as t:
                        k = [1]

                        def link(ins, t=t):
                            k[0] += 1
                            ins.then_inc(c, 1)
                            wait_then_pass(dve, c, t * STEP + k[0], passed["dve"])

                        wait_then_pass(dve, stored, t * 16 + 16, passed["dve"])
                        nc.vector.tensor_copy(wt[:, :], ew[:, bass.ds(t, 1)])
                        nc.vector.tensor_copy(to_i[:, :], src_i[:, bass.ds(t, 1)])
                        nc.vector.tensor_copy(from_i[:, :], dst_i[:, bass.ds(t, 1)]).then_inc(picked, 1)
                        link(nc.vector.tensor_copy(to_f[:, :], src_f[:, bass.ds(t, 1)]))
                        link(nc.vector.tensor_scalar(diag[:, :], ident[:, :], to_f[:, 0:1], None, ALU.mult))
                        wait_then_pass(dve, spread, t + 1, passed["dve"])
                        link(nc.vector.tensor_scalar(same[:, :], bc[:, :], to_f[:, 0:1], None, ALU.is_equal))
                        link(nc.vector.tensor_tensor(early[:, :], same[:, :], below[:, :], ALU.mult))
                        link(nc.vector.reduce_max(ecount[:, :], early[:, :], AX.X))
                        wait_then_pass(dve, gathered, t * 16 + 16, passed["dve"])
                        link(nc.vector.tensor_scalar(msg[:, :], rows[:, :], wt[:, 0:1], None, ALU.mult))
                        link(nc.vector.scalar_tensor_tensor(first_f[:, :], ecount[:, :], float(2 * NT * P), to_f[:, :],
                                                            ALU.mult, ALU.add))
                        link(nc.vector.tensor_copy(first_i[:, :], first_f[:, :]))
                        assert k[0] == STEP + 1
                        wait_then_pass(dve, merge_done, t + 1, passed["dve"])
                        wait_then_pass(dve, old_in, t * 16 + 16, passed["dve"])
                        nc.vector.tensor_tensor(new[:, :], merged[:, :], old[:, :], ALU.add).then_inc(new_done, 1)
                    dve.sem_inc(h_done, 2)

                    def add(g, pair, j, rows):
                        r = rows[0]
                        wait_then_pass(dve, h_in[j], pair * 16 + 16, passed["dve"])
                        a = hin[:, j, :, :] if len(rows) == GT else hin[:r, j, 0, :]
                        nc.vector.tensor_tensor(node_tiles(h, g, rows), node_tiles(h, g, rows), a,
                                                ALU.add).then_inc(h_done, 1)

                    groups(dve, add)


def ffn_stage(nc, router_w, w1, b1, w2, b2, h, ident, iota8, out):
    with Stage(nc, "ffn") as st:
        w1s = st.sb("w1s", [P, NEXP, KC, D])
        w2s = st.sb("w2s", [P, NEXP, KC, D])
        b1s = st.sb("b1s", [P, NEXP, KC])
        b2s = st.sb("b2s", [NEXP, D])
        rws = st.sb("rws", [NEXP, D])
        rwT = st.sb("rwT", [P, KC, NEXP])
        eps = st.sb("eps", [P, 1])
        stats = st.sb("stats", [P, GT, 6])
        mv = st.sb("mv", [P, GT, 2])
        std = st.sb("std", [P, GT])
        rstd = st.sb("rstd", [P, GT])
        hn = st.sb("hn", [P, GT, D])
        hnT = st.sb("hnT", [P, 2, KC, GROUP])
        logits = st.sb("logits", [P, GT, NEXP])
        top = st.sb("top", [P, GT, 8])
        nmax = st.sb("nmax", [P, GT])
        ex = st.sb("ex", [P, GT, NEXP])
        z = st.sb("z", [P, GT])
        rz = st.sb("rz", [P, GT])
        prob = st.sb("prob", [P, GT, NEXP])
        best = st.sb("best", [P, GT, 8])
        best_i = st.sb("best_i", [P, GT, 8], U32)
        best_f = st.sb("best_f", [P, GT, 8])
        psum2 = st.sb("psum2", [P, GT])
        rs2 = st.sb("rs2", [P, GT])
        rw = st.sb("rw", [P, GT, 2])
        comb = st.sb("comb", [P, 2, GT, NEXP])
        comb2 = st.sb("comb2", [P, GT, NEXP])
        combT = st.sb("combT", [NEXP, GROUP])
        g1 = st.sb("g1", [P, 2, KC, GROUP])
        acc = st.sb("acc", [P, 2, GT, D])
        hp = [st.ps(f"hp{k}", [P, GROUP]) for k in range(2)]
        yp = [st.ps(f"yp{k}", [P, GROUP]) for k in range(4)]
        tp = [st.ps(f"tp{k}", [P, GROUP]) for k in range(2)]
        w_in = st.sem("w_in")
        const = st.sem("const")
        rw_turned = st.sem("rw_turned")
        rw_out = st.sem("rw_out")
        c = st.sem("c")
        std_done = st.sem("std_done")
        hn_turned = st.sem("hn_turned")
        hnT_out = st.sem("hnT_out")
        routed = st.sem("routed")
        expd = st.sem("expd")
        comb_done = st.sem("comb_done")
        comb_turned = st.sem("comb_turned")
        combT_out = st.sem("combT_out")
        b2_done = st.sem("b2_done")
        up = st.sem("up")
        act_done = st.sem("act_done")
        down = st.sem("down")
        added = st.sem("added")
        acc_done = st.sem("acc_done")
        out_done = [st.sem(f"out_done{j}") for j in range(2)]
        passed = {e: st.sem(f"passed_{e}") for e in ("sp", "act", "pe", "dve")}
        W_LOADS = 5

        with nc.Block() as block:

            @block.sync
            def _(sp):
                sp.dma_start(rws[:, :], router_w).then_inc(w_in, 16)
                sp.dma_start(w1s[:, :, :, :], w1.rearrange("e (c p) f -> p e c f", p=P)).then_inc(w_in, 16)
                sp.dma_start(w2s[:, :, :, :], w2.rearrange("e (c p) f -> p e c f", p=P)).then_inc(w_in, 16)
                with nc.allow_non_contiguous_dma(reason="one column per expert and feature block"):
                    for e in range(NEXP):
                        sp.dma_start(b1s[:, e, :], b1[e].rearrange("(c p) -> p c", p=P)).then_inc(w_in, 16)
                sp.dma_start(b2s[:, :], b2).then_inc(w_in, 16)

                def store(g, pair, j, rows):
                    wait_then_pass(sp, acc_done, g + 1, passed["sp"])
                    src = acc[:, j, :, :] if len(rows) == GT else acc[0:rows[0], j, 0, :]
                    sp.dma_start(node_view(out, g, rows), src).then_inc(out_done[j], 16)

                groups(sp, store)
                sp.wait_ge(out_done[0], 16 * (NG // 2 + 1))
                sp.wait_ge(out_done[1], 16 * (NG // 2))

            @block.tensor
            def _(pe):
                pe.wait_ge(w_in, 16 * (4 + NEXP))
                for k in range(KC):
                    last = nc.tensor.transpose(tp[0][:, k * NEXP:(k + 1) * NEXP], rws[:, k * P:(k + 1) * P],
                                               ident[0:NEXP, 0:NEXP])
                last.then_inc(rw_turned, 1)
                pe.wait_ge(rw_out, 1)
                pe.sem_inc(act_done, 1)
                pe.sem_inc(added, 2)

                def prep(g, pair, j, rows):
                    n, r = len(rows), rows[0]
                    wait_then_pass(pe, c, g * 9 + 3, passed["pe"])
                    for k in range(KC):
                        for s in range(n):
                            last = transpose(nc, tp[k][:, s * P:s * P + r], hn[:r, s, k * P:(k + 1) * P], ident, r)
                    last.then_inc(hn_turned, 1)
                    wait_then_pass(pe, hnT_out, g + 1, passed["pe"])
                    for s in range(n):
                        for k in range(KC):
                            last = nc.tensor.matmul(tp[0][:r, s * NEXP:(s + 1) * NEXP],
                                                    hnT[:, j, k, s * P:s * P + r], rwT[:, k, :],
                                                    start=k == 0, stop=k == KC - 1)
                    last.then_inc(routed, 1)
                    wait_then_pass(pe, comb_done, g + 1, passed["pe"])
                    for s in range(n):
                        last = transpose(nc, tp[1][0:NEXP, s * P:s * P + r], comb[:r, j, s, :], ident, r)
                    last.then_inc(comb_turned, 1)

                def experts(g, pair, j, rows):
                    n, r, w = len(rows), rows[0], sum(rows)
                    wait_then_pass(pe, combT_out, g + 1, passed["pe"])

                    def down_rows(dst_of, lhs_of, rhs_of, parts):
                        for s in range(n):
                            for k in range(parts):
                                last = nc.tensor.matmul(dst_of(s), lhs_of(s, k), rhs_of(k),
                                                        start=k == 0, stop=k == parts - 1)
                        return last

                    def y(s, half):
                        return yp[2 * half + s // 2][:r, (s % 2) * D:(s % 2 + 1) * D]

                    wait_then_pass(pe, added, g * (NEXP + 1) + 1, passed["pe"])
                    down_rows(lambda s: y(s, 0), lambda s, k: combT[:, s * P:s * P + r],
                              lambda k: b2s[:, :], 1).then_inc(b2_done, 1)
                    for e in range(NEXP + 1):
                        if e < NEXP:
                            wait_then_pass(pe, act_done, g * NEXP + e + 1, passed["pe"])
                            for f in range(KC):
                                for k in range(KC):
                                    last = nc.tensor.matmul(hp[f][:, 0:w], w1s[:, e, k, f * P:(f + 1) * P],
                                                            hnT[:, j, k, 0:w], start=k == 0, stop=k == KC - 1)
                            last.then_inc(up, 1)
                        if e > 0:
                            d = e - 1
                            half = (d + 1) % 2
                            wait_then_pass(pe, act_done, g * NEXP + d + 2, passed["pe"])
                            wait_then_pass(pe, added, g * (NEXP + 1) + d + 2, passed["pe"])
                            down_rows(lambda s: y(s, half), lambda s, k: g1[:, d % 2, k, s * P:s * P + r],
                                      lambda k: w2s[:, d, k, :], KC).then_inc(down, 1)

                def both(g, pair, j, rows):
                    prep(g, pair, j, rows)
                    experts(g, pair, j, rows)

                groups(pe, both)

            @block.scalar
            def _(act):
                act.wait_ge(const, 1)
                act.wait_ge(rw_turned, 1)
                nc.scalar.copy(rwT[:, :, :].rearrange("p c e -> p (c e)"), tp[0][:, 0:KC * NEXP]).then_inc(rw_out, 1)
                act.wait_ge(w_in, 16 * (4 + NEXP))
                act.wait_ge(rw_out, 1)

                def run(g, pair, j, rows):
                    n, r, w = len(rows), rows[0], sum(rows)
                    wait_then_pass(act, c, g * 9 + 1, passed["act"])
                    nc.scalar.activation(std[:r, 0:n], mv[:r, 0:n, 1], ACT.Sqrt, bias=eps[:r, :]).then_inc(std_done, 1)
                    wait_then_pass(act, hn_turned, g + 1, passed["act"])
                    for k in range(KC):
                        last = nc.scalar.copy(hnT[:, j, k, 0:w], tp[k][:, 0:w])
                    last.then_inc(hnT_out, 1)
                    wait_then_pass(act, c, g * 9 + 5, passed["act"])
                    for s in range(n):
                        last = nc.scalar.activation(ex[:r, s, :], logits[:r, s, :], ACT.Exp, bias=nmax[:r, s:s + 1],
                                                    accum_out=z[:r, s:s + 1])
                    last.then_inc(expd, 1)
                    wait_then_pass(act, comb_turned, g + 1, passed["act"])
                    nc.scalar.copy(combT[:, 0:w], tp[1][0:NEXP, 0:w]).then_inc(combT_out, 1)
                    for e in range(NEXP):
                        wait_then_pass(act, up, g * NEXP + e + 1, passed["act"])
                        if e >= 2:
                            wait_then_pass(act, down, g * NEXP + e - 1, passed["act"])
                        for f in range(KC):
                            last = nc.scalar.activation(g1[:, e % 2, f, 0:w], hp[f][:, 0:w], ACT.Gelu,
                                                        bias=b1s[:, e, f:f + 1])
                        last.then_inc(act_done, 1)

                groups(act, run)

            @block.vector
            def _(dve):
                nc.vector.memset(eps[:, :], EPS).then_inc(const, 1)

                def run(g, pair, j, rows):
                    n, r = len(rows), rows[0]
                    k = [0]

                    def link(ins):
                        k[0] += 1
                        ins.then_inc(c, 1)
                        wait_then_pass(dve, c, g * 9 + k[0], passed["dve"])

                    def tile(s):
                        return h[:r, g * GT, :] if n == 1 else h[:, bass.ds(g * GT + s, 1), :].rearrange("p a d -> p (a d)")

                    for s in range(n):
                        last = nc.vector.bn_stats(stats[:r, s, :], tile(s))
                    last.then_inc(const, 1)
                    wait_then_pass(dve, const, g + 2, passed["dve"])
                    for s in range(n):
                        last = nc.vector.bn_aggr(mv[:r, s, :], stats[:r, s, :])
                    link(last)
                    wait_then_pass(dve, std_done, g + 1, passed["dve"])
                    link(nc.vector.reciprocal(rstd[:r, 0:n], std[:r, 0:n]))
                    for s in range(n):
                        last = nc.vector.tensor_scalar(hn[:r, s, :], tile(s), mv[:r, s, 0:1], rstd[:r, s:s + 1],
                                                       ALU.subtract, ALU.mult)
                    link(last)
                    wait_then_pass(dve, routed, g + 1, passed["dve"])
                    nc.vector.tensor_copy(logits[:r, 0:n, :].rearrange("p s e -> p (s e)"), tp[0][:r, 0:n * NEXP])
                    for s in range(n):
                        last = nc.vector.max(top[:r, s, :], tp[0][:r, s * NEXP:(s + 1) * NEXP])
                    link(last)
                    link(nc.vector.tensor_scalar_mul(nmax[:r, 0:n], top[:r, 0:n, 0], -1.0))
                    wait_then_pass(dve, expd, g + 1, passed["dve"])
                    link(nc.vector.reciprocal(rz[:r, 0:n], z[:r, 0:n]))
                    for s in range(n):
                        last = nc.vector.tensor_scalar(prob[:r, s, :], ex[:r, s, :], rz[:r, s:s + 1], None, ALU.mult)
                    last.then_inc(top2, 1)
                    wait_then_pass(dve, top2, g * 6 + 1, passed["dve"])
                    for s in range(n):
                        last = nc.vector.max(best[:r, s, :], prob[:r, s, :])
                    last.then_inc(top2, 1)
                    wait_then_pass(dve, top2, g * 6 + 2, passed["dve"])
                    for s in range(n):
                        nc.vector.max_index(best_i[:r, s, :], best[:r, s, :], prob[:r, s, :])
                    nc.vector.tensor_tensor(psum2[:r, 0:n], best[:r, 0:n, 0], best[:r, 0:n, 1], ALU.add).then_inc(top2, 1)
                    wait_then_pass(dve, top2, g * 6 + 3, passed["dve"])
                    nc.vector.tensor_copy(best_f[:r, 0:n, :], best_i[:r, 0:n, :])
                    nc.vector.tensor_scalar_max(psum2[:r, 0:n], psum2[:r, 0:n], 1e-12).then_inc(top2, 1)
                    wait_then_pass(dve, top2, g * 6 + 4, passed["dve"])
                    nc.vector.reciprocal(rs2[:r, 0:n], psum2[:r, 0:n]).then_inc(top2, 1)
                    wait_then_pass(dve, top2, g * 6 + 5, passed["dve"])
                    for s in range(n):
                        last = nc.vector.tensor_scalar(rw[:r, s, :], best[:r, s, 0:2], rs2[:r, s:s + 1], None, ALU.mult)
                    last.then_inc(top2, 1)
                    wait_then_pass(dve, top2, g * 6 + 6, passed["dve"])
                    for s in range(n):
                        nc.vector.tensor_scalar(comb[:r, j, s, :], iota8[:r, :], best_f[:r, s, 0:1], rw[:r, s, 0:1],
                                                ALU.is_equal, ALU.mult)
                        last = nc.vector.tensor_scalar(comb2[:r, s, :], iota8[:r, :], best_f[:r, s, 1:2],
                                                       rw[:r, s, 1:2], ALU.is_equal, ALU.mult)
                    link(last)
                    nc.vector.tensor_tensor(comb[:r, j, 0:n, :], comb[:r, j, 0:n, :], comb2[:r, 0:n, :],
                                            ALU.add).then_inc(comb_done, 1)
                    wait_then_pass(dve, out_done[j], pair * 16, passed["dve"])
                    for s in range(n):
                        last = nc.vector.tensor_tensor(acc[:r, j, s, :], tile(s), hn[:r, s, :], ALU.add)
                    link(last)
                    wait_then_pass(dve, b2_done, g + 1, passed["dve"])
                    for s in range(n):
                        last = nc.vector.tensor_tensor(acc[:r, j, s, :], acc[:r, j, s, :],
                                                       yp[s // 2][:r, (s % 2) * D:(s % 2 + 1) * D], ALU.add)
                    last.then_inc(added, 1)
                    for e in range(NEXP):
                        half = (e + 1) % 2
                        wait_then_pass(dve, down, g * NEXP + e + 1, passed["dve"])
                        wait_then_pass(dve, added, g * (NEXP + 1) + e + 3, passed["dve"])
                        for s in range(n):
                            last = nc.vector.scalar_tensor_tensor(
                                acc[:r, j, s, :], yp[2 * half + s // 2][:r, (s % 2) * D:(s % 2 + 1) * D],
                                comb[:r, j, s, e:e + 1], acc[:r, j, s, :], ALU.mult, ALU.add)
                        last.then_inc(added, 1)
                    wait_then_pass(dve, added, g * (NEXP + 1) + NEXP + 3, passed["dve"])
                    dve.sem_inc(acc_done, 1)
                    link(nc.vector.memset(z1[:, :], 0.0))
                    assert k[0] == 9, k

                top2 = st.sem("top2")
                z1 = st.sb("z1", [P, 1])
                groups(dve, run)


def gps_layer(nc, x, src_t, dst_t, ew_t, W_qk, b_qk, W_v, b_v, gamma, beta, router_w, w1, b1, w2, b2, out):
    xn_dram = nc.dram_tensor("xn_scratch", [N, D], F32).ap()
    sum_dram = nc.dram_tensor("sum_scratch", [NT * P, D], F32).ap()
    with Stage(nc, "all") as st:
        ident = st.sb("ident", [P, P])
        below = st.sb("below", [P, P])
        iota8 = st.sb("iota8", [P, NEXP])
        above = st.sb("above", [P, P], BF16)
        above_f = st.sb("above_f", [P, P])
        iota128 = st.sb("iota128", [P, P])
        iota49 = st.sb("iota49", [P, NB], BF16)
        iota_i = st.sb("iota_i", [P, P], I32)
        flag = st.sb("flag", [1, 1], I32)
        low_i = st.sb("low_i", [1, NCH], I32)
        xn = st.sb("xn", [P, NT, D])
        set_ = st.sem("set")
        with nc.Block() as block:

            @block.gpsimd
            def _(pool):
                pool.memset(ident[:, :], 0.0).then_inc(set_, 1)
                pool.memset(below[:, :], 1.0).then_inc(set_, 1)
                pool.memset(above_f[:, :], 1.0).then_inc(set_, 1)
                pool.iota(iota_i[:, :], [[1, P]], base=0, channel_multiplier=0).then_inc(set_, 1)
                pool.wait_ge(set_, 4)
                pool.affine_select(out=ident[:, :], in_=ident[:, :], compare_op=ALU.not_equal, fill=1.0,
                                   base=0, pattern=[[-1, P]], channel_multiplier=1)
                pool.affine_select(out=below[:, :], in_=below[:, :], compare_op=ALU.is_gt, fill=0.0,
                                   base=0, pattern=[[-1, P]], channel_multiplier=1)
                pool.affine_select(out=above_f[:, :], in_=above_f[:, :], compare_op=ALU.is_gt, fill=0.0,
                                   base=0, pattern=[[1, P]], channel_multiplier=-1).then_inc(set_, 1)
                pool.wait_ge(set_, 5)
                pool.tensor_copy(above[:, :], above_f[:, :])
                pool.tensor_copy(iota8[:, :], iota_i[:, 0:NEXP])
                pool.tensor_copy(iota49[:, :], iota_i[:, 0:NB])
                pool.tensor_copy(iota128[:, :], iota_i[:, :])

        with Stage(nc, "turned") as tr:
            xnT = tr.sb("xnT", [P, KC, N])
            norm_stage(nc, x, xn_dram, xn, xnT, ident)
            mix_stage(nc, x, W_qk, b_qk, W_v, b_v, gamma, beta, xn, xnT, ident)
        with Stage(nc, "bins") as bs:
            rec = bs.sb("rec", [P, NB, 3, NCH])
            bin_stage(nc, src_t, dst_t, ew_t, rec, low_i, flag, ident, above, iota49, iota128)
            sum_stage(nc, src_t, dst_t, ew_t, xn_dram, sum_dram, rec, low_i, flag, xn, ident, below, iota128)
        ffn_stage(nc, router_w, w1, b1, w2, b2, xn, ident, iota8, out)


def edge_tiles(a, fill):
    return np.ascontiguousarray(np.concatenate([a, fill.astype(a.dtype)]).reshape(ET, P).T)


def kernel(x, src, dst, edge_weight, L0_mix_W_qk, L0_mix_b_qk, L0_mix_W_v, L0_mix_b_v, L0_mix_gamma, L0_mix_beta,
           L0_ffn_router_w, L0_ffn_w1, L0_ffn_b1, L0_ffn_w2, L0_ffn_b2):
    import concourse.bacc as bacc
    from concourse.bass_utils import run_bass_kernel_spmd

    pad = ET * P - E
    arrays = {
        "x": x,
        "src": edge_tiles(np.asarray(src), np.arange(pad) * P % N),
        "dst": edge_tiles(np.asarray(dst), np.full(pad, N - 1)),
        "edge_weight": edge_tiles(np.asarray(edge_weight), np.zeros(pad)),
        "W_qk": L0_mix_W_qk, "b_qk": L0_mix_b_qk, "W_v": L0_mix_W_v, "b_v": L0_mix_b_v,
        "gamma": L0_mix_gamma, "beta": L0_mix_beta, "router_w": L0_ffn_router_w,
        "w1": L0_ffn_w1, "b1": L0_ffn_b1, "w2": L0_ffn_w2, "b2": L0_ffn_b2,
    }
    arrays = {f"in_{k}": np.ascontiguousarray(v) for k, v in arrays.items()}
    nc = bacc.Bacc("TRN2", target_bir_lowering=False, num_devices=1)
    args = [nc.dram_tensor(k, v.shape, mybir.dt.from_np(v.dtype), kind="ExternalInput").ap() for k, v in arrays.items()]
    out = nc.dram_tensor("out", (N, D), F32, kind="ExternalOutput").ap()
    gps_layer(nc, *args, out)
    r = run_bass_kernel_spmd(nc, [arrays], core_ids=[0])
    return r.results[0]["out"]
```

```python
from contextlib import ExitStack

import concourse.bass as bass
from concourse import mybir
import numpy as np

F32 = mybir.dt.float32
BF16 = mybir.dt.bfloat16
I32 = mybir.dt.int32
U32 = mybir.dt.uint32
ALU = mybir.AluOpType
ACT = mybir.ActivationFunctionType
AX = mybir.AxisListType

P = 128
N = 6250
D = 256
KC = D // P
E = 200000
NEXP = 8
NXT = (2 * N + NEXP * (P - 1)) // P
EPS = 1e-5
GT = 4
GROUP = GT * P
NG = N // GROUP
TAIL = N - NG * GROUP
NT = NG * GT + 1
CT = 29
NCH = -(-E // (CT * P))
ET = NCH * CT
NB = NT
CB = 6
NQ = NCH // CB
U3 = CB // 2
assert NXT % 2 == 1 and NXT <= P
assert 0 < TAIL <= P and NG % 2 == 0 and NQ * CB == NCH and CB % 2 == 0 and NQ % 2 == 1


def groups(eng, step):
    for j in range(2):
        step(j, 0, j, [P] * GT)
    with eng.Fori(1, NG // 2) as pair:
        for j in range(2):
            step(pair * 2 + j, pair, j, [P] * GT)
    step(NG, NG // 2, 0, [TAIL])


class Stage:

    def __init__(self, nc, name):
        self.nc, self.name, self.ctx = nc, name, ExitStack()

    def __enter__(self):
        self.ctx.__enter__()
        return self

    def __exit__(self, *a):
        return self.ctx.__exit__(*a)

    def sb(self, name, shape, dt=F32):
        return self.ctx.enter_context(self.nc.sbuf_tensor(f"{self.name}_{name}", shape, dt))

    def ps(self, name, shape, dt=F32):
        return self.ctx.enter_context(self.nc.psum_tensor(f"{self.name}_{name}", shape, dt))

    def sem(self, name):
        return self.ctx.enter_context(self.nc.semaphore(f"{self.name}_{name}"))


def wait_then_pass(eng, sem, value, passed):
    if isinstance(value, int):
        if value > 0:
            eng.wait_ge(sem, value)
        return
    eng.wait_ge(sem, value)
    eng.sem_inc(passed, 1)


def node_view(dram, g, rows):
    if len(rows) == GT:
        return dram[bass.ds(g * GROUP, GROUP), :].rearrange("(s p) d -> p s d", p=P)
    return dram[g * GROUP:g * GROUP + rows[0], :]


def node_tiles(sb, g, rows):
    if len(rows) == GT:
        return sb[:, bass.ds(g * GT, GT), :]
    return sb[0:rows[0], g * GT, :]


def norm_stage(nc, x, W_k, b_k, xn_dram, xn, xnT, keyT, gmax, ident):
    LAG = 3
    with Stage(nc, "ln") as st:
        xin = st.sb("xin", [P, 2, GT, D])
        stats = st.sb("stats", [P, 2, GT, 6])
        mv = st.sb("mv", [P, 2, GT, 2])
        std = st.sb("std", [P, 2, GT])
        rstd = st.sb("rstd", [P, 2, GT])
        xnb = st.sb("xnb", [P, 2, GT, D])
        eps = st.sb("eps", [P, 1])
        wk = st.sb("wk", [P, KC, D])
        bk = st.sb("bk", [P, KC])
        tp = [st.ps(f"tp{k}", [P, GROUP]) for k in range(2 * KC)]
        kp = [st.ps(f"kp{k}", [P, GROUP]) for k in range(2 * KC)]
        w_in = st.sem("w_in")
        keyed = st.sem("keyed")
        key_out = st.sem("key_out")
        maxed = st.sem("maxed")
        x_in = [st.sem(f"x_in{j}") for j in range(2)]
        xn_out = [st.sem(f"xn_out{j}") for j in range(2)]
        xn_kept = [st.sem(f"xn_kept{j}") for j in range(2)]
        eps_set = st.sem("eps_set")
        stats_done = st.sem("stats_done")
        var_done = st.sem("var_done")
        std_done = st.sem("std_done")
        rstd_done = st.sem("rstd_done")
        xn_done = st.sem("xn_done")
        turned = st.sem("turned")
        evacuated = st.sem("evacuated")
        passed = {e: st.sem(f"passed_{e}") for e in ("sp", "act", "pe", "dve", "pool")}
        with nc.Block() as block:

            @block.sync
            def _(sp):
                def load(g, pair, j, rows):
                    wait_then_pass(sp, xn_done, g + 1, passed["sp"])
                    dst = xin[:, j, :, :] if len(rows) == GT else xin[0:rows[0], j, 0, :]
                    sp.dma_start(dst, node_view(x, g, rows)).then_inc(x_in[j], 16)

                groups(sp, load)

            @block.gpsimd
            def _(pool):
                pool.dma_start(wk[:, :, :], W_k.rearrange("(c p) e -> p c e", p=P)).then_inc(w_in, 16)
                with nc.allow_non_contiguous_dma(reason="one column per feature block"):
                    pool.dma_start(bk[:, :], b_k.rearrange("(c p) -> p c", p=P)).then_inc(w_in, 16)

            @block.vector
            def _(dve):
                nc.vector.memset(eps[:, :], EPS).then_inc(eps_set, 1)
                dve.sem_inc(xn_done, 2)

                def greatest(g, w):
                    wait_then_pass(dve, key_out, g + 3, passed["dve"])
                    for e in range(KC):
                        last = nc.vector.reduce_max(gmax[:, e, bass.ds(g, 1)],
                                                    keyT[:, e, bass.ds(g * GROUP, w)], AX.X)
                    last.then_inc(maxed, 1)

                def normalise(g, pair, j, rows):
                    n, r = len(rows), rows[0]
                    wait_then_pass(dve, x_in[j], pair * 16 + 16, passed["dve"])
                    for s in range(n):
                        last = nc.vector.bn_stats(stats[:r, j, s, :], xin[:r, j, s, :])
                    last.then_inc(stats_done, 1)
                    wait_then_pass(dve, stats_done, g + 1, passed["dve"])
                    for s in range(n):
                        last = nc.vector.bn_aggr(mv[:r, j, s, :], stats[:r, j, s, :])
                    last.then_inc(var_done, 1)
                    wait_then_pass(dve, std_done, g + 1, passed["dve"])
                    nc.vector.reciprocal(rstd[:r, j, 0:n], std[:r, j, 0:n]).then_inc(rstd_done, 1)
                    wait_then_pass(dve, rstd_done, g + 1, passed["dve"])
                    wait_then_pass(dve, xn_out[j], pair * 16, passed["dve"])
                    wait_then_pass(dve, xn_kept[j], pair * 16, passed["dve"])
                    wait_then_pass(dve, evacuated, g + 1, passed["dve"])
                    for s in range(n):
                        last = nc.vector.tensor_scalar(
                            xnb[:r, j, s, :], xin[:r, j, s, :], mv[:r, j, s, 0:1],
                            rstd[:r, j, s:s + 1], ALU.subtract, ALU.mult)
                    last.then_inc(xn_done, 1)
                    if not isinstance(g, int) or g >= LAG:
                        greatest(g - LAG, GROUP)

                whole = [P] * GT
                for g in range(4):
                    normalise(g, g // 2, g % 2, whole)
                with dve.Fori(2, NG // 2) as pair:
                    for j in range(2):
                        normalise(pair * 2 + j, pair, j, whole)
                normalise(NG, NG // 2, 0, [TAIL])
                for g in range(NG + 1 - LAG, NG + 1):
                    greatest(g, GROUP if g < NG else TAIL)
                dve.wait_ge(maxed, NG + 1)

            @block.tensor
            def _(pe):
                pe.sem_inc(evacuated, 2)
                pe.sem_inc(key_out, 2)

                def turn(g, pair, j, rows):
                    n, r = len(rows), rows[0]
                    wait_then_pass(pe, xn_done, g + 3, passed["pe"])
                    wait_then_pass(pe, evacuated, g + 1, passed["pe"])
                    for s in range(n):
                        for k in range(KC):
                            last = transpose(nc, tp[2 * j + k][:, s * P:s * P + r],
                                             xnb[:r, j, s, k * P:(k + 1) * P], ident, r)
                    last.then_inc(turned, 1)

                def keys(g, j, w):
                    wait_then_pass(pe, evacuated, g + 3, passed["pe"])
                    wait_then_pass(pe, key_out, g + 1, passed["pe"])
                    for e in range(KC):
                        for k in range(KC):
                            last = nc.tensor.matmul(kp[2 * j + e][:, 0:w], wk[:, k, e * P:(e + 1) * P],
                                                    xnT[:, k, bass.ds(g * GROUP, w)],
                                                    start=k == 0, stop=k == KC - 1)
                    last.then_inc(keyed, 1)

                whole = [P] * GT
                turn(0, 0, 0, whole)
                turn(1, 0, 1, whole)
                pe.wait_ge(w_in, 32)
                keys(0, 0, GROUP)
                with pe.Fori(1, NG // 2) as pair:
                    turn(pair * 2, pair, 0, whole)
                    keys(pair * 2 - 1, 1, GROUP)
                    turn(pair * 2 + 1, pair, 1, whole)
                    keys(pair * 2, 0, GROUP)
                turn(NG, NG // 2, 0, [TAIL])
                keys(NG - 1, 1, GROUP)
                keys(NG, 0, TAIL)

            @block.scalar
            def _(act):
                act.wait_ge(eps_set, 1)

                act.wait_ge(w_in, 32)

                def root(g, j):
                    wait_then_pass(act, var_done, g + 1, passed["act"])
                    nc.scalar.activation(std[:, j, :], mv[:, j, :, 1], ACT.Sqrt, bias=eps[:, :]).then_inc(std_done, 1)

                def keep_keys(g, j, w):
                    wait_then_pass(act, keyed, g + 1, passed["act"])
                    for e in range(KC):
                        last = nc.scalar.activation(keyT[:, e, bass.ds(g * GROUP, w)], kp[2 * j + e][:, 0:w],
                                                    ACT.Identity, bias=bk[:, e:e + 1])
                    last.then_inc(key_out, 1)

                def finish(g, pair, j, rows):
                    n, r = len(rows), rows[0]
                    wait_then_pass(act, xn_done, g + 3, passed["act"])
                    src = xnb[:, j, :, :] if n == GT else xnb[:r, j, 0, :]
                    act.dma_start(node_view(xn_dram, g, rows), src).then_inc(xn_out[j], 16)
                    act.dma_start(node_tiles(xn, g, rows), src).then_inc(xn_kept[j], 16)
                    if n == GT:
                        root(g + 1, 1 - j)
                    wait_then_pass(act, turned, g + 1, passed["act"])
                    w = sum(rows)
                    for k in range(KC):
                        last = nc.scalar.copy(xnT[:, k, bass.ds(g * GROUP, w)], tp[2 * j + k][:, 0:w])
                    last.then_inc(evacuated, 1)
                    if not isinstance(g, int) or g >= 2:
                        keep_keys(g - 2, j, GROUP)

                root(0, 0)
                groups(act, finish)
                keep_keys(NG - 1, 1, GROUP)
                keep_keys(NG, 0, TAIL)
                for out in (xn_out, xn_kept):
                    act.wait_ge(out[0], 16 * (NG // 2 + 1))
                    act.wait_ge(out[1], 16 * (NG // 2))


def transpose(nc, out, in_, ident, rows):
    return nc.tensor.transpose(out, in_, ident[0:rows, 0:rows])


def mix_stage(nc, x, W_q, b_q, W_v, b_v, gamma, beta, xn, xnT, keyT, gmax, ident):
    with Stage(nc, "mix") as st:
        wq = st.sb("wq", [P, KC, D])
        wv = st.sb("wv", [P, KC, D])
        bq = st.sb("bq", [P, KC])
        bv = st.sb("bv", [1, D])
        gam = st.sb("gam", [P, KC])
        bet = st.sb("bet", [P, KC])
        ones = st.sb("ones", [P, P])
        zeros = st.sb("zeros", [P, P])
        eps = st.sb("eps", [P, 1])
        ek = st.sb("ek", [P, 2, KC, GROUP])
        gsum = st.sb("gsum", [P, KC, NG + 1])
        tmax = st.sb("tmax", [P, KC])
        nmax = st.sb("nmax", [P, KC])
        esum = st.sb("esum", [P, KC])
        rsum = st.sb("rsum", [P, KC])
        pt = st.sb("pt", [P, 2, GT, D])
        M = st.sb("M", [P, KC, D])
        MT = st.sb("MT", [P, KC, D])
        wqT = st.sb("wqT", [P, KC, D])
        lam = st.sb("lam", [P, KC, D])
        bn = st.sb("bn", [P, KC, D])
        stats = st.sb("stats", [P, KC, 6])
        mv = st.sb("mv", [P, KC, 2])
        std = st.sb("std", [P, KC])
        rstd = st.sb("rstd", [P, KC])
        scl = st.sb("scl", [P, KC])
        msc = st.sb("msc", [P, KC])
        shf = st.sb("shf", [P, KC])
        bqb = st.sb("bqb", [P, KC, P])
        wqbn = st.sb("wqbn", [P, KC, D])
        qbias = st.sb("qbias", [P, D])
        xin = st.sb("xin", [P, 2, GT, D])
        xs = ek
        kp = [st.ps(f"kp{k}", [P, GROUP]) for k in range(4)]
        mp = [st.ps(f"mp{k}", [P, GROUP]) for k in range(2)]
        lp = [st.ps(f"lp{k}", [P, GROUP]) for k in range(2)]
        w_in = st.sem("w_in")
        const = st.sem("const")
        maxed = st.sem("maxed")
        neg = st.sem("neg")
        exped = st.sem("exped")
        p_turned = st.sem("p_turned")
        p_out = st.sem("p_out")
        p_used = st.sem("p_used")
        c = st.sem("c")
        pe_c = st.sem("pe_c")
        act_c = st.sem("act_c")
        x_in = [st.sem(f"x_in{j}") for j in range(2)]
        xs_done = st.sem("xs_done")
        mixed = st.sem("mixed")
        xq_done = st.sem("xq_done")
        h_done = st.sem("h_done")
        passed = {e: st.sem(f"passed_{e}") for e in ("sp", "act", "pe", "dve")}
        W_LOADS = 6

        with nc.Block() as block:

            @block.sync
            def _(sp):
                for dst, src in ((wq, W_q), (wv, W_v)):
                    sp.dma_start(dst[:, :, :], src.rearrange("(c p) e -> p c e", p=P)).then_inc(w_in, 16)
                with nc.allow_non_contiguous_dma(reason="one column per feature block"):
                    for dst, src in ((bq, b_q), (gam, gamma), (bet, beta)):
                        sp.dma_start(dst[:, :], src.rearrange("(c p) -> p c", p=P)).then_inc(w_in, 16)
                sp.dma_start(bv[:, :], b_v.rearrange("(a e) -> a e", a=1)).then_inc(w_in, 16)

                def load(g, pair, j, rows):
                    wait_then_pass(sp, h_done, g + 1, passed["sp"])
                    dst = xin[:, j, :, :] if len(rows) == GT else xin[0:rows[0], j, 0, :]
                    sp.dma_start(dst, node_view(x, g, rows)).then_inc(x_in[j], 16)

                groups(sp, load)

            @block.tensor
            def _(pe):
                pe.wait_ge(w_in, 16 * W_LOADS)
                pe.wait_ge(const, 3)
                for e in range(KC):
                    nc.tensor.matmul(mp[e][:, 0:D], zeros[:, :], wq[:, 0, :], start=True, stop=False)
                pe.sem_inc(p_out, 2)

                def turn(g, j, rows):
                    wait_then_pass(pe, exped, g + 1, passed["pe"])
                    wait_then_pass(pe, p_out, g + 1, passed["pe"])
                    for s, r in enumerate(rows):
                        for e in range(KC):
                            last = transpose(nc, kp[2 * j + s // 2][0:r, (s % 2) * D + e * P:(s % 2) * D + (e + 1) * P],
                                             ek[:, j, e, s * P:s * P + r], ident, P)
                    last.then_inc(p_turned, 1)

                def accumulate(g, j, rows, stop):
                    wait_then_pass(pe, p_out, g + 3, passed["pe"])
                    for s, r in enumerate(rows):
                        xt = xn[:r, g * GT, :] if stop else \
                            xn[:, bass.ds(g * GT + s, 1), :].rearrange("p a d -> p (a d)")
                        for e in range(KC):
                            last = nc.tensor.matmul(mp[e][:, 0:D], pt[:r, j, s, e * P:(e + 1) * P], xt,
                                                    start=False, stop=stop)
                    last.then_inc(p_used, 1)

                whole = [P] * GT
                turn(0, 0, whole)
                with pe.Fori(0, NG // 2 - 1) as i:
                    turn(i * 2 + 1, 1, whole)
                    accumulate(i * 2, 0, whole, False)
                    turn(i * 2 + 2, 0, whole)
                    accumulate(i * 2 + 1, 1, whole, False)
                turn(NG - 1, 1, whole)
                accumulate(NG - 2, 0, whole, False)
                turn(NG, 0, [TAIL])
                accumulate(NG - 1, 1, whole, False)
                accumulate(NG, 0, [TAIL], True)
                pe.wait_ge(c, 4)
                for a in range(KC):
                    for b in range(KC):
                        nc.tensor.transpose(kp[a][:, b * P:(b + 1) * P], M[:, b, a * P:(a + 1) * P], ident[:, :])
                for a in range(KC):
                    for b in range(KC):
                        last = nc.tensor.transpose(kp[2 + a][:, b * P:(b + 1) * P], wq[:, b, a * P:(a + 1) * P],
                                                   ident[:, :])
                last.then_inc(pe_c, 1)
                pe.wait_ge(c, 5)
                for a in range(KC):
                    for k in range(KC):
                        nc.tensor.matmul(lp[a][:, 0:D], MT[:, k, a * P:(a + 1) * P], wv[:, k, :],
                                         start=k == 0, stop=False)
                    last = nc.tensor.matmul(lp[a][:, 0:D], ones[0:1, :], bv[:, :], start=False, stop=True)
                last.then_inc(pe_c, 1)
                pe.wait_ge(c, 13)
                for a in range(KC):
                    for k in range(KC):
                        nc.tensor.matmul(kp[a][:, 0:D], wqT[:, k, a * P:(a + 1) * P], bn[:, k, :],
                                         start=k == 0, stop=k == KC - 1)
                for k in range(KC):
                    last = nc.tensor.matmul(kp[2][:, 0:D], bqb[:, k, :], bn[:, k, :],
                                            start=k == 0, stop=k == KC - 1)
                last.then_inc(pe_c, 1)
                pe.wait_ge(c, 14)
                pe.sem_inc(xq_done, 2)

                def mix(g, pair, j, rows):
                    wait_then_pass(pe, xs_done, g + 3, passed["pe"])
                    wait_then_pass(pe, xq_done, g + 1, passed["pe"])
                    for s, r in enumerate(rows):
                        for k in range(KC):
                            last = nc.tensor.matmul(kp[2 * j + s // 2][:r, (s % 2) * D:(s % 2 + 1) * D],
                                                    xs[:, j, k, s * P:s * P + r], wqbn[:, k, :],
                                                    start=k == 0, stop=k == KC - 1)
                    last.then_inc(mixed, 1)

                groups(pe, mix)

            @block.scalar
            def _(act):
                act.wait_ge(neg, 1)

                def exps(g, pair, j, rows):
                    w = sum(rows)
                    wait_then_pass(act, p_turned, g + 1, passed["act"])
                    for e in range(KC):
                        last = nc.scalar.activation(ek[:, j, e, 0:w], keyT[:, e, bass.ds(g * GROUP, w)], ACT.Exp,
                                                    bias=nmax[:, e:e + 1], accum_out=gsum[:, e, bass.ds(g, 1)])
                    last.then_inc(exped, 1)

                act.sem_inc(p_turned, 2)
                groups(act, exps)
                act.wait_ge(c, 7)
                nc.scalar.activation(std[:, :], mv[:, :, 1], ACT.Sqrt, bias=eps[:, :]).then_inc(act_c, 1)
                act.sem_inc(xs_done, 2)

                def fix(g, pair, j, rows):
                    w = sum(rows)
                    wait_then_pass(act, mixed, g + 1, passed["act"])
                    for k in range(KC):
                        last = nc.scalar.copy(xs[:, j, k, 0:w], xnT[:, k, bass.ds(g * GROUP, w)])
                    last.then_inc(xs_done, 1)

                act.sem_inc(mixed, 2)
                groups(act, fix)

            @block.vector
            def _(dve):
                nc.vector.memset(ones[:, :], 1.0).then_inc(const, 1)
                nc.vector.memset(zeros[:, :], 0.0).then_inc(const, 1)
                nc.vector.memset(eps[:, :], EPS).then_inc(const, 1)
                nc.vector.tensor_reduce(tmax[:, :], gmax[:, :, :], AX.X, ALU.max).then_inc(maxed, 1)
                dve.wait_ge(maxed, 1)
                nc.vector.tensor_scalar_mul(nmax[:, :], tmax[:, :], -1.0).then_inc(neg, 1)
                dve.sem_inc(p_used, 2)

                def evac(g, pair, j, rows):
                    wait_then_pass(dve, p_turned, g + 3, passed["dve"])
                    wait_then_pass(dve, p_used, g + 1, passed["dve"])
                    if len(rows) == GT:
                        for b in range(2):
                            last = nc.vector.tensor_copy(pt[:, j, 2 * b:2 * b + 2, :],
                                                         kp[2 * j + b][:, :].rearrange("p (s d) -> p s d", s=2))
                    else:
                        last = nc.vector.tensor_copy(pt[:rows[0], j, 0, :], kp[2 * j][:rows[0], 0:D])
                    last.then_inc(p_out, 1)

                groups(dve, evac)
                dve.wait_ge(exped, NG + 1)

                n = [0]

                def link(ins):
                    n[0] += 1
                    ins.then_inc(c, 1)
                    dve.wait_ge(c, n[0])

                for e in range(KC):
                    last = nc.vector.reduce_sum(esum[:, e:e + 1], gsum[:, e, :], AX.X)
                link(last)
                link(nc.vector.reciprocal(rsum[:, :], esum[:, :]))
                dve.wait_ge(p_used, NG + 3)
                for e in range(KC):
                    link(nc.vector.tensor_scalar(M[:, e, :], mp[e][:, 0:D], rsum[:, e:e + 1], None, ALU.mult))
                dve.wait_ge(pe_c, 1)
                for a in range(KC):
                    nc.vector.tensor_copy(MT[:, a, :], kp[a][:, 0:D])
                for a in range(KC):
                    last = nc.vector.tensor_copy(wqT[:, a, :], kp[2 + a][:, 0:D])
                link(last)
                dve.wait_ge(pe_c, 2)
                for a in range(KC):
                    nc.vector.tensor_copy(lam[:, a, :], lp[a][:, 0:D])
                    last = nc.vector.bn_stats(stats[:, a, :], lp[a][:, 0:D])
                link(last)
                for a in range(KC):
                    last = nc.vector.bn_aggr(mv[:, a, :], stats[:, a, :])
                link(last)
                dve.wait_ge(act_c, 1)
                link(nc.vector.reciprocal(rstd[:, :], std[:, :]))
                link(nc.vector.tensor_tensor(scl[:, :], rstd[:, :], gam[:, :], ALU.mult))
                link(nc.vector.tensor_tensor(msc[:, :], mv[:, :, 0], scl[:, :], ALU.mult))
                link(nc.vector.tensor_tensor(shf[:, :], bet[:, :], msc[:, :], ALU.subtract))
                for k in range(KC):
                    last = nc.vector.tensor_scalar(bn[:, k, :], lam[:, k, :], scl[:, k:k + 1], shf[:, k:k + 1],
                                                   ALU.mult, ALU.add)
                link(last)
                for k in range(KC):
                    last = nc.vector.tensor_scalar(bqb[:, k, :], ones[:, :], bq[:, k:k + 1], None, ALU.mult)
                link(last)
                assert n[0] == 13, n
                dve.wait_ge(pe_c, 3)
                for k in range(KC):
                    nc.vector.tensor_copy(wqbn[:, k, :], kp[k][:, 0:D])
                link(nc.vector.tensor_copy(qbias[:, :], kp[2][:, 0:D]))
                dve.sem_inc(h_done, 2)

                def add(g, pair, j, rows):
                    n, r = len(rows), rows[0]
                    wait_then_pass(dve, x_in[j], pair * 16 + 16, passed["dve"])
                    wait_then_pass(dve, mixed, g + 3, passed["dve"])
                    for s in range(n):
                        last = nc.vector.tensor_tensor(xin[:r, j, s, :], kp[2 * j + s // 2][:r, (s % 2) * D:(s % 2 + 1) * D],
                                                       xin[:r, j, s, :], ALU.add)
                    last.then_inc(xq_done, 1)
                    wait_then_pass(dve, xq_done, g + 3, passed["dve"])
                    if n == GT:
                        out, a, b = xn[:, bass.ds(g * GT, GT), :], xin[:, j, :, :], \
                            qbias[:, :].rearrange("p (a d) -> p a d", a=1).to_broadcast([P, GT, D])
                    else:
                        out, a, b = xn[:r, g * GT, :], xin[:r, j, 0, :], qbias[:r, :]
                    nc.vector.tensor_tensor(out, a, b, ALU.add).then_inc(h_done, 1)

                groups(dve, add)


def edge_stage(nc, src_t, dst_t, ew_t, xn_dram, sum_dram, low_i, flag, h, ident, above, iota49, iota128):
    with Stage(nc, "edge") as st:
        at_first = st.sb("at_first", [P, max(2 * ET, 4 * U3 * D)], I32)
        src_i, tmp_i = at_first[:, 0:ET], at_first[:, ET:2 * ET]
        dst_i = st.sb("dst_i", [P, ET], I32)
        ew = st.sb("ew", [P, ET])
        blk = st.sb("blk", [P, ET], BF16)
        dst_f = tmp_i.bitcast(F32)
        code = dst_i[:, :].bitcast(F32)
        cmin = st.sb("cmin", [P, NCH])
        cmax = st.sb("cmax", [P, NCH])
        low = st.sb("low", [NCH, 1])
        high = st.sb("high", [NCH, 1])
        span = st.sb("span", [NCH, 1])
        diag = st.sb("diag", [NCH, NCH])
        ones = st.sb("ones", [NCH, P])
        lowb = st.sb("lowb", [P, NCH])
        onehot = st.sb("onehot", [P, CT, CB, NB], BF16)
        before = st.sb("before", [P, CT + 1, CB, NB], BF16)
        slot = st.sb("slot", [P, CT, CB])
        most = st.sb("most", [P, NQ])
        most1 = st.sb("most1", [P, 1])
        R = st.sb("R", [P, 2, CT, 2, NB])
        SL = st.sb("SL", [P, 2, CT, P])
        raw = st.sb("raw", [P, NB, 2, CB])
        code_i = st.sb("code_i", [P, NB, CB], I32)
        part_i = st.sb("part_i", [P, NB, CB], I32)
        rec = st.sb("rec", [P, NB, U3 + 2 * CB])
        SRC, DST, WT = slice(0, U3), slice(U3, U3 + CB), slice(U3 + CB, U3 + 2 * CB)
        rows_f = st.sb("rows_f", [P, NB, U3])
        next_rows = st.sb("next_rows", [P, NB, U3], I32)
        row_i = st.sb("row_i", [P, NB * U3], I32)
        row = st.sb("row", [1, P + NCH])
        bad = st.sb("bad", [1, 2])
        bad1 = st.sb("bad1", [1, 1])
        win = st.sb("win", [P, 2 * U3, D])
        hots = st.sb("hots", [P, 2, U3 + CB, P])
        src1h, dst1h = hots[:, :, SRC, :], hots[:, :, DST, :]
        weighted = st.sb("weighted", [P, 3, CB, P])
        A = st.sb("A", [P, 2, U3, P])
        G = at_first[:, :].bitcast(F32)[:, 0:4 * U3 * D].rearrange("p (j c d) -> p j c d", j=4, c=U3)
        mm = st.ps("mm", [P, GROUP])
        base = st.ps("base", [P, CB * NB])
        bp = [st.ps(f"bp{j}", [P, 2 * NB]) for j in range(2)]
        ap = [st.ps(f"ap{j}", [P, U3 * P]) for j in range(2)]
        op = [st.ps(f"op{j}", [P, D]) for j in range(2)]
        e_in = st.sem("e_in")
        c = st.sem("c")
        pe_c = st.sem("pe_c")
        hot = st.sem("hot")
        based = st.sem("based")
        based_free = st.sem("based_free")
        chain = st.sem("chain")
        rs_done = st.sem("rs_done")
        binned = st.sem("binned")
        kept = st.sem("kept")
        decoded = st.sem("decoded")
        rows_ready = st.sem("rows_ready")
        rows_taken = st.sem("rows_taken")
        low_ready = st.sem("low_ready")
        win_in = st.sem("win_in")
        win_ready = st.sem("win_ready")
        h_saved = st.sem("h_saved")
        flag_in = st.sem("flag_in")
        hot_done = st.sem("hot_done")
        weighted_done = st.sem("weighted_done")
        gathered = [st.sem(f"gathered{j}") for j in range(4)]
        a_done = st.sem("a_done")
        a_kept = st.sem("a_kept")
        stepped = st.sem("stepped")
        summed = st.sem("summed")
        passed = {e: st.sem(f"passed_{e}") for e in ("sp", "pool", "act", "pe", "dve")}
        LINKS_A_STEP = 5
        HOT_AT = 0
        BASE_AT = HOT_AT + CB
        CHAIN_AT = BASE_AT + 3
        SLOT_AT = CHAIN_AT + (CT + 1) // LINKS_A_STEP
        CHUNK_AT = SLOT_AT + 2
        CHUNK_STEPS = 4
        BIN_AT = CHUNK_AT + CHUNK_STEPS
        KEEP_AT = BIN_AT + CHUNK_STEPS
        ROWS_AT = KEEP_AT + CHUNK_STEPS * (U3 - 1) + 2
        assert (CT + 1) % LINKS_A_STEP == 0 and KEEP_AT + CHUNK_STEPS * (CB - 1) < NB
        SHARE = -(-CT // CHUNK_STEPS)
        USES = [(NB - 1) // 3] * 3 + [1]
        BEFORE = 3
        assert (NB - 1) % 3 == 0
        LINKS = CT + 15

        def buffer(b):
            return 2 if b == NB - 1 else b % 2

        def row_buffer(b):
            return 3 if b == NB - 1 else b % 3

        with nc.Block() as block:

            @block.sync
            def _(sp):
                for d, x in ((src_i, src_t), (dst_i, dst_t), (ew, ew_t)):
                    sp.dma_start(d[:, :], x).then_inc(e_in, 16)
                sp.dma_start(sum_dram[0:NG * GROUP, :].rearrange("(s p) d -> p s d", p=P),
                             h[:, 0:NG * GT, :]).then_inc(h_saved, 16)
                sp.dma_start(sum_dram[NG * GROUP:N, :], h[0:TAIL, NG * GT, :]).then_inc(h_saved, 16)
                sp.wait_ge(low_ready, 1)

                def load_windows(q, j):
                    for i in range(U3):
                        first = sp.value_load(low_i[0:1, bass.ds(q * CB + U3 + i, 1)], min_val=0, max_val=N - P)
                        sp.dma_start(win[:, j * U3 + i, :], xn_dram[bass.ds(first, P), :]).then_inc(win_in, 16)
                    wait_then_pass(sp, win_in, (q + 1) * 16 * U3, passed["sp"])
                    sp.sem_inc(win_ready, 1)

                load_windows(0, 0)
                load_windows(1, 1)
                with sp.Fori(1, NQ // 2) as pair:
                    for j in range(2):
                        wait_then_pass(sp, stepped, (pair * 2 + j - 1) * NB + BEFORE, passed["sp"])
                        load_windows(pair * 2 + j, j)
                sp.wait_ge(stepped, (NQ - 2) * NB + BEFORE)
                load_windows(NQ - 1, 0)
                sp.wait_ge(h_saved, 32)

            @block.gpsimd
            def _(pool):
                pool.sem_inc(stepped, BEFORE)
                with pool.Fori(0, NQ) as q:
                    wait_then_pass(pool, rows_ready, q + 1, passed["pool"])
                    nc.gpsimd.tensor_copy(row_i[:, :], next_rows[:, :, :].rearrange("p b c -> p (b c)"))\
                        .then_inc(rows_taken, 1)
                    wait_then_pass(pool, rows_taken, q + 1, passed["pool"])
                    for b in range(NB):
                        wait_then_pass(pool, stepped, q * NB + b - 2 + BEFORE, passed["pool"])
                        for i in range(U3):
                            pool.indirect_dma_start(
                                out=G[:, row_buffer(b), i, :], out_offset=None, in_=xn_dram,
                                in_offset=bass.IndirectOffsetOnAxis(ap=row_i[:, b * U3 + i:b * U3 + i + 1],
                                                                    axis=0)).then_inc(gathered[row_buffer(b)], 16)
                    for j in range(4):
                        wait_then_pass(pool, gathered[j], (q + 1) * USES[j] * 16 * U3, passed["pool"])

            @block.tensor
            def _(pe):
                pe.wait_ge(c, 5)
                nc.tensor.transpose(mm[0:NCH, 0:P], cmin[:, :], ident[:, :])
                nc.tensor.transpose(mm[0:NCH, P:2 * P], cmax[:, :], ident[:, :]).then_inc(pe_c, 1)
                pe.wait_ge(c, 9)
                nc.tensor.matmul(mm[:, 0:NCH], ones[:, :], diag[:, :], start=True, stop=True).then_inc(pe_c, 1)
                pe.sem_inc(kept, 2)
                pe.sem_inc(a_done, 2)
                
                def bin_share(q, n):
                    if n in (BASE_AT, BASE_AT + 1):
                        a, b = ((0, CT // 2), (CT // 2, CT))[n - BASE_AT]
                        if n == BASE_AT:
                            wait_then_pass(pe, hot, (q + 1) * CB, passed["pe"])
                            wait_then_pass(pe, based_free, q + 1, passed["pe"])
                        for j in range(a, b):
                            last = nc.tensor.matmul(base[:, :], above[:, :],
                                                    onehot[:, j, :, :].rearrange("p c b -> p (c b)"),
                                                    start=j == 0, stop=j == CT - 1)
                        if b == CT:
                            last.then_inc(based, 1)
                    k, part = divmod(n - BIN_AT, CHUNK_STEPS)
                    if 0 <= k < CB:
                        if part == 0:
                            wait_then_pass(pe, rs_done, q * CB + k + 1, passed["pe"])
                            wait_then_pass(pe, kept, q * CB + k + 1, passed["pe"])
                        for j in range(part * SHARE, min((part + 1) * SHARE, CT)):
                            last = nc.tensor.matmul(bp[k % 2][:, :], SL[:, k % 2, j, :],
                                                    R[:, k % 2, j, :, :].rearrange("p w b -> p (w b)"),
                                                    start=j == 0, stop=j == CT - 1)
                        if part == CHUNK_STEPS - 1:
                            last.then_inc(binned, 1)

                def products(q, turn, b):
                    j, buf, t = b % 2, buffer(b), q * NB + b
                    rb = row_buffer(b)
                    wait_then_pass(pe, weighted_done, t + 1, passed["pe"])
                    for i in range(U3):
                        last = nc.tensor.matmul(ap[j][:, i * P:(i + 1) * P], src1h[:, j, i, :],
                                                weighted[:, buf, U3 + i, :], start=True, stop=True)
                    last.then_inc(a_done, 1)
                    wait_then_pass(pe, summed, t + (2 if b == 0 else 1), passed["pe"])
                    wait_then_pass(pe, gathered[rb], (q * USES[rb] + (1 if rb == 3 else b // 3 + 1)) * 16 * U3,
                                   passed["pe"])
                    for i in range(U3):
                        nc.tensor.matmul(op[j][:, :], weighted[:, buf, i, :], G[:, rb, i, :], start=i == 0, stop=False)
                    wait_then_pass(pe, a_kept, t + 1, passed["pe"])
                    for i in range(U3):
                        w = win[:, bass.ds(turn * U3 + i, 1), :].rearrange("p a d -> p (a d)")
                        last = nc.tensor.matmul(op[j][:, :], A[:, j, i, :], w, start=False, stop=i == U3 - 1)
                    last.then_inc(stepped, 1)

                for n in range(NB):
                    bin_share(0, n)
                with pe.Fori(0, NQ // 2) as pair:
                    with pe.Fori(0, 2) as turn:
                        q = pair * 2 + turn
                        wait_then_pass(pe, win_ready, q + 1, passed["pe"])
                        for b in range(NB):
                            products(q, turn, b)
                            bin_share(q + 1, b)
                pe.wait_ge(flag_in, 1)
                nc.tensor.transpose(mm[0:1, 0:P], most1[:, :], ident[:, :])
                nc.tensor.transpose(mm[0:1, P:P + NCH], span[:, :], ident[0:NCH, 0:NCH]).then_inc(pe_c, 1)
                pe.wait_ge(win_ready, NQ)
                for b in range(NB):
                    products(NQ - 1, 0, b)

            @block.scalar
            def _(act):
                def bin_share(q, n):
                    k, late = divmod(n - KEEP_AT, CHUNK_STEPS)
                    if 0 <= k < CB and late == 0:
                        if k == 0:
                            wait_then_pass(act, decoded, q, passed["act"])
                        wait_then_pass(act, binned, q * CB + k + 3, passed["act"])
                        nc.scalar.copy(raw[:, :, :, k],
                                       bp[k % 2][:, :].rearrange("p (w b) -> p b w", w=2)).then_inc(kept, 1)

                def keep(q, b):
                    j = b % 2
                    wait_then_pass(act, a_done, q * NB + b + 3, passed["act"])
                    nc.scalar.copy(A[:, j, :, :].rearrange("p c s -> p (c s)"), ap[j][:, :]).then_inc(a_kept, 1)

                def weigh(q, b):
                    buf = buffer(b)
                    wait_then_pass(act, hot_done, q * NB + b + 1, passed["act"])
                    wait_then_pass(act, stepped, q * NB + b - 1 + BEFORE, passed["act"])
                    for k in range(CB):
                        w = WT.start + k
                        last = nc.scalar.activation(weighted[:, buf, k, :], dst1h[:, b % 2, k, :], ACT.Copy,
                                                    scale=rec[:, b, w:w + 1])
                    last.then_inc(weighted_done, 1)

                for n in range(NB):
                    bin_share(0, n)
                weigh(0, 0)
                with act.Fori(0, NQ - 1) as q:
                    for b in range(NB):
                        keep(q, b)
                        weigh(*((q, b + 1) if b + 1 < NB else (q + 1, 0)))
                        bin_share(q + 1, b)
                for b in range(NB):
                    keep(NQ - 1, b)
                    if b + 1 < NB:
                        weigh(NQ - 1, b + 1)

            @block.vector
            def _(dve):
                count = [0]

                def link(ins):
                    count[0] += 1
                    ins.then_inc(c, 1)
                    dve.wait_ge(c, count[0])

                nc.vector.memset(ones[:, :], 1.0)
                dve.wait_ge(e_in, 48)
                link(nc.vector.tensor_single_scalar(tmp_i[:, :], src_i[:, :], 7, op=ALU.arith_shift_right))
                link(nc.vector.tensor_copy(blk[:, :], tmp_i[:, :]))
                nc.vector.tensor_single_scalar(src_i[:, :], src_i[:, :], P - 1, op=ALU.bitwise_and)
                link(nc.vector.tensor_copy(dst_f, dst_i[:, :]))
                by_chunk = dst_f.rearrange("p (c j) -> p c j", j=CT)
                link(nc.vector.tensor_reduce(cmin[:, :], by_chunk, AX.X, ALU.min))
                link(nc.vector.tensor_reduce(cmax[:, :], by_chunk, AX.X, ALU.max))
                dve.wait_ge(pe_c, 1)
                nc.vector.tensor_reduce(low[:, :], mm[0:NCH, 0:P], AX.X, ALU.min)
                link(nc.vector.tensor_reduce(high[:, :], mm[0:NCH, P:2 * P], AX.X, ALU.max))
                link(nc.vector.tensor_scalar_min(low[:, :], low[:, :], float(N - P)))
                link(nc.vector.tensor_tensor(span[:, :], high[:, :], low[:, :], ALU.subtract))
                link(nc.vector.tensor_scalar(diag[:, :], ident[0:NCH, 0:NCH], low[:, 0:1], None, ALU.mult))
                dve.wait_ge(pe_c, 2)
                nc.vector.tensor_copy(low_i[:, :], mm[0:1, 0:NCH]).then_inc(low_ready, 1)
                link(nc.vector.tensor_copy(lowb[:, :], mm[:, 0:NCH]))
                link(nc.vector.tensor_tensor(by_chunk, by_chunk,
                                             lowb[:, :].rearrange("p (c a) -> p c a", a=1).to_broadcast([P, NCH, CT]),
                                             ALU.subtract))
                link(nc.vector.tensor_copy(code, src_i[:, :]))
                link(nc.vector.scalar_tensor_tensor(code, code, float(P), dst_f, ALU.mult, ALU.add))
                dve.sem_inc(based_free, 1)
                dve.sem_inc(binned, 2)
                dve.sem_inc(summed, 2)
                links = [0]

                def next_link(q, ins):
                    links[0] += 1
                    ins.then_inc(chain, 1)
                    wait_then_pass(dve, chain, q * LINKS + links[0], passed["dve"])

                def of_chunk(a, q, k):
                    return a[:, bass.ds(q * CB * CT + k * CT, CT)].rearrange("p (j a) -> p j a", a=1)\
                        .to_broadcast([P, CT, NB])

                def bin_share(q, n):
                    if n == HOT_AT:
                        links[0] = 0
                    if HOT_AT <= n < BASE_AT:
                        k = n - HOT_AT
                        nc.vector.tensor_tensor(
                            onehot[:, :, k, :],
                            iota49[:, :].rearrange("p (a b) -> p a b", a=1).to_broadcast([P, CT, NB]),
                            of_chunk(blk, q, k), ALU.is_equal).then_inc(hot, 1)
                    if n == CHAIN_AT:
                        wait_then_pass(dve, based, q + 1, passed["dve"])
                        next_link(q, nc.vector.tensor_copy(before[:, 0, :, :].rearrange("p c b -> p (c b)"),
                                                           base[:, :]))
                        dve.sem_inc(based_free, 1)
                    if CHAIN_AT <= n < SLOT_AT:
                        for j in range((n - CHAIN_AT) * LINKS_A_STEP - 1, (n - CHAIN_AT + 1) * LINKS_A_STEP - 1):
                            if j >= 0:
                                next_link(q, nc.vector.tensor_tensor(before[:, j + 1, :, :], before[:, j, :, :],
                                                                     onehot[:, j, :, :], ALU.add))
                    if n == SLOT_AT:
                        nc.vector.tensor_reduce(most[:, bass.ds(q, 1)],
                                                before[:, CT, :, :].rearrange("p c b -> p (c b)"), AX.X, ALU.max)
                    if n in (SLOT_AT, SLOT_AT + 1):
                        a, b = ((0, CT // 2), (CT // 2, CT))[n - SLOT_AT]
                        next_link(q, nc.vector.tensor_tensor(before[:, a:b, :, :].rearrange("p j c b -> p (j c b)"),
                                                             before[:, a:b, :, :].rearrange("p j c b -> p (j c b)"),
                                                             onehot[:, a:b, :, :].rearrange("p j c b -> p (j c b)"),
                                                             ALU.mult))
                    k, part = divmod(n - CHUNK_AT, CHUNK_STEPS)
                    if 0 <= k < CB:
                        if part == 0:
                            ins = nc.vector.tensor_reduce(slot[:, :, k:k + 1], before[:, 0:CT, k, :], AX.X, ALU.add)
                            wait_then_pass(dve, binned, q * CB + k + 1, passed["dve"])
                            next_link(q, ins)
                        elif part == 1:
                            for w, values in enumerate((code, ew)):
                                nc.vector.tensor_tensor(R[:, k % 2, :, w, :], onehot[:, :, k, :],
                                                        of_chunk(values, q, k), ALU.mult)
                        else:
                            a, b = ((0, CT // 2), (CT // 2, CT))[part - 2]
                            ins = nc.vector.tensor_tensor(
                                SL[:, k % 2, a:b, :],
                                iota128[:, :].rearrange("p (a s) -> p a s", a=1).to_broadcast([P, b - a, P]),
                                slot[:, a:b, k:k + 1].to_broadcast([P, b - a, P]), ALU.is_equal)
                            if b == CT:
                                ins.then_inc(rs_done, 1)
                    if n == ROWS_AT:
                        wait_then_pass(dve, kept, q * CB + U3 + 2, passed["dve"])
                        wait_then_pass(dve, rows_taken, q, passed["dve"])
                        next_link(q, nc.vector.tensor_copy(code_i[:, :, 0:U3], raw[:, :, 0, 0:U3]))
                        next_link(q, nc.vector.tensor_single_scalar(part_i[:, :, 0:U3], code_i[:, :, 0:U3], P - 1,
                                                                    op=ALU.bitwise_and))
                        next_link(q, nc.vector.tensor_copy(rows_f[:, :, :], part_i[:, :, 0:U3]))
                        lows = lowb[:, bass.ds(q * CB, U3)].rearrange("p (a c) -> p a c", a=1)
                        nc.vector.tensor_tensor(next_rows[:, :, :], rows_f[:, :, :],
                                                lows.to_broadcast([P, NB, U3]), ALU.add).then_inc(rows_ready, 1)

                def decode(q):
                    wait_then_pass(dve, kept, (q + 1) * CB + 2, passed["dve"])
                    wait_then_pass(dve, weighted_done, q * NB, passed["dve"])
                    next_link(q, nc.vector.tensor_copy(code_i[:, :, :], raw[:, :, 0, :]))
                    next_link(q, nc.vector.tensor_single_scalar(part_i[:, :, U3:CB], code_i[:, :, U3:CB], P - 1,
                                                                op=ALU.bitwise_and))
                    nc.vector.tensor_copy(rec[:, :, SRC], part_i[:, :, U3:CB])
                    nc.vector.tensor_single_scalar(code_i[:, :, :], code_i[:, :, :], 7, op=ALU.arith_shift_right)
                    next_link(q, nc.vector.tensor_copy(rec[:, :, WT], raw[:, :, 1, :]))
                    nc.vector.tensor_copy(rec[:, :, DST], code_i[:, :, :]).then_inc(decoded, 1)
                    wait_then_pass(dve, decoded, q + 1, passed["dve"])
                    assert links[0] == LINKS, links

                def one_hots(q, b):
                    wait_then_pass(dve, a_done, q * NB + b + (2 if b == 0 else 1), passed["dve"])
                    nc.vector.tensor_tensor(
                        hots[:, b % 2, :, :],
                        iota128[:, :].rearrange("p (a s) -> p a s", a=1).to_broadcast([P, U3 + CB, P]),
                        rec[:, b, 0:U3 + CB].rearrange("p (c a) -> p c a", a=1).to_broadcast([P, U3 + CB, P]),
                        ALU.is_equal).then_inc(hot_done, 1)

                def finish(q, b):
                    wait_then_pass(dve, stepped, q * NB + b + 1 + BEFORE, passed["dve"])
                    r = TAIL if b == NB - 1 else P
                    nc.vector.tensor_tensor(h[:r, b, :], h[:r, b, :], op[b % 2][:r, :], ALU.add).then_inc(summed, 1)

                def sum_step(q, b):
                    if b >= 1:
                        one_hots(q, b)
                    if b >= 2:
                        finish(q, b - 2)

                for n in range(NB):
                    bin_share(0, n)
                decode(0)
                one_hots(0, 0)
                dve.wait_ge(h_saved, 32)
                with dve.Fori(0, NQ - 1) as q:
                    for b in range(NB):
                        sum_step(q, b)
                        bin_share(q + 1, b)
                    decode(q + 1)
                    one_hots(q + 1, 0)
                    finish(q, NB - 2)
                    finish(q, NB - 1)
                nc.vector.tensor_reduce(most1[:, :], most[:, :], AX.X, ALU.max).then_inc(flag_in, 1)
                for b in range(NB):
                    sum_step(NQ - 1, b)
                finish(NQ - 1, NB - 2)
                finish(NQ - 1, NB - 1)
                dve.wait_ge(pe_c, 3)
                nc.vector.tensor_reduce(bad[:, 0:1], mm[0:1, 0:P], AX.X, ALU.max)
                link(nc.vector.tensor_reduce(bad[:, 1:2], mm[0:1, P:P + NCH], AX.X, ALU.max))
                nc.vector.tensor_single_scalar(row[:, 0:1], bad[:, 0:1], float(P), op=ALU.is_gt)
                link(nc.vector.tensor_single_scalar(row[:, 1:2], bad[:, 1:2], float(P), op=ALU.is_ge))
                link(nc.vector.tensor_reduce(bad1[:, :], row[:, 0:2], AX.X, ALU.max))
                link(nc.vector.tensor_copy(flag[:, :], bad1[:, :]))


def any_edges_stage(nc, src_t, dst_t, ew_t, xn_dram, sum_dram, flag, h, ident, below):
    with Stage(nc, "any") as st:
        src_i = st.sb("src_i", [P, ET], I32)
        dst_i = st.sb("dst_i", [P, ET], I32)
        ew = st.sb("ew", [P, ET])
        src_f = st.sb("src_f", [P, ET])
        ones = st.sb("ones", [P, P])
        to_i = st.sb("to_i", [P, 1], I32)
        from_i = st.sb("from_i", [P, 1], I32)
        first_i = st.sb("first_i", [P, 1], I32)
        to_f = st.sb("to_f", [P, 1])
        wt = st.sb("wt", [P, 1])
        diag = st.sb("diag", [P, P])
        same = st.sb("same", [P, P])
        early = st.sb("early", [P, P])
        ecount = st.sb("ecount", [P, 1])
        first_f = st.sb("first_f", [P, 1])
        rows = st.sb("rows", [P, D])
        msg = st.sb("msg", [P, D])
        old = st.sb("old", [P, D])
        new = st.sb("new", [P, D])
        bc = st.ps("bc", [P, P])
        merged = st.ps("merged", [P, D])
        e_in = st.sem("e_in")
        const = st.sem("const")
        picked = st.sem("picked")
        gathered = st.sem("gathered")
        old_in = st.sem("old_in")
        c = st.sem("c")
        spread = st.sem("spread")
        merge_done = st.sem("merge_done")
        new_done = st.sem("new_done")
        stored = st.sem("stored")
        h_in = st.sem("h_in")
        passed = {e: st.sem(f"passed_{e}") for e in ("pool", "pe", "dve")}
        STEP = 8
        with nc.Block() as block:

            @block.sync
            def _(sp):
                with sp.If(sp.value_load(flag[0:1, 0:1], min_val=0, max_val=1) < 1):
                    sp.nop()
                with sp.Else():
                    for d, s in ((src_i, src_t), (dst_i, dst_t), (ew, ew_t)):
                        sp.dma_start(d[:, :], s).then_inc(e_in, 16)
                    sp.wait_ge(stored, 16 * ET)
                    sp.dma_start(h[:, 0:NG * GT, :],
                                 sum_dram[0:NG * GROUP, :].rearrange("(s p) d -> p s d", p=P)).then_inc(h_in, 16)
                    sp.dma_start(h[0:TAIL, NG * GT, :], sum_dram[NG * GROUP:N, :]).then_inc(h_in, 16)
                    sp.wait_ge(h_in, 32)

            @block.gpsimd
            def _(pool):
                with pool.If(pool.value_load(flag[0:1, 0:1], min_val=0, max_val=1) < 1):
                    pool.nop()
                with pool.Else():
                    def tile(t):
                        wait_then_pass(pool, picked, t + 1, passed["pool"])
                        pool.indirect_dma_start(
                            out=rows[:, :], out_offset=None, in_=xn_dram,
                            in_offset=bass.IndirectOffsetOnAxis(ap=from_i[:, 0:1], axis=0)).then_inc(gathered, 16)
                        wait_then_pass(pool, stored, t * 16, passed["pool"])
                        pool.indirect_dma_start(
                            out=old[:, :], out_offset=None, in_=sum_dram,
                            in_offset=bass.IndirectOffsetOnAxis(ap=to_i[:, 0:1], axis=0)).then_inc(old_in, 16)
                        wait_then_pass(pool, new_done, t + 1, passed["pool"])
                        pool.indirect_dma_start(
                            out=sum_dram, out_offset=bass.IndirectOffsetOnAxis(ap=first_i[:, 0:1], axis=0),
                            in_=new[:, :], in_offset=None, bounds_check=N - 1, oob_is_err=False).then_inc(stored, 16)

                    tile(0)
                    with pool.Fori(1, ET) as t:
                        tile(t)

            @block.tensor
            def _(pe):
                with pe.If(pe.value_load(flag[0:1, 0:1], min_val=0, max_val=1) < 1):
                    pe.nop()
                with pe.Else():
                    pe.wait_ge(const, 1)
                    with pe.Fori(0, ET) as t:
                        wait_then_pass(pe, c, t * STEP + 3, passed["pe"])
                        nc.tensor.matmul(bc[:, :], ones[:, :], diag[:, :], start=True, stop=True).then_inc(spread, 1)
                        wait_then_pass(pe, c, t * STEP + 7, passed["pe"])
                        nc.tensor.matmul(merged[:, :], same[:, :], msg[:, :], start=True, stop=True).then_inc(merge_done, 1)

            @block.vector
            def _(dve):
                with dve.If(dve.value_load(flag[0:1, 0:1], min_val=0, max_val=1) < 1):
                    dve.nop()
                with dve.Else():
                    nc.vector.memset(ones[:, :], 1.0).then_inc(const, 1)
                    dve.wait_ge(e_in, 48)
                    nc.vector.tensor_copy(src_f[:, :], src_i[:, :]).then_inc(c, 1)
                    dve.wait_ge(c, 1)
                    def tile(t):
                        k = [1]

                        def link(ins):
                            k[0] += 1
                            ins.then_inc(c, 1)
                            wait_then_pass(dve, c, t * STEP + k[0], passed["dve"])

                        wait_then_pass(dve, stored, t * 16, passed["dve"])
                        nc.vector.tensor_copy(wt[:, :], ew[:, bass.ds(t, 1)])
                        nc.vector.tensor_copy(to_i[:, :], src_i[:, bass.ds(t, 1)])
                        nc.vector.tensor_copy(from_i[:, :], dst_i[:, bass.ds(t, 1)]).then_inc(picked, 1)
                        link(nc.vector.tensor_copy(to_f[:, :], src_f[:, bass.ds(t, 1)]))
                        link(nc.vector.tensor_scalar(diag[:, :], ident[:, :], to_f[:, 0:1], None, ALU.mult))
                        wait_then_pass(dve, spread, t + 1, passed["dve"])
                        link(nc.vector.tensor_scalar(same[:, :], bc[:, :], to_f[:, 0:1], None, ALU.is_equal))
                        link(nc.vector.tensor_tensor(early[:, :], same[:, :], below[:, :], ALU.mult))
                        link(nc.vector.reduce_max(ecount[:, :], early[:, :], AX.X))
                        wait_then_pass(dve, gathered, t * 16 + 16, passed["dve"])
                        link(nc.vector.tensor_scalar(msg[:, :], rows[:, :], wt[:, 0:1], None, ALU.mult))
                        link(nc.vector.scalar_tensor_tensor(first_f[:, :], ecount[:, :], float(2 * NT * P), to_f[:, :],
                                                            ALU.mult, ALU.add))
                        link(nc.vector.tensor_copy(first_i[:, :], first_f[:, :]))
                        assert k[0] == STEP + 1
                        wait_then_pass(dve, merge_done, t + 1, passed["dve"])
                        wait_then_pass(dve, old_in, t * 16 + 16, passed["dve"])
                        nc.vector.tensor_tensor(new[:, :], merged[:, :], old[:, :], ALU.add).then_inc(new_done, 1)

                    tile(0)
                    with dve.Fori(1, ET) as t:
                        tile(t)


def ffn_stage(nc, router_w, w1, b1, w2, b2, h, ident, above, iota8, iota128, hn_dram, ys_dram, out):
    with Stage(nc, "ffn") as st:
        w1s = st.sb("w1s", [P, NEXP, KC, D])
        w2s = st.sb("w2s", [P, NEXP, KC, D])
        b1s = st.sb("b1s", [P, NEXP, D])
        b2s = st.sb("b2s", [P, NEXP, D])
        logits = st.sb("logits", [P, NT, NEXP])
        share = st.sb("share", [P, 2, NT])
        place = st.sb("place", [P, 2, NT], I32)
        target = st.sb("target", [P, NXT], I32)
        token = st.sb("token", [P, NXT], I32)
        expert = st.sb("expert", [1, NXT], I32)
        wx_in = st.sem("wx_in")
        norm2_block(nc, router_w, (w1, b1, w2, b2), (w1s, b1s, w2s, b2s), wx_in, h, logits, hn_dram, ident)
        route_block(nc, logits, share, place, expert, above, iota8, iota128)
        list_block(nc, place, token, target, iota128)
        expert_block(nc, hn_dram, ys_dram, w1s, b1s, w2s, b2s, wx_in, token, target, expert, ident)
        combine_block(nc, ys_dram, share, h, out)


def norm2_block(nc, router_w, weights, kept_weights, wx_in, h, logits, hn_dram, ident):
    with Stage(nc, "norm2") as st:
        rws = st.sb("rws", [NEXP, D])
        rwT = st.sb("rwT", [P, KC, NEXP])
        eps = st.sb("eps", [P, 1])
        stats = st.sb("stats", [P, 2, GT, 6])
        mv = st.sb("mv", [P, 2, GT, 2])
        std = st.sb("std", [P, 2, GT])
        rstd = st.sb("rstd", [P, 2, GT])
        hnb = st.sb("hnb", [P, 2, GT, D])
        hnT = st.sb("hnT", [P, 2, KC, GROUP])
        tp = [st.ps(f"tp{k}", [P, GROUP]) for k in range(2 * KC)]
        lp = [st.ps(f"lp{j}", [P, GT * NEXP]) for j in range(2)]
        rp = st.ps("rp", [P, KC * NEXP])
        rw_in = st.sem("rw_in")
        const = st.sem("const")
        rw_turned = st.sem("rw_turned")
        rw_out = st.sem("rw_out")
        stats_done = st.sem("stats_done")
        var_done = st.sem("var_done")
        std_done = st.sem("std_done")
        rstd_done = st.sem("rstd_done")
        hn_done = st.sem("hn_done")
        h_done = st.sem("h_done")
        turned = st.sem("turned")
        evacuated = st.sem("evacuated")
        scored = st.sem("scored")
        kept = st.sem("kept")
        hn_out = [st.sem(f"hn_out{j}") for j in range(2)]
        passed = {e: st.sem(f"passed_{e}") for e in ("sp", "act", "pe", "dve", "pool")}
        with nc.Block() as block:

            @block.sync
            def _(sp):
                sp.dma_start(rws[:, :], router_w).then_inc(rw_in, 16)
                for (w, b), (ws, bs) in ((weights[0:2], kept_weights[0:2]), (weights[2:4], kept_weights[2:4])):
                    sp.dma_start(ws[:, :, :, :], w.rearrange("e (c p) f -> p e c f", p=P)).then_inc(wx_in, 16)
                    sp.dma_start(bs[:, :, :].rearrange("p e f -> p (e f)"),
                                 b.rearrange("e f -> (e f)").rearrange("(a n) -> a n", a=1)
                                 .to_broadcast([P, NEXP * D])).then_inc(wx_in, 16)

                def store(g, pair, j, rows):
                    wait_then_pass(sp, hn_done, g + 1, passed["sp"])
                    src = hnb[:, j, :, :] if len(rows) == GT else hnb[:rows[0], j, 0, :]
                    sp.dma_start(node_view(hn_dram, g, rows), src).then_inc(hn_out[j], 16)

                groups(sp, store)
                sp.wait_ge(hn_out[0], 16 * (NG // 2 + 1))
                sp.wait_ge(hn_out[1], 16 * (NG // 2))

            @block.gpsimd
            def _(pool):
                def keep(g, pair, j, rows):
                    wait_then_pass(pool, hn_done, g + 1, passed["pool"])
                    src = hnb[:, j, :, :] if len(rows) == GT else hnb[:rows[0], j, 0, :]
                    nc.gpsimd.tensor_tensor(node_tiles(h, g, rows), node_tiles(h, g, rows), src, ALU.add)\
                        .then_inc(h_done, 1)

                groups(pool, keep)

            @block.tensor
            def _(pe):
                pe.wait_ge(rw_in, 16)
                for k in range(KC):
                    last = nc.tensor.transpose(rp[:, k * NEXP:(k + 1) * NEXP], rws[:, k * P:(k + 1) * P],
                                               ident[0:NEXP, 0:NEXP])
                last.then_inc(rw_turned, 1)
                pe.wait_ge(rw_out, 1)

                def turn(g, pair, j, rows):
                    r = rows[0]
                    wait_then_pass(pe, hn_done, g + 1, passed["pe"])
                    wait_then_pass(pe, evacuated, g - 1, passed["pe"])
                    for s in range(len(rows)):
                        for k in range(KC):
                            last = transpose(nc, tp[2 * j + k][:, s * P:s * P + r],
                                             hnb[:r, j, s, k * P:(k + 1) * P], ident, r)
                    last.then_inc(turned, 1)

                def score(g, pair, j, rows):
                    r = rows[0]
                    wait_then_pass(pe, evacuated, g + 1, passed["pe"])
                    wait_then_pass(pe, kept, g - 1, passed["pe"])
                    for s in range(len(rows)):
                        for k in range(KC):
                            last = nc.tensor.matmul(lp[j][:r, s * NEXP:(s + 1) * NEXP],
                                                    hnT[:, j, k, s * P:s * P + r], rwT[:, k, :],
                                                    start=k == 0, stop=k == KC - 1)
                    last.then_inc(scored, 1)

                whole = [P] * GT
                turn(0, 0, 0, whole)
                turn(1, 0, 1, whole)
                score(0, 0, 0, whole)
                with pe.Fori(1, NG // 2) as pair:
                    turn(pair * 2, pair, 0, whole)
                    score(pair * 2 - 1, pair, 1, whole)
                    turn(pair * 2 + 1, pair, 1, whole)
                    score(pair * 2, pair, 0, whole)
                turn(NG, NG // 2, 0, [TAIL])
                score(NG - 1, 0, 1, whole)
                score(NG, 0, 0, [TAIL])

            @block.scalar
            def _(act):
                act.wait_ge(const, 1)
                act.wait_ge(rw_turned, 1)
                nc.scalar.copy(rwT[:, :, :].rearrange("p c e -> p (c e)"), rp[:, :]).then_inc(rw_out, 1)

                def finish(g, pair, j, rows):
                    n, r, w = len(rows), rows[0], sum(rows)
                    wait_then_pass(act, var_done, g + 1, passed["act"])
                    nc.scalar.activation(std[:r, j, 0:n], mv[:r, j, 0:n, 1], ACT.Sqrt,
                                         bias=eps[:r, :]).then_inc(std_done, 1)
                    wait_then_pass(act, turned, g + 1, passed["act"])
                    wait_then_pass(act, scored, g - 1, passed["act"])
                    for k in range(KC):
                        last = nc.scalar.copy(hnT[:, j, k, 0:w], tp[2 * j + k][:, 0:w])
                    last.then_inc(evacuated, 1)

                groups(act, finish)

            @block.vector
            def _(dve):
                nc.vector.memset(eps[:, :], EPS).then_inc(const, 1)
                nc.vector.memset(logits[:, :, :], 0.0)

                def tile(g, s, n):
                    return h[:, bass.ds(g * GT + s, 1), :].rearrange("p a d -> p (a d)") if n > 1 else h[:TAIL, g * GT, :]

                def keep_logits(g, j, rows):
                    n, r = len(rows), rows[0]
                    wait_then_pass(dve, scored, g + 1, passed["dve"])
                    if n == 1:
                        nc.vector.tensor_copy(logits[:r, g * GT, :], lp[j][:r, 0:NEXP]).then_inc(kept, 1)
                    else:
                        nc.vector.tensor_copy(logits[:, bass.ds(g * GT, GT), :],
                                              lp[j][:, :].rearrange("p (s e) -> p s e", s=GT)).then_inc(kept, 1)

                def run(g, pair, j, rows):
                    n, r = len(rows), rows[0]
                    for s in range(n):
                        last = nc.vector.bn_stats(stats[:r, j, s, :], tile(g, s, n))
                    last.then_inc(stats_done, 1)
                    wait_then_pass(dve, stats_done, g + 1, passed["dve"])
                    for s in range(n):
                        last = nc.vector.bn_aggr(mv[:r, j, s, :], stats[:r, j, s, :])
                    last.then_inc(var_done, 1)
                    wait_then_pass(dve, std_done, g + 1, passed["dve"])
                    nc.vector.reciprocal(rstd[:r, j, 0:n], std[:r, j, 0:n]).then_inc(rstd_done, 1)
                    wait_then_pass(dve, rstd_done, g + 1, passed["dve"])
                    wait_then_pass(dve, turned, g - 1, passed["dve"])
                    wait_then_pass(dve, h_done, g - 1, passed["dve"])
                    wait_then_pass(dve, hn_out[j], pair * 16, passed["dve"])
                    for s in range(n):
                        last = nc.vector.tensor_scalar(hnb[:r, j, s, :], tile(g, s, n), mv[:r, j, s, 0:1],
                                                       rstd[:r, j, s:s + 1], ALU.subtract, ALU.mult)
                    last.then_inc(hn_done, 1)

                whole = [P] * GT
                run(0, 0, 0, whole)
                run(1, 0, 1, whole)
                with dve.Fori(1, NG // 2) as pair:
                    run(pair * 2, pair, 0, whole)
                    keep_logits(pair * 2 - 2, 0, whole)
                    run(pair * 2 + 1, pair, 1, whole)
                    keep_logits(pair * 2 - 1, 1, whole)
                run(NG, NG // 2, 0, [TAIL])
                keep_logits(NG - 2, 0, whole)
                keep_logits(NG - 1, 1, whole)
                keep_logits(NG, 0, [TAIL])


def route_block(nc, logits, share, place, expert, above, iota8, iota128):
    NE = NT * NEXP
    with Stage(nc, "route") as st:
        m = st.sb("m", [P, NT])
        z = st.sb("z", [P, NT])
        rz = st.sb("rz", [P, NT])
        low = st.sb("low", [P, NT])
        best = [st.sb(f"best{k}", [P, NT]) for k in range(2)]
        total = st.sb("total", [P, NT])
        prob = st.sb("prob", [P, NT, NEXP])
        rest = st.sb("rest", [P, NT, NEXP])
        eq = st.sb("eq", [P, NT, NEXP])
        oh = [st.sb(f"oh{k}", [P, NT, NEXP]) for k in range(2)]
        iota8m = st.sb("iota8m", [P, NEXP])
        cnt = st.sb("cnt", [P, NT, NEXP])
        cntb = st.sb("cntb", [P, NT, NEXP], BF16)
        onesb = st.sb("onesb", [P, P], BF16)
        ones = st.sb("ones", [P, NT])
        cum = st.sb("cum", [P, NT, NEXP])
        rank = st.sb("rank", [P, NT, NEXP])
        n_i = st.sb("n_i", [P, NEXP], I32)
        tiles = st.sb("tiles", [P, NEXP])
        tend = st.sb("tend", [P, NEXP])
        first = st.sb("first", [P, NEXP])
        pos = st.sb("pos", [P, NT])
        ge = st.sb("ge", [1, NXT])
        exf = st.sb("exf", [1, NXT])
        pre = st.ps("pre", [P, NE])
        tot = st.ps("tot", [P, NE])
        c = st.sem("c")
        act_c = st.sem("act_c")
        pool_c = st.sem("pool_c")
        pe_c = st.sem("pe_c")

        def over_e(a):
            return a[:, :].rearrange("p (t a) -> p t a", a=1).to_broadcast([P, NT, NEXP])

        def over_t(a):
            return a[:, :].rearrange("p (a e) -> p a e", a=1).to_broadcast([P, NT, NEXP])

        SHIFTED, COUNTED, CAST = 2, 17, 18
        with nc.Block() as block:

            @block.scalar
            def _(act):
                act.wait_ge(c, SHIFTED)
                nc.scalar.activation(prob[:, :, :], prob[:, :, :], ACT.Exp).then_inc(act_c, 1)

            @block.gpsimd
            def _(pool):
                pool.wait_ge(c, COUNTED)
                pool.affine_select(out=cnt[:, :, :], in_=cnt[:, :, :], compare_op=ALU.is_ge, fill=0.0, base=N - 1,
                                   pattern=[[-P, NT], [0, NEXP]], channel_multiplier=-1).then_inc(pool_c, 1)

            @block.tensor
            def _(pe):
                pe.wait_ge(c, CAST)
                flat = cntb[:, :, :].rearrange("p t e -> p (t e)")
                nc.tensor.matmul(pre[:, :], above[:, :], flat, start=True, stop=True)
                nc.tensor.matmul(tot[:, :], onesb[:, :], flat, start=True, stop=True).then_inc(pe_c, 1)

            @block.vector
            def _(dve):
                v = nc.vector
                n = [0]

                def link(ins):
                    n[0] += 1
                    ins.then_inc(c, 1)
                    dve.wait_ge(c, n[0])

                v.memset(onesb[:, :], 1.0)
                v.memset(ones[:, :], 1.0)
                v.tensor_scalar_add(iota8m[:, :], iota8[:, :], -float(NEXP))
                link(v.tensor_reduce(m[:, :], logits[:, :, :], AX.X, ALU.max))
                link(v.tensor_tensor(prob[:, :, :], logits[:, :, :], over_e(m), ALU.subtract))
                assert n[0] == SHIFTED
                dve.wait_ge(act_c, 1)
                link(v.tensor_reduce(z[:, :], prob[:, :, :], AX.X, ALU.add))
                link(v.reciprocal(rz[:, :], z[:, :]))
                link(v.tensor_tensor(prob[:, :, :], prob[:, :, :], over_e(rz), ALU.mult))
                for k, p in enumerate((prob, rest)):
                    link(v.tensor_reduce(best[k][:, :], p[:, :, :], AX.X, ALU.max))
                    link(v.tensor_tensor(eq[:, :, :], p[:, :, :], over_e(best[k]), ALU.is_equal))
                    link(v.scalar_tensor_tensor(eq[:, :, :], eq[:, :, :], -float(NEXP), over_t(iota8), ALU.mult, ALU.add))
                    link(v.tensor_reduce(low[:, :], eq[:, :, :], AX.X, ALU.min))
                    link(v.tensor_tensor(oh[k][:, :, :], over_t(iota8m), over_e(low), ALU.is_equal))
                    if k == 0:
                        link(v.scalar_tensor_tensor(rest[:, :, :], oh[0][:, :, :], -2.0, prob[:, :, :], ALU.mult, ALU.add))
                link(v.tensor_tensor(cnt[:, :, :], oh[0][:, :, :], oh[1][:, :, :], ALU.add))
                assert n[0] == COUNTED
                dve.wait_ge(pool_c, 1)
                link(v.tensor_copy(cntb[:, :, :], cnt[:, :, :]))
                assert n[0] == CAST
                link(v.tensor_tensor(total[:, :], best[0][:, :], best[1][:, :], ALU.add))
                link(v.tensor_scalar_max(total[:, :], total[:, :], 1e-12))
                link(v.reciprocal(total[:, :], total[:, :]))
                for k in range(2):
                    v.tensor_tensor(share[:, k, :], best[k][:, :], total[:, :], ALU.mult)
                dve.wait_ge(pe_c, 1)
                tot3 = tot[:, :].rearrange("p (t e) -> p t e", e=NEXP)
                pre3 = pre[:, :].rearrange("p (t e) -> p t e", e=NEXP)
                for e in range(NEXP):
                    last = v.tensor_tensor_scan(cum[:, :, e], ones[:, :], tot3[:, :, e], 0.0, ALU.mult, ALU.add)
                link(last)
                link(v.tensor_tensor(rank[:, :, :], cum[:, :, :], tot3, ALU.subtract))
                link(v.tensor_tensor(rank[:, :, :], rank[:, :, :], pre3, ALU.add))
                link(v.tensor_scalar_add(n_i[:, :], cum[:, NT - 1, :], float(P - 1)))
                link(v.tensor_single_scalar(n_i[:, :], n_i[:, :], 7, op=ALU.arith_shift_right))
                link(v.tensor_copy(tiles[:, :], n_i[:, :]))
                link(v.tensor_tensor_scan(tend[:, :], ones[:, 0:NEXP], tiles[:, :], 0.0, ALU.mult, ALU.add))
                link(v.tensor_tensor(first[:, :], tend[:, :], tiles[:, :], ALU.subtract))
                link(v.tensor_scalar_mul(first[:, :], first[:, :], float(P)))
                link(v.tensor_tensor(rank[:, :, :], rank[:, :, :], over_t(first), ALU.add))
                for k in range(2):
                    link(v.tensor_tensor(eq[:, :, :], oh[k][:, :, :], rank[:, :, :], ALU.mult))
                    link(v.tensor_reduce(pos[:, :], eq[:, :, :], AX.X, ALU.add))
                    link(v.tensor_copy(place[:, k, :], pos[:, :]))
                link(v.tensor_scalar(exf[:, :], iota128[0:1, 0:NXT], tend[0:1, 0:1], None, ALU.is_ge))
                for e in range(1, NEXP - 1):
                    link(v.tensor_scalar(ge[:, :], iota128[0:1, 0:NXT], tend[0:1, e:e + 1], None, ALU.is_ge))
                    link(v.tensor_tensor(exf[:, :], exf[:, :], ge[:, :], ALU.add))
                link(v.tensor_copy(expert[:, :], exf[:, :]))


def list_block(nc, place, token, target, iota128):
    PIECES = [(k, a, b) for k in range(2) for a, b in ((0, NT // 2), (NT // 2, NT))]
    with Stage(nc, "list") as st:
        number_i = st.sb("number_i", [P, NT], I32)
        number = st.sb("number", [P, NT])
        entry = st.sb("entry", [P, 2, NT])
        found = st.sb("found", [P, NXT])
        beyond = st.sb("beyond", [P, NXT])
        found_i = st.sb("found_i", [P, NXT], I32)
        part_i = st.sb("part_i", [P, 2, NT], I32)
        in_tile = st.sb("in_tile", [P, 2, NT])
        in_row = st.sb("in_row", [P, 2, NT])
        value = st.sb("value", [P, 2, NT, NXT])
        rows = st.sb("rows", [P, 2, NT, P])
        listed = st.ps("listed", [P, NXT])
        numbered = st.sem("numbered")
        c = st.sem("c")
        made = st.sem("made")
        summed = st.sem("summed")
        with nc.Block() as block:

            @block.gpsimd
            def _(pool):
                pool.iota(number_i[:, :], [[P, NT]], base=0, channel_multiplier=1).then_inc(numbered, 1)

            @block.tensor
            def _(pe):
                for n, (k, a, b) in enumerate(PIECES):
                    pe.wait_ge(made, n + 1)
                    for t in range(a, b):
                        r = TAIL if t == NT - 1 else P
                        last = nc.tensor.matmul(listed[:, :], rows[:r, k, t, :], value[:r, k, t, :],
                                                start=n == 0 and t == 0, stop=n == len(PIECES) - 1 and t == NT - 1)
                last.then_inc(summed, 1)

            @block.vector
            def _(dve):
                v = nc.vector
                n = [0]

                def link(ins):
                    n[0] += 1
                    ins.then_inc(c, 1)
                    dve.wait_ge(c, n[0])

                dve.wait_ge(numbered, 1)
                link(v.tensor_copy(number[:, :], number_i[:, :]))
                for k in range(2):
                    v.tensor_scalar(entry[:, k, :], number[:, :], 2.0, float(k + 1), ALU.mult, ALU.add)
                link(v.tensor_single_scalar(part_i[:, :, :], place[:, :, :], 7, op=ALU.arith_shift_right))
                link(v.tensor_copy(in_tile[:, :, :], part_i[:, :, :]))
                link(v.tensor_single_scalar(part_i[:, :, :], place[:, :, :], P - 1, op=ALU.bitwise_and))
                link(v.tensor_copy(in_row[:, :, :], part_i[:, :, :]))

                def over(a, width):
                    return a.rearrange("p (t a) -> p t a", a=1).to_broadcast([P, a.shape[1], width])

                for k, a, b in PIECES:
                    link(v.tensor_tensor(
                        value[:, k, a:b, :],
                        iota128[:, 0:NXT].rearrange("p (a s) -> p a s", a=1).to_broadcast([P, b - a, NXT]),
                        over(in_tile[:, k, a:b], NXT), ALU.is_equal))
                    v.tensor_tensor(value[:, k, a:b, :], value[:, k, a:b, :], over(entry[:, k, a:b], NXT), ALU.mult)
                    v.tensor_tensor(
                        rows[:, k, a:b, :],
                        iota128[:, :].rearrange("p (a s) -> p a s", a=1).to_broadcast([P, b - a, P]),
                        over(in_row[:, k, a:b], P), ALU.is_equal).then_inc(made, 1)
                dve.wait_ge(summed, 1)
                link(v.tensor_copy(found[:, :], listed[:, :]))
                link(v.tensor_scalar(beyond[:, :], found[:, :], 0.5, float(4 * N), ALU.is_lt, ALU.mult))
                v.scalar_tensor_tensor(target[:, :], found[:, :], -1.0, beyond[:, :], ALU.add, ALU.add)
                link(v.tensor_scalar(found_i[:, :], found[:, :], -1.0, 0.0, ALU.add, ALU.max))
                link(v.tensor_single_scalar(token[:, :], found_i[:, :], 1, op=ALU.arith_shift_right))


def expert_block(nc, hn_dram, ys_dram, w1s, b1s, w2s, b2s, wx_in, token, target, expert, ident):
    with Stage(nc, "exp") as st:
        idx = st.sb("idx", [P, 2], I32)
        to = st.sb("to", [P, 2], I32)
        xt = st.sb("xt", [P, 2, D])
        xT = st.sb("xT", [P, 2, KC, P])
        hid = st.sb("hid", [P, 2, D])
        g1 = st.sb("g1", [P, 2, D])
        gT = st.sb("gT", [P, 2, KC, P])
        yt = st.sb("yt", [P, 2, D])
        t1 = [st.ps(f"t1{j}", [P, D]) for j in range(2)]
        up = [st.ps(f"up{j}", [P, D]) for j in range(2)]
        t2 = [st.ps(f"t2{j}", [P, D]) for j in range(2)]
        dn = [st.ps(f"dn{j}", [P, D]) for j in range(2)]
        x_in = [st.sem(f"x_in{j}") for j in range(2)]
        y_out = [st.sem(f"y_out{j}") for j in range(2)]
        idx_done = st.sem("idx_done")
        to_done = st.sem("to_done")
        t1_done = st.sem("t1_done")
        xT_done = st.sem("xT_done")
        up_done = st.sem("up_done")
        hid_done = st.sem("hid_done")
        g1_done = st.sem("g1_done")
        t2_done = st.sem("t2_done")
        gT_done = st.sem("gT_done")
        dn_done = st.sem("dn_done")
        y_done = st.sem("y_done")
        passed = {e: st.sem(f"passed_{e}") for e in ("sp", "act", "pe", "dve", "pool")}

        AHEAD = 5

        def ticks(eng, count, tick):
            for i in range(6):
                tick(i, i // 2, i % 2)
            with eng.Fori(3, NXT // 2) as half:
                for j in range(2):
                    tick(half * 2 + j, half, j)
            for i in range(NXT // 2 * 2, count):
                tick(i, i // 2, i % 2)

        def live(i, lag):
            return not isinstance(i, int) or 0 <= i - lag < NXT

        def expert_of(eng, i):
            row = expert[0:1, i:i + 1] if isinstance(i, int) else expert[0:1, bass.ds(i, 1)]
            return eng.value_load(row, min_val=0, max_val=NEXP - 1)

        with nc.Block() as block:

            @block.gpsimd
            def _(pool):
                def tick(i, half, j):
                    if live(i, 0):
                        wait_then_pass(pool, t1_done, i - 1, passed["pool"])
                        pool.tensor_copy(idx[:, j:j + 1], token[:, bass.ds(i, 1)]).then_inc(idx_done, 1)
                        wait_then_pass(pool, idx_done, i + 1, passed["pool"])
                        pool.indirect_dma_start(
                            out=xt[:, j, :], out_offset=None, in_=hn_dram,
                            in_offset=bass.IndirectOffsetOnAxis(ap=idx[:, j:j + 1], axis=0)).then_inc(x_in[j], 16)
                    if live(i, AHEAD):
                        wait_then_pass(pool, y_done, i - AHEAD + 1, passed["pool"])
                        pool.tensor_copy(to[:, 1 - j:2 - j], target[:, bass.ds(i - AHEAD, 1)]).then_inc(to_done, 1)
                        wait_then_pass(pool, to_done, i - AHEAD + 1, passed["pool"])
                        pool.indirect_dma_start(
                            out=ys_dram, out_offset=bass.IndirectOffsetOnAxis(ap=to[:, 1 - j:2 - j], axis=0),
                            in_=yt[:, 1 - j, :], in_offset=None, bounds_check=2 * N - 1,
                            oob_is_err=False).then_inc(y_out[1 - j], 16)

                ticks(pool, NXT + AHEAD, tick)
                pool.wait_ge(y_out[0], 16 * (NXT // 2 + 1))
                pool.wait_ge(y_out[1], 16 * (NXT // 2))

            @block.tensor
            def _(pe):
                pe.wait_ge(wx_in, 64)

                def tick(i, half, j):
                    e_up = expert_of(pe, i - 1) if live(i, 1) else None
                    if live(i, 0):
                        wait_then_pass(pe, x_in[j], half * 16 + 16, passed["pe"])
                        for k in range(KC):
                            last = transpose(nc, t1[j][:, k * P:(k + 1) * P], xt[:, j, k * P:(k + 1) * P], ident, P)
                        last.then_inc(t1_done, 1)
                    if live(i, 2):
                        wait_then_pass(pe, g1_done, i - 1, passed["pe"])
                        for k in range(KC):
                            last = transpose(nc, t2[j][:, k * P:(k + 1) * P], g1[:, j, k * P:(k + 1) * P], ident, P)
                        last.then_inc(t2_done, 1)
                    if live(i, 1):
                        wait_then_pass(pe, xT_done, i, passed["pe"])
                        for k in range(KC):
                            last = nc.tensor.matmul(up[1 - j][:, :], xT[:, 1 - j, k, :],
                                                    w1s[:, bass.ds(e_up, 1), k, :].rearrange("p a f -> p (a f)"),
                                                    start=k == 0, stop=k == KC - 1)
                        last.then_inc(up_done, 1)
                    if live(i, 2):
                        e_dn = expert_of(pe, i - 2)
                        wait_then_pass(pe, gT_done, i - 1, passed["pe"])
                        wait_then_pass(pe, y_done, i - 3, passed["pe"])
                        for k in range(KC):
                            last = nc.tensor.matmul(dn[j][:, :], gT[:, j, k, :],
                                                    w2s[:, bass.ds(e_dn, 1), k, :].rearrange("p a f -> p (a f)"),
                                                    start=k == 0, stop=k == KC - 1)
                        last.then_inc(dn_done, 1)

                ticks(pe, NXT + 2, tick)

            @block.scalar
            def _(act):
                def tick(i, half, j):
                    if live(i, 0):
                        wait_then_pass(act, t1_done, i + 1, passed["act"])
                        wait_then_pass(act, up_done, i - 1, passed["act"])
                        nc.scalar.copy(xT[:, j, :, :].rearrange("p c r -> p (c r)"), t1[j][:, :]).then_inc(xT_done, 1)
                    if live(i, 1):
                        wait_then_pass(act, hid_done, i, passed["act"])
                        wait_then_pass(act, t2_done, i - 2, passed["act"])
                        nc.scalar.activation(g1[:, 1 - j, :], hid[:, 1 - j, :], ACT.Gelu).then_inc(g1_done, 1)

                ticks(act, NXT + 1, tick)

            @block.vector
            def _(dve):
                dve.wait_ge(wx_in, 64)

                def tick(i, half, j):
                    if live(i, 2):
                        wait_then_pass(dve, t2_done, i - 1, passed["dve"])
                        wait_then_pass(dve, dn_done, i - 3, passed["dve"])
                        nc.vector.tensor_copy(gT[:, j, :, :].rearrange("p c r -> p (c r)"), t2[j][:, :]).then_inc(gT_done, 1)
                    if live(i, 1):
                        e_up = expert_of(dve, i - 1)
                        wait_then_pass(dve, up_done, i, passed["dve"])
                        wait_then_pass(dve, g1_done, i - 2, passed["dve"])
                        nc.vector.tensor_tensor(hid[:, 1 - j, :], up[1 - j][:, :],
                                                b1s[:, bass.ds(e_up, 1), :].rearrange("p a f -> p (a f)"),
                                                ALU.add).then_inc(hid_done, 1)
                    if live(i, 2):
                        e_dn = expert_of(dve, i - 2)
                        wait_then_pass(dve, dn_done, i - 1, passed["dve"])
                        wait_then_pass(dve, y_out[j], half * 16 - 16, passed["dve"])
                        nc.vector.tensor_tensor(yt[:, j, :], dn[j][:, :],
                                                b2s[:, bass.ds(e_dn, 1), :].rearrange("p a f -> p (a f)"),
                                                ALU.add).then_inc(y_done, 1)

                ticks(dve, NXT + 2, tick)


def combine_block(nc, ys_dram, share, h, out):
    with Stage(nc, "comb") as st:
        wt = st.sb("wt", [P, 2, 2, GT])
        ys = st.sb("ys", [P, 2, GT, 2 * D])
        acc = st.sb("acc", [P, 2, GT, D])
        wt_done = st.sem("wt_done")
        ys_in = [st.sem(f"ys_in{j}") for j in range(2)]
        half_done = st.sem("half_done")
        acc_done = st.sem("acc_done")
        out_done = [st.sem(f"out_done{j}") for j in range(2)]
        passed = {e: st.sem(f"passed_{e}") for e in ("sp", "act", "dve")}
        both = ys_dram.rearrange("(n k) d -> n (k d)", k=2)

        with nc.Block() as block:

            @block.sync
            def _(sp):
                def load(g, pair, j, rows):
                    wait_then_pass(sp, acc_done, g - 1, passed["sp"])
                    dst = ys[:, j, :, :] if len(rows) == GT else ys[0:rows[0], j, 0, :]
                    sp.dma_start(dst, node_view(both, g, rows)).then_inc(ys_in[j], 16)

                groups(sp, load)

            @block.vector
            def _(dve):
                def add(g, pair, j, rows):
                    n, r = len(rows), rows[0]
                    nc.vector.tensor_copy(wt[:, j, :, 0:n], share[:, :, bass.ds(g * GT, n)]).then_inc(wt_done, 1)
                    wait_then_pass(dve, wt_done, g + 1, passed["dve"])
                    wait_then_pass(dve, ys_in[j], (pair + 1) * 16, passed["dve"])
                    wait_then_pass(dve, out_done[j], pair * 16, passed["dve"])
                    for s in range(n):
                        base = h[:, bass.ds(g * GT + s, 1), :].rearrange("p a d -> p (a d)") if n == GT else \
                            h[:r, g * GT, :]
                        last = nc.vector.scalar_tensor_tensor(acc[:r, j, s, :], ys[:r, j, s, 0:D], wt[:r, j, 0, s:s + 1],
                                                              base, ALU.mult, ALU.add)
                    last.then_inc(half_done, 1)
                    wait_then_pass(dve, half_done, g + 1, passed["dve"])
                    for s in range(n):
                        last = nc.vector.scalar_tensor_tensor(acc[:r, j, s, :], ys[:r, j, s, D:2 * D],
                                                              wt[:r, j, 1, s:s + 1], acc[:r, j, s, :], ALU.mult, ALU.add)
                    last.then_inc(acc_done, 1)

                groups(dve, add)

            @block.scalar
            def _(act):
                def store(g, pair, j, rows):
                    wait_then_pass(act, acc_done, g + 1, passed["act"])
                    src = acc[:, j, :, :] if len(rows) == GT else acc[0:rows[0], j, 0, :]
                    act.dma_start(node_view(out, g, rows), src).then_inc(out_done[j], 16)

                groups(act, store)
                act.wait_ge(out_done[0], 16 * (NG // 2 + 1))
                act.wait_ge(out_done[1], 16 * (NG // 2))


def gps_layer(nc, x, src_t, dst_t, ew_t, W_qk, b_qk, W_v, b_v, gamma, beta, router_w, w1, b1, w2, b2, out):
    xn_dram = nc.dram_tensor("xn_scratch", [N, D], F32).ap()
    sum_dram = nc.dram_tensor("sum_scratch", [N, D], F32).ap()
    with Stage(nc, "all") as st:
        ident = st.sb("ident", [P, P])
        below = st.sb("below", [P, P])
        iota8 = st.sb("iota8", [P, NEXP])
        above = st.sb("above", [P, P], BF16)
        above_f = st.sb("above_f", [P, P])
        iota128 = st.sb("iota128", [P, P])
        iota49 = st.sb("iota49", [P, NB], BF16)
        iota_i = st.sb("iota_i", [P, P], I32)
        flag = st.sb("flag", [1, 1], I32)
        low_i = st.sb("low_i", [1, NCH], I32)
        xn = st.sb("xn", [P, NT, D])
        set_ = st.sem("set")
        with nc.Block() as block:

            @block.gpsimd
            def _(pool):
                pool.memset(ident[:, :], 0.0).then_inc(set_, 1)
                pool.memset(below[:, :], 1.0).then_inc(set_, 1)
                pool.memset(above_f[:, :], 1.0).then_inc(set_, 1)
                pool.iota(iota_i[:, :], [[1, P]], base=0, channel_multiplier=0).then_inc(set_, 1)
                pool.wait_ge(set_, 4)
                pool.affine_select(out=ident[:, :], in_=ident[:, :], compare_op=ALU.not_equal, fill=1.0,
                                   base=0, pattern=[[-1, P]], channel_multiplier=1)
                pool.affine_select(out=below[:, :], in_=below[:, :], compare_op=ALU.is_gt, fill=0.0,
                                   base=0, pattern=[[-1, P]], channel_multiplier=1)
                pool.affine_select(out=above_f[:, :], in_=above_f[:, :], compare_op=ALU.is_gt, fill=0.0,
                                   base=0, pattern=[[1, P]], channel_multiplier=-1).then_inc(set_, 1)
                pool.wait_ge(set_, 5)
                pool.tensor_copy(above[:, :], above_f[:, :])
                pool.tensor_copy(iota8[:, :], iota_i[:, 0:NEXP])
                pool.tensor_copy(iota49[:, :], iota_i[:, 0:NB])
                pool.tensor_copy(iota128[:, :], iota_i[:, :])

        with Stage(nc, "turned") as tr:
            xnT = tr.sb("xnT", [P, KC, N])
            keyT = tr.sb("keyT", [P, KC, N])
            gmax = tr.sb("gmax", [P, KC, NG + 1])
            norm_stage(nc, x, W_qk[1], b_qk[1], xn_dram, xn, xnT, keyT, gmax, ident)
            mix_stage(nc, x, W_qk[0], b_qk[0], W_v, b_v, gamma, beta, xn, xnT, keyT, gmax, ident)
        edge_stage(nc, src_t, dst_t, ew_t, xn_dram, sum_dram, low_i, flag, xn, ident, above, iota49, iota128)
        any_edges_stage(nc, src_t, dst_t, ew_t, xn_dram, sum_dram, flag, xn, ident, below)
        hn_dram = nc.dram_tensor("hn_scratch", [N, D], F32).ap()
        ys_dram = nc.dram_tensor("ys_scratch", [2 * N, D], F32).ap()
        ffn_stage(nc, router_w, w1, b1, w2, b2, xn, ident, above, iota8, iota128, hn_dram, ys_dram, out)


def edge_tiles(a, fill):
    return np.ascontiguousarray(np.concatenate([a, fill.astype(a.dtype)]).reshape(ET, P).T)


def kernel(x, src, dst, edge_weight, L0_mix_W_qk, L0_mix_b_qk, L0_mix_W_v, L0_mix_b_v, L0_mix_gamma, L0_mix_beta,
           L0_ffn_router_w, L0_ffn_w1, L0_ffn_b1, L0_ffn_w2, L0_ffn_b2):
    import concourse.bacc as bacc
    from concourse.bass_utils import run_bass_kernel_spmd

    pad = ET * P - E
    arrays = {
        "x": x,
        "src": edge_tiles(np.asarray(src), np.arange(pad) * P % N),
        "dst": edge_tiles(np.asarray(dst), np.full(pad, N - 1)),
        "edge_weight": edge_tiles(np.asarray(edge_weight), np.zeros(pad)),
        "W_qk": L0_mix_W_qk, "b_qk": L0_mix_b_qk, "W_v": L0_mix_W_v, "b_v": L0_mix_b_v,
        "gamma": L0_mix_gamma, "beta": L0_mix_beta, "router_w": L0_ffn_router_w,
        "w1": L0_ffn_w1, "b1": L0_ffn_b1, "w2": L0_ffn_w2, "b2": L0_ffn_b2,
    }
    arrays = {f"in_{k}": np.ascontiguousarray(v) for k, v in arrays.items()}
    nc = bacc.Bacc("TRN2", target_bir_lowering=False, num_devices=1)
    args = [nc.dram_tensor(k, v.shape, mybir.dt.from_np(v.dtype), kind="ExternalInput").ap() for k, v in arrays.items()]
    out = nc.dram_tensor("out", (N, D), F32, kind="ExternalOutput").ap()
    gps_layer(nc, *args, out)
    r = run_bass_kernel_spmd(nc, [arrays], core_ids=[0])
    return r.results[0]["out"]
```
